# Optimizing a Trainium2 kernel written in Bass

```python
import numpy as np
import jax
import jax.numpy as jnp

def _softmax(x, axis=-1):
    return jax.nn.softmax(x, axis=axis)

def _gelu(x):
    return jax.nn.gelu(x, approximate=True)

def _silu(x):
    return jax.nn.silu(x)

def _sigmoid(x):
    return jax.nn.sigmoid(x)

def _layernorm(x, axis=-1, eps=1e-05):
    m = jnp.mean(x, axis=axis, keepdims=True)
    v = jnp.var(x, axis=axis, keepdims=True)
    return (x - m) / jnp.sqrt(v + eps)

def _scatter_add(tgt, idx, src, axis=0):
    return tgt.at[idx].add(src)

def _segment_sum(src, seg, n):
    return jax.ops.segment_sum(src, seg, n)
kernel_name = 'mk_gnn_preln_d4_gnn_r8_098d6d'

def setup_inputs(seed: int=0):
    np.random.seed(seed)
    _w = jnp.asarray

    def _rec_inputs():
        import jax
        import jax.numpy as jnp
        _gk = jax.random.key(seed)
        x = -0.000202 + 1 * jax.random.normal(jax.random.fold_in(_gk, 1), (6250, 64), jnp.float32)
        src = jax.random.randint(jax.random.fold_in(_gk, 2), (200000,), 0, 6250, jnp.int32)
        dst = jnp.minimum((6250 * jax.random.uniform(jax.random.fold_in(_gk, 3), (200000,)) ** 2.0).astype(jnp.int32), 49999)
        _o = jnp.argsort(dst, stable=True)
        src = src[_o]
        dst = dst[_o]
        edge_attr_32 = -5.16925e-05 + 1.00005 * jax.random.normal(jax.random.fold_in(_gk, 13), (200000, 32), jnp.float32)
        edge_attr_64 = -9.77346e-05 + 0.999888 * jax.random.normal(jax.random.fold_in(_gk, 14), (200000, 64), jnp.float32)
        edge_weight = jax.random.uniform(jax.random.fold_in(_gk, 16), (200000,), jnp.float32, 0.0, 0.999998)
        return (x, src, dst, edge_attr_32, edge_attr_64, edge_weight)
    x, src, dst, edge_attr_32, edge_attr_64, edge_weight = _rec_inputs()

    def _L0_gnn_setup():
        import jax, jax.numpy as jnp
        import numpy as np
        N_NODES = 12500
        N_EDGES = 400000
        EDGE_OUT = 32
        HID = 128
        NODE_OUT = 64
        N_GRAPHS = 16
        key = jax.random.key(seed)
        ks = jax.random.split(key, 9)
        x = jax.random.normal(ks[0], (N_NODES, 64), dtype=jnp.float32)
        edge_index = jax.random.randint(ks[1], (2, N_EDGES), 0, N_NODES, dtype=jnp.int64)
        edge_attr = jax.random.normal(ks[2], (N_EDGES, EDGE_OUT), dtype=jnp.float32)
        u = jax.random.normal(ks[3], (N_GRAPHS, 1), dtype=jnp.float32)
        batch = jnp.sort(jax.random.randint(ks[4], (N_NODES,), 0, N_GRAPHS, dtype=jnp.int64))
        d_in = 3 * EDGE_OUT + 1
        W1 = jax.random.normal(ks[5], (d_in, HID), dtype=jnp.float32) / np.sqrt(d_in)
        b1 = jnp.zeros((HID,), dtype=jnp.float32)
        W2 = jax.random.normal(ks[6], (HID, NODE_OUT), dtype=jnp.float32) / np.sqrt(HID)
        b2 = jnp.zeros((NODE_OUT,), dtype=jnp.float32)
        return {'x': x, 'edge_index': edge_index, 'edge_attr': edge_attr, 'u': u, 'batch': batch, 'W1': W1, 'b1': b1, 'W2': W2, 'b2': b2}
    _L0_gnn_all = _L0_gnn_setup()
    _L0_gnn_in = {k: v for k, v in _L0_gnn_all.items() if k in ('u', 'W1', 'b1', 'W2', 'b2')}
    del _L0_gnn_all

    def _L1_gnn_setup():
        import jax, jax.numpy as jnp
        import numpy as np
        N_NODES = 12500
        N_EDGES = 200000
        D_FEAT = 64
        EMB_DIM = 64

        def _norm_by_degree(x, degree):
            return x * jax.lax.rsqrt(jnp.maximum(degree.astype(x.dtype), 1.0))[:, None]
        key = jax.random.key(seed)
        k1, k2, k3, k4 = jax.random.split(key, 4)
        x = jax.random.normal(k1, (N_NODES, D_FEAT), dtype=jnp.float32)
        senders = jax.random.randint(k2, (N_EDGES,), 0, N_NODES, dtype=jnp.int32)
        receivers = jax.random.randint(k3, (N_EDGES,), 0, N_NODES, dtype=jnp.int32)
        W = jax.random.normal(k4, (2 * D_FEAT, EMB_DIM), dtype=jnp.float32) * (1.0 / np.sqrt(2 * D_FEAT))
        b = jnp.zeros((EMB_DIM,), dtype=jnp.float32)
        return {'x': x, 'senders': senders, 'receivers': receivers, 'W': W, 'b': b}
    _L1_gnn_all = _L1_gnn_setup()
    _L1_gnn_in = {k: v for k, v in _L1_gnn_all.items() if k in ('W', 'b')}
    del _L1_gnn_all

    def _L2_gnn_setup():
        import jax, jax.numpy as jnp
        import numpy as np
        N_NODES = 6250
        N_EDGES = 100000
        D_FEAT = 64
        key = jax.random.key(seed)
        k1, k2, k3 = jax.random.split(key, 3)
        x = jax.random.normal(k1, (N_NODES, D_FEAT), dtype=jnp.float32)
        edge_index = jax.random.randint(k2, (2, N_EDGES), 0, N_NODES, dtype=jnp.int64)
        edge_weight = jax.random.uniform(k3, (N_EDGES,), dtype=jnp.float32)
        eps = jnp.zeros((1,), dtype=jnp.float32)
        return {'x': x, 'edge_index': edge_index, 'edge_weight': edge_weight, 'eps': eps}
    _L2_gnn_all = _L2_gnn_setup()
    _L2_gnn_in = {k: v for k, v in _L2_gnn_all.items() if k in ('eps',)}
    del _L2_gnn_all

    def _L3_gnn_setup():
        import jax, jax.numpy as jnp
        import numpy as np
        N = 6250
        E = 100000
        H = 64
        R = 2

        def _gru_cell(x, h, w_ih, b_ih, w_hh, b_hh):
            gi = x @ w_ih.T + b_ih
            gh = h @ w_hh.T + b_hh
            i_r, i_z, i_n = jnp.split(gi, 3, axis=1)
            h_r, h_z, h_n = jnp.split(gh, 3, axis=1)
            r = jax.nn.sigmoid(i_r + h_r)
            z = jax.nn.sigmoid(i_z + h_z)
            n = jnp.tanh(i_n + r * h_n)
            return (1.0 - z) * n + z * h
        key = jax.random.key(seed)
        ks = jax.random.split(key, 10)
        s = 1.0 / np.sqrt(H)
        return {'hv': jax.random.normal(ks[0], (N, H), jnp.float32), 'he': jax.random.normal(ks[1], (E, H), jnp.float32), 'src': jax.random.randint(ks[2], (E,), 0, N, jnp.int32), 'dst': jax.random.randint(ks[3], (E,), 0, N, jnp.int32), 'w_msg': jax.random.uniform(ks[4], (R, 2 * H, 3 * H), jnp.float32, -s, s), 'b_msg': jax.random.uniform(ks[5], (R, 2 * H), jnp.float32, -s, s), 'w_ih': jax.random.uniform(ks[6], (R, 3 * H, 2 * H), jnp.float32, -s, s), 'w_hh': jax.random.uniform(ks[7], (R, 3 * H, H), jnp.float32, -s, s), 'b_ih': jax.random.uniform(ks[8], (R, 3 * H), jnp.float32, -s, s), 'b_hh': jax.random.uniform(ks[9], (R, 3 * H), jnp.float32, -s, s)}
    _L3_gnn_all = _L3_gnn_setup()
    _L3_gnn_in = {k: v for k, v in _L3_gnn_all.items() if k in ('w_msg', 'b_msg', 'w_ih', 'w_hh', 'b_ih', 'b_hh')}
    del _L3_gnn_all
    return {'x': x, 'src': src, 'dst': dst, 'edge_attr_32': edge_attr_32, 'edge_attr_64': edge_attr_64, 'edge_weight': edge_weight, 'L0_gnn_u': _L0_gnn_in['u'], 'L0_gnn_W1': _L0_gnn_in['W1'], 'L0_gnn_b1': _L0_gnn_in['b1'], 'L0_gnn_W2': _L0_gnn_in['W2'], 'L0_gnn_b2': _L0_gnn_in['b2'], 'L1_gnn_W': _L1_gnn_in['W'], 'L1_gnn_b': _L1_gnn_in['b'], 'L2_gnn_eps': _L2_gnn_in['eps'], 'L3_gnn_w_msg': _L3_gnn_in['w_msg'], 'L3_gnn_b_msg': _L3_gnn_in['b_msg'], 'L3_gnn_w_ih': _L3_gnn_in['w_ih'], 'L3_gnn_w_hh': _L3_gnn_in['w_hh'], 'L3_gnn_b_ih': _L3_gnn_in['b_ih'], 'L3_gnn_b_hh': _L3_gnn_in['b_hh']}

def reference(x, src, dst, edge_attr_32, edge_attr_64, edge_weight, L0_gnn_u, L0_gnn_W1, L0_gnn_b1, L0_gnn_W2, L0_gnn_b2, L1_gnn_W, L1_gnn_b, L2_gnn_eps, L3_gnn_w_msg, L3_gnn_b_msg, L3_gnn_w_ih, L3_gnn_w_hh, L3_gnn_b_ih, L3_gnn_b_hh):
    import jax
    import jax.numpy as jnp

    def _L0_gnn_ref(x, edge_index, edge_attr, u, batch, W1, b1, W2, b2):
        import jax, jax.numpy as jnp
        import numpy as np
        N_NODES = 12500
        N_EDGES = 400000
        EDGE_OUT = 32
        HID = 128
        NODE_OUT = 64
        N_GRAPHS = 16
        N = x.shape[0]
        row = edge_index[0]
        seg_sum = jax.ops.segment_sum(edge_attr, row, num_segments=N)
        seg_max = jax.ops.segment_max(edge_attr, row, num_segments=N)
        cnt = jax.ops.segment_sum(jnp.ones((edge_attr.shape[0], 1), edge_attr.dtype), row, num_segments=N)
        seg_mean = seg_sum / jnp.maximum(cnt, 1.0)
        seg_max = jnp.where(cnt > 0, seg_max, 0.0)
        h = jnp.concatenate([seg_sum, seg_max, seg_mean, u[batch]], axis=1)
        h = jax.nn.relu(h @ W1 + b1)
        return h @ W2 + b2

    def _L1_gnn_ref(x, senders, receivers, W, b):
        import jax, jax.numpy as jnp
        import numpy as np
        N_NODES = 12500
        N_EDGES = 200000
        D_FEAT = 64
        EMB_DIM = 64

        def _norm_by_degree(x, degree):
            return x * jax.lax.rsqrt(jnp.maximum(degree.astype(x.dtype), 1.0))[:, None]
        n = x.shape[0]
        all_nodes = jnp.arange(n, dtype=senders.dtype)
        s = jnp.concatenate([senders, all_nodes])
        r = jnp.concatenate([receivers, all_nodes])
        ones = jnp.ones_like(s)
        deg_s = jax.ops.segment_sum(ones, s, num_segments=n)
        deg_r = jax.ops.segment_sum(ones, r, num_segments=n)
        xn = _norm_by_degree(x, deg_s)
        summed = jax.ops.segment_sum(xn[s], r, num_segments=n)
        mean = summed / jnp.maximum(deg_r.astype(x.dtype), 1.0)[:, None]
        x_updated = _norm_by_degree(mean, deg_r)
        combined = jnp.concatenate([x, x_updated], axis=-1)
        return combined @ W + b

    def _L2_gnn_ref(x, edge_index, edge_weight, eps):
        import jax, jax.numpy as jnp
        import numpy as np
        N_NODES = 6250
        N_EDGES = 100000
        D_FEAT = 64
        row, col = (edge_index[0], edge_index[1])
        w = jnp.where(row != col, edge_weight, jnp.zeros_like(edge_weight))
        msgs = w[:, None] * x[col]
        agg = jax.ops.segment_sum(msgs, row, num_segments=x.shape[0])
        return (1.0 + eps[0]) * x + agg

    def _L3_gnn_ref(hv, he, src, dst, w_msg, b_msg, w_ih, w_hh, b_ih, b_hh):
        import jax, jax.numpy as jnp
        import numpy as np
        N = 6250
        E = 100000
        H = 64
        R = 2

        def _gru_cell(x, h, w_ih, b_ih, w_hh, b_hh):
            gi = x @ w_ih.T + b_ih
            gh = h @ w_hh.T + b_hh
            i_r, i_z, i_n = jnp.split(gi, 3, axis=1)
            h_r, h_z, h_n = jnp.split(gh, 3, axis=1)
            r = jax.nn.sigmoid(i_r + h_r)
            z = jax.nn.sigmoid(i_z + h_z)
            n = jnp.tanh(i_n + r * h_n)
            return (1.0 - z) * n + z * h
        n_nodes = hv.shape[0]
        for t in range(R):
            msg_in = jnp.concatenate([hv[dst], hv[src], he], axis=1)
            e_act = msg_in @ w_msg[t].T + b_msg[t]
            a = jax.ops.segment_sum(e_act, dst, num_segments=n_nodes)
            hv = _gru_cell(a, hv, w_ih[t], b_ih[t], w_hh[t], b_hh[t])
        return hv
    edge_index = jnp.stack([src, dst])
    batch0 = jnp.zeros((6250,), jnp.int32)
    h = jnp.maximum(_layernorm(x, axis=-1), 0.0)
    x = x + _L0_gnn_ref(h, edge_index, edge_attr_32, L0_gnn_u, batch0, L0_gnn_W1, L0_gnn_b1, L0_gnn_W2, L0_gnn_b2)
    h = jnp.maximum(_layernorm(x, axis=-1), 0.0)
    x = x + _L1_gnn_ref(h, src, dst, L1_gnn_W, L1_gnn_b)
    h = jnp.maximum(_layernorm(x, axis=-1), 0.0)
    x = x + _L2_gnn_ref(h, edge_index, edge_weight, L2_gnn_eps)
    h = jnp.maximum(_layernorm(x, axis=-1), 0.0)
    x = x + _L3_gnn_ref(h, edge_attr_64, src, dst, L3_gnn_w_msg, L3_gnn_b_msg, L3_gnn_w_ih, L3_gnn_w_hh, L3_gnn_b_ih, L3_gnn_b_hh)
    return x

_drawn_inputs = setup_inputs


def setup_inputs(seed=0):
    import zlib

    import numpy as np

    out = dict(_drawn_inputs(seed))
    spreads = {'L0_gnn_b1': (0.0, 0.1), 'L0_gnn_b2': (0.0, 0.1), 'L1_gnn_b': (0.0, 0.1)}
    factors = {'L3_gnn_w_hh': 3.446, 'L3_gnn_b_ih': 23.776, 'L3_gnn_b_hh': 26.227}
    for name, (base, spread) in spreads.items():
        noise = np.random.default_rng([zlib.crc32(name.encode()), seed]).standard_normal(out[name].shape)
        drawn = base * np.exp(spread * noise) if base else spread * noise
        out[name] = jnp.asarray(drawn.astype(out[name].dtype))
    for name, factor in factors.items():
        out[name] = (out[name] * factor).astype(out[name].dtype)
    return out
```

```python
from contextlib import ExitStack

import concourse.bass as bass
from concourse import mybir
from concourse.alu_op_type import AluOpType as ALU

F32 = mybir.dt.float32
BF16 = mybir.dt.bfloat16
FP16 = mybir.dt.float16
I32 = mybir.dt.int32
ACT = mybir.ActivationFunctionType
AX_X = mybir.AxisListType.X
PE, DVE, ACTE = mybir.EngineType.PE, mybir.EngineType.DVE, mybir.EngineType.Activation
SPE = mybir.EngineType.SP

P = 128
N = 6250
E = 200000
EP = 125
NT = E // EP
D = 64
DA = 32
HID = 128
HI = -(-N // P)
W = 8
KEYW = HI * W
NWIN = 800
WBATCH = 10
WGRP = 3
SLAB_W = 50
NSLAB = NWIN // SLAB_W
SLAB = SLAB_W * W
NPAD = NWIN * W
NB = NPAD // P
HGRP = 8
TPAD = NT + WGRP
RU = 16
RG = RU // 2
QUAD = 4
NG = NT // RG
ROW = DA + 3
TB = -(-NT // P)
TLAST = NT - (TB - 1) * P
KB = -(-NWIN // P)
HUGE = 3.0e38
RANGES = "the ranges are worked out within the tiles"


class Scope(ExitStack):

    spent = []
    made = 0

    def __init__(self, nc, turn=""):
        super().__init__()
        self.nc, self.turn = nc, turn

    def sb(self, name, shape, dt):
        return self.enter_context(self.nc.sbuf_tensor(name + self.turn, shape, dt))

    def ps(self, name, shape, dt=F32):
        return self.enter_context(self.nc.psum_tensor(name + self.turn, shape, dt))

    def sem(self, name):
        Scope.made += 1
        handle = self.nc.alloc_semaphore(f"{name}_{Scope.made}")
        self.spent.append(handle)
        return handle

    def block(self):
        return self.enter_context(self.nc.Block())


class Serial:

    def __init__(self, eng, sem):
        self.eng, self.sem, self.n = eng, sem, 0

    def __call__(self, ins):
        self.n += 1
        ins.then_inc(self.sem, 1)
        self.eng.wait_ge(self.sem, self.n)


def clear_spent(nc):
    nc.clear_and_free_semaphores(Scope.spent)
    Scope.spent.clear()
    nc.all_engine_barrier()


def two_parts(queue, out, in_, sem):
    queue.dma_start(out[0:112], in_[0:112]).then_inc(sem, 16)
    queue.dma_start(out[112:EP], in_[112:EP]).then_inc(sem, 16)


def prepare_keys(nc, g, src, dst, edge_weight):
    with Scope(nc) as s:
        raw_i = s.sb("raw_i", [EP, 2, NT], I32)
        raw_w = s.sb("raw_w", [EP, NT], F32)
        part_i = s.sb("part_i", [EP, NT], I32)
        tile_i = s.sb("tile_i", [P, 2, TB, EP], I32)
        tile_f = s.sb("tile_f", [P, 2, TB, EP], F32)
        key_i = s.sb("key_i", [EP, 4, NT], I32)
        count_i = s.sb("count_i", [P, NWIN], I32)
        turned = s.ps("turned", [P, 8, 512])
        loaded = s.sem("loaded")
        consts = s.sem("consts")
        dve_step = s.sem("dve_step")
        tiles_float = s.sem("tiles_float")
        turned_ready = s.sem("turned_ready")
        turned_used = s.sem("turned_used")
        block = s.block()
        @block.sync
        def _(sp):
            sp.dma_start(raw_i[:, 0, :], src.rearrange("(p j) -> p j", p=EP)).then_inc(loaded, 16)
            sp.dma_start(raw_i[:, 1, :], dst.rearrange("(p j) -> p j", p=EP)).then_inc(loaded, 16)
            sp.dma_start(raw_w[:, :], edge_weight.rearrange("(p j) -> p j", p=EP)).then_inc(loaded, 16)

        @block.scalar
        def _(act):
            for n, x in enumerate((src, dst)):
                rows = x.rearrange("(t e) -> t e", e=EP)
                full = (TB - 1) * P
                act.dma_start(tile_i[:, n, 0:TB - 1, :],
                              rows[0:full, :].rearrange("(b t) e -> t b e", t=P)).then_inc(loaded, 16)
                act.dma_start(tile_i[0:TLAST, n, TB - 1, :], rows[full:NT, :]).then_inc(loaded, 16)

        @block.gpsimd
        def _(pool):
            pool.iota(count_i[:, :], pattern=[[1, NWIN]], base=0, channel_multiplier=0).then_inc(consts, 1)
            pool.iota(g["rowid_i"][:, :], pattern=[[0, 1]], base=0, channel_multiplier=1).then_inc(consts, 1)
            pool.memset(g["ident"][:, :], 0.0).then_inc(consts, 1)
            pool.memset(g["below"][:, :], 1.0).then_inc(consts, 1)
            pool.memset(g["ones"][:, :], 1.0).then_inc(consts, 1)
            pool.wait_ge(consts, 5)
            pool.affine_select(out=g["ident"][:, :], in_=g["ident"][:, :], compare_op=ALU.not_equal, fill=1.0,
                               base=0, pattern=[[-1, P]], channel_multiplier=1).then_inc(consts, 1)
            pool.affine_select(out=g["below"][:, :], in_=g["below"][:, :], compare_op=ALU.is_gt, fill=0.0,
                               base=0, pattern=[[1, P]], channel_multiplier=-1).then_inc(consts, 1)
            pool.tensor_copy(g["iota"][:, :], count_i[:, 0:512]).then_inc(consts, 1)
            pool.tensor_copy(g["rowid"][:, :], g["rowid_i"][:, :]).then_inc(consts, 1)
            pool.memset(g["mkeys"][:, NT:TPAD], -1.0).then_inc(consts, 1)
            pool.memset(g["skeys"][:, NT:TPAD], -1.0).then_inc(consts, 1)

        @block.tensor
        def _(pe):
            pe.wait_ge(tiles_float, 4)
            pe.wait_ge(consts, 11)
            for n in range(2):
                for b in range(TB):
                    rows = P if b < TB - 1 else TLAST
                    last = nc.tensor.transpose(turned[0:EP, 4 * n + b // 4, (b % 4) * P:(b % 4) * P + rows],
                                               tile_f[0:rows, n, b, :], g["ident"][0:rows, 0:rows])
                last.then_inc(turned_ready, 1)

        @block.vector
        def _(dve):
            step = Serial(dve, dve_step)
            dve.wait_ge(loaded, 7 * 16)
            for n in range(2):
                nc.vector.tensor_copy(tile_f[:, n, 0:TB - 1, :], tile_i[:, n, 0:TB - 1, :]).then_inc(tiles_float, 1)
                nc.vector.tensor_copy(tile_f[0:TLAST, n, TB - 1, :],
                                      tile_i[0:TLAST, n, TB - 1, :]).then_inc(tiles_float, 1)
            dve.wait_ge(consts, 11)
            nc.vector.memset(g["zerob"][:, :], 0.0).then_inc(dve_step, 1)
            nc.vector.tensor_copy(g["identb"][:, :], g["ident"][:, :]).then_inc(dve_step, 1)
            nc.vector.tensor_copy(g["belowb"][:, :], g["below"][:, :]).then_inc(dve_step, 1)
            nc.vector.tensor_scalar(g["winbase"][:, :], count_i[:, :], 512.0, None, ALU.mult).then_inc(dve_step, 1)
            nc.vector.tensor_copy(g["sdw"][:, :, 0], raw_i[:, 0, :]).then_inc(dve_step, 1)
            nc.vector.tensor_copy(g["sdw"][:, :, 1], raw_i[:, 1, :]).then_inc(dve_step, 1)
            nc.vector.tensor_copy(g["sdw"][:, :, 2], raw_w[:, :]).then_inc(dve_step, 1)
            step.n = 7
            step(nc.vector.tensor_single_scalar(part_i[:, :], raw_i[:, 0, :], P - 1, ALU.bitwise_and))
            step(nc.vector.tensor_copy(g["lo"][:, 0:NT], part_i[:, :]))
            step(nc.vector.tensor_single_scalar(part_i[:, :], raw_i[:, 0, :], 7, ALU.arith_shift_right))
            step(nc.vector.tensor_copy(g["hi"][:, 0:NT], part_i[:, :]))
            step(nc.vector.memset(g["lo"][:, NT:NT + RG], 0.0))
            step(nc.vector.memset(g["hi"][:, NT:NT + RG], 0.0))
            step(nc.vector.tensor_copy(g["iota_rg"][:, :, :], g["iota"][:, 0:P].unsqueeze(2).broadcast_to([P, P, RG])))
            dve.wait_ge(tiles_float, 4)
            for op, c in ((ALU.min, 0), (ALU.max, 1)):
                step(nc.vector.tensor_reduce(g["span"][:, c, 0:TB - 1], tile_f[:, 1, 0:TB - 1, :], AX_X, op))
                step(nc.vector.tensor_reduce(g["span"][0:TLAST, c, TB - 1:TB], tile_f[0:TLAST, 1, TB - 1:TB, :],
                                             AX_X, op))
            for n in range(2):
                dve.wait_ge(turned_ready, n + 1)
                flat = turned[0:EP, 4 * n:4 * n + 4, :].rearrange("p a b -> p (a b)")
                if n:
                    step(nc.vector.tensor_copy(g["dkey"][:, 0:NT], flat[:, 0:NT]))
                step(nc.vector.tensor_copy(key_i[:, n, :], flat[:, 0:NT]))
            s_i, d_i, u_i, v_i = (key_i[:, n, :] for n in range(4))
            step(nc.vector.tensor_single_scalar(u_i, d_i, 3, ALU.arith_shift_right))
            step(nc.vector.tensor_single_scalar(v_i, d_i, W - 1, ALU.bitwise_and))
            step(nc.vector.tensor_single_scalar(d_i, s_i, 7, ALU.arith_shift_right))
            step(nc.vector.scalar_tensor_tensor(raw_w[:, :], d_i, float(W), v_i, ALU.mult, ALU.add))
            step(nc.vector.scalar_tensor_tensor(g["mkeys"][:, 0:NT], u_i, 512.0, raw_w[:, :], ALU.mult, ALU.add))
            step(nc.vector.tensor_single_scalar(v_i, s_i, P - 1, ALU.bitwise_and))
            step(nc.vector.scalar_tensor_tensor(g["skeys"][:, 0:NT], u_i, 512.0, v_i, ALU.mult, ALU.add))


def one_hots(nc, g, out_lo, out_hi, n):
    def keys(x, width):
        return x[:, bass.ds(n * RG, RG)].unsqueeze(1).broadcast_to([EP, width, RG])
    nc.vector.tensor_tensor(out_lo, g["iota_rg"][0:EP, :, :], keys(g["lo"], P), ALU.is_equal)
    return nc.vector.tensor_tensor(out_hi, g["iota_rg"][0:EP, 0:HI, :], keys(g["hi"], HI), ALU.is_equal)


def count_sources(nc, g):
    with Scope(nc) as s:
        oh_lo = s.sb("hist_lo", [EP, 2, P, RG], BF16)
        oh_hi = s.sb("hist_hi", [EP, 2, HI, RG], BF16)
        totals = s.sb("totals", [P, HI], F32)
        upto = s.sb("upto", [P, HI], F32)
        zeros = s.sb("zeros", [P, HI], F32)
        hist = s.ps("hist", [P, HI])
        sums = s.ps("sums", [P, 2, HI])
        oh_ready = s.sem("oh_ready")
        oh_used = s.sem("oh_used")
        sums_ready = s.sem("sums_ready")
        dve_step = s.sem("dve_step")
        block = s.block()
        @block.vector
        def _(dve):
            step = Serial(dve, dve_step)
            step(nc.vector.memset(zeros[:, :], 0.0))
            with dve.Fori(0, NG // 2) as i:
                for h in range(2):
                    dve.wait_ge(oh_used, 2 * i + h + 1)
                    one_hots(nc, g, oh_lo[:, h], oh_hi[:, h], 2 * i + h).then_inc(oh_ready, 1)
            dve.wait_ge(oh_used, NG + 2)
            step(nc.vector.tensor_copy(g["out_deg"][:, 0:HI], hist[:, :]))
            step(nc.vector.memset(g["out_deg"][:, HI:NB], 0.0))
            dve.wait_ge(sums_ready, 1)
            step(nc.vector.tensor_copy(totals[:, :], sums[:, 1, :]))
            step(nc.vector.tensor_tensor_scan(upto[:, :], totals[:, :], zeros[:, :], 0.0, ALU.add, ALU.add))
            step(nc.vector.tensor_tensor(upto[:, :], upto[:, :], totals[:, :], ALU.subtract))
            step(nc.vector.tensor_tensor(g["start"][:, 0:HI], sums[:, 0, :], upto[:, :], ALU.add))

        @block.tensor
        def _(pe):
            pe.sem_inc(oh_used, 2)
            nc.tensor.matmul(hist[:, :], g["zerob"][:, 0:P], g["zerob"][:, 0:HI], start=True, stop=True)
            with pe.Fori(0, NG // 2) as i:
                for h in range(2):
                    pe.wait_ge(oh_ready, 2 * i + h + 1)
                    for u in range(RG):
                        last = nc.tensor.matmul(hist[:, :], oh_lo[:, h, :, u], oh_hi[:, h, :, u], start=False,
                                                stop=True, skip_group_check=True)
                    last.then_inc(oh_used, 1)
            pe.wait_ge(dve_step, 2)
            nc.tensor.matmul(sums[:, 0, :], g["below"][:, :], g["out_deg"][:, 0:HI], start=True, stop=True)
            nc.tensor.matmul(sums[:, 1, :], g["ones"][:, :], g["out_deg"][:, 0:HI], start=True,
                             stop=True).then_inc(sums_ready, 1)


def rank_and_scatter(nc, g, edge_attr_32, sorted_rows):
    with Scope(nc) as s:
        oh_lo = s.sb("oh_lo", [EP, 2, P, RG], BF16)
        oh_hi = s.sb("oh_hi", [EP, 2, HI, RG], BF16)
        lo_rows_b = s.sb("lo_rows_b", [P, 2, 2, QUAD, EP], BF16)
        lo_rows_f = s.sb("lo_rows_f", [P, 2, 2, QUAD, EP], F32)
        earlier = s.sb("earlier", [EP, 2, 2, QUAD, EP], BF16)
        counts = s.sb("counts", [P, 2, HI], F32)
        picked = s.sb("picked", [EP, 2, RG, HI], BF16)
        place = s.sb("place", [EP, 2, RG], F32)
        place_i = s.sb("place_i", [EP, 2, RG], I32)
        attr = s.sb("attr", [EP, 2, RG, DA], F32)
        rows = s.sb("rows", [EP, 2, RG, ROW], F32)
        turned0 = s.ps("turned0", [P, QUAD, P], BF16)
        turned1 = s.ps("turned1", [P, QUAD, P], BF16)
        same0 = s.ps("same0", [EP, QUAD * EP])
        same1 = s.ps("same1", [EP, QUAD * EP])
        count_rows = [s.ps(f"count_rows{b}", [EP, 2, HI]) for b in range(2)]
        running = s.ps("running", [P, HI])
        oh_ready = s.sem("oh_ready")
        turned_ready = s.sem("turned_ready")
        lo_rows_ready = s.sem("lo_rows_ready")
        same_ready = s.sem("same_ready")
        earlier_ready = s.sem("earlier_ready")
        counts_ready = s.sem("counts_ready")
        count_rows_ready = s.sem("count_rows_ready")
        updated = s.sem("updated")
        placed = s.sem("placed")
        places_ready = s.sem("places_ready")
        rows_ready = s.sem("rows_ready")
        attr0 = s.sem("attr0")
        attr1 = s.sem("attr1")
        scattered0 = s.sem("scattered0")
        scattered1 = s.sem("scattered1")
        pool_turns = s.sem("pool_turns")
        block = s.block()
        turned, same = (turned0, turned1), (same0, same1)
        attr_in, scattered = (attr0, attr1), (scattered0, scattered1)
        attrs = edge_attr_32.rearrange("(p j) c -> p (j c)", p=EP)
        ALL = 16 * RG

        @block.sync
        def _(sp):
            with sp.Fori(0, NG // 2) as i:
                for h in range(2):
                    sp.wait_ge(rows_ready, 2 * i + h + 1)
                    sp.dma_start(attr[:, h].rearrange("p j c -> p (j c)"),
                                 attrs[:, bass.ds((2 * i + h) * RG * DA, RG * DA)]).then_inc(attr_in[h], 16)

        @block.gpsimd
        def _(pool):
            with pool.Fori(0, NG // 2) as i:
                for h in range(2):
                    pool.wait_ge(places_ready, 2 * i + h + 1)
                    pool.wait_ge(rows_ready, 2 * i + h + 3)
                    pool.sem_inc(pool_turns, 1)
                    for u in range(RG):
                        pool.indirect_dma_start(sorted_rows[:, :],
                                                bass.IndirectOffsetOnAxis(ap=place_i[:, h, u:u + 1], axis=0),
                                                rows[:, h, u, :], None).then_inc(scattered[h], 16)
            for h in range(2):
                pool.wait_ge(scattered[h], ALL * NG // 2)

        @block.vector
        def _(dve):
            def lo_hi(n, h):
                one_hots(nc, g, oh_lo[:, h], oh_hi[:, h], n).then_inc(oh_ready, 1)

            def mask(n, h):
                for q in range(2):
                    dve.wait_ge(same_ready, 2 * n + q + 1)
                    nc.vector.tensor_tensor(earlier[:, h, q], same[q][:, :].rearrange("p (u e) -> p u e", u=QUAD),
                                            g["belowb"][0:EP, 0:EP].unsqueeze(1).broadcast_to([EP, QUAD, EP]),
                                            ALU.mult).then_inc(earlier_ready, 1)

            def pick(n, h, u):
                if u % 2 == 0:
                    dve.wait_ge(count_rows_ready, n * RG + u + 3)
                nc.vector.tensor_tensor_reduce(out=picked[:, h, u, :], in0=count_rows[u // 2 % 2][:, u % 2, :],
                                               in1=oh_hi[:, h, :, u], scale=1.0, scalar=0.0, op0=ALU.mult,
                                               op1=ALU.add, accum_out=place[:, h, u:u + 1]).then_inc(placed, 1)

            dve.sem_inc(placed, 4)
            lo_hi(0, 0)
            mask(0, 0)
            def turn(i, first):
                for h in range(2):
                    n = 2 * i + h
                    dve.wait_ge(count_rows_ready, n * RG + 1)
                    dve.wait_ge(placed, n * RG + 4)
                    lo_hi(n + 1, 1 - h)
                    for u in range(RG):
                        pick(n, h, u)
                        if u == 3:
                            mask(n + 1, 1 - h)
                    dve.wait_ge(placed, n * RG + RG + 4)
                    if not first:
                        dve.wait_ge(scattered[h], ALL * i)
                    nc.vector.tensor_copy(place_i[:, h, :], place[:, h, :]).then_inc(places_ready, 1)

            turn(0, True)
            with dve.Fori(1, NG // 2) as i:
                turn(i, False)

        @block.scalar
        def _(act):
            act.sem_inc(rows_ready, 2)

            def lo_rows(n, h, q):
                act.wait_ge(turned_ready, 2 * n + q + 1)
                nc.scalar.copy(lo_rows_b[:, h, q], turned[q][:, :, 0:EP])
                nc.scalar.copy(lo_rows_f[:, h, q], turned[q][:, :, 0:EP]).then_inc(lo_rows_ready, 1)

            nc.scalar.copy(counts[:, 0, :], g["start"][:, 0:HI]).then_inc(counts_ready, 1)
            for q in range(2):
                lo_rows(0, 0, q)
            def turn(i, first):
                for h in range(2):
                    n = 2 * i + h
                    for u in range(RG):
                        if u in (1, 2):
                            lo_rows(n + 1, 1 - h, u - 1)
                        if u == 6:
                            act.wait_ge(attr_in[h], 16 * (i + 1))
                            if not first:
                                act.wait_ge(scattered[h], ALL * i)
                            nc.scalar.copy(rows[:, h, :, 0:DA], attr[:, h])
                            nc.scalar.copy(rows[:, h, :, DA:ROW],
                                           g["sdw"][:, bass.ds(n * RG, RG), :]).then_inc(rows_ready, 1)
                        act.wait_ge(updated, n * RG + u + 1)
                        nc.scalar.copy(counts[:, (u + 1) % 2, :], running[:, :]).then_inc(counts_ready, 1)

            turn(0, True)
            with act.Fori(1, NG // 2) as i:
                turn(i, False)

        @block.tensor
        def _(pe):
            pe.sem_inc(count_rows_ready, 1)

            def turn(n, h):
                pe.wait_ge(oh_ready, n + 1)
                for q in range(2):
                    for u in range(QUAD):
                        last = nc.tensor.transpose(turned[q][:, u, 0:EP],
                                                   oh_lo[:, h, :, q * QUAD + u], g["identb"][0:EP, 0:EP])
                    last.then_inc(turned_ready, 1)

            def compare(n, h):
                for q in range(2):
                    pe.wait_ge(lo_rows_ready, 2 * n + q + 1)
                    for u in range(QUAD):
                        x = lo_rows_b[:, h, q, u, :]
                        last = nc.tensor.matmul(same[q][:, u * EP:(u + 1) * EP], x, x, start=True, stop=True)
                    last.then_inc(same_ready, 1)

            def chain(n, h, u):
                q, v = divmod(u, QUAD)
                if v == 0:
                    pe.wait_ge(earlier_ready, 2 * n + q + 1)
                pe.wait_ge(counts_ready, n * RG + u + 1)
                nc.tensor.matmul(running[:, :], oh_lo[:, h, :, u], oh_hi[:, h, :, u], start=False, stop=True,
                                 skip_group_check=True).then_inc(updated, 1)
                if u % 2 == 0:
                    pe.wait_ge(placed, n * RG + u + 2)
                out = count_rows[u // 2 % 2][:, u % 2, :]
                nc.tensor.matmul(out, lo_rows_f[:, h, q, v, :], counts[:, u % 2, :], start=True, stop=False)
                nc.tensor.matmul(out, earlier[:, h, q, v, :], oh_hi[:, h, :, u], start=False,
                                 stop=True).then_inc(count_rows_ready, 1)

            nc.tensor.matmul(running[:, :], g["ident"][:, :], g["start"][:, 0:HI], start=True, stop=True)
            turn(0, 0)
            compare(0, 0)
            with pe.Fori(0, NG // 2) as i:
                for h in range(2):
                    n = 2 * i + h
                    turn(n + 1, 1 - h)
                    for u in range(RG):
                        if u == 3:
                            compare(n + 1, 1 - h)
                        chain(n, h, u)


def scan_sorted(nc, g, sorted_rows, scanned, carries):
    J = 160
    STEPS = NT // J
    with Scope(nc) as s:
        rows = [s.sb(f"scan_rows{b}", [EP, J, ROW], F32) for b in range(2)]
        out = [s.sb(f"scan_out{b}", [EP, J, 2 * DA], F32) for b in range(2)]
        cap = s.sb("cap", [EP, J], F32)
        differs = s.sb("differs", [EP, J], F32)
        last_key = s.sb("last_key", [EP, 1], F32)
        carry = s.sb("carry", [EP, 2 * DA], F32)
        state = s.sb("state", [2 * DA, EP], F32)
        turned_carry = s.sb("turned_carry", [2 * DA, EP], F32)
        key_row = s.sb("key_row", [2 * DA, EP], F32)
        keep = s.sb("keep", [2 * DA, EP], F32)
        keep_cap = s.sb("keep_cap", [DA, EP], F32)
        carry_in = s.sb("carry_in", [EP, 2 * DA], F32)
        ps_carry = s.ps("ps_carry", [2 * DA, EP])
        ps_key = s.ps("ps_key", [2 * DA, EP])
        ps_in = s.ps("ps_in", [EP, 2 * DA])
        rows_in = [s.sem(f"rows_in{b}") for b in range(2)]
        rows_out = [s.sem(f"rows_out{b}") for b in range(2)]
        dve_step = s.sem("dve_step")
        scans_done = s.sem("scans_done")
        pe_done = s.sem("pe_done")
        shifted = s.sem("shifted")
        carried = s.sem("carried")
        block = s.block()
        src_v = sorted_rows[:, :].rearrange("(p j) c -> p j c", p=EP)
        dst_v = scanned[:, :].rearrange("(p j) c -> p j c", p=EP)

        @block.sync
        def _(sp):
            for k in range(STEPS):
                if k >= 2:
                    sp.wait_ge(scans_done, k - 1)
                two_parts(sp, rows[k % 2][:, :, :], src_v[:, k * J:(k + 1) * J, :], rows_in[k % 2])

        @block.scalar
        def _(act):
            for k in range(STEPS):
                act.wait_ge(scans_done, k + 1)
                two_parts(act, dst_v[:, k * J:(k + 1) * J, :], out[k % 2][:, :, :], rows_out[k % 2])
            act.wait_ge(carried, 1)
            act.dma_start(carries[:, :], carry_in[:, :]).then_inc(rows_out[0], 16)
            act.wait_ge(rows_out[0], 16 * (STEPS + 1))
            act.wait_ge(rows_out[1], 16 * STEPS)

        @block.vector
        def _(dve):
            step = Serial(dve, dve_step)
            step(nc.vector.memset(last_key[:, :], -1.0))
            step(nc.vector.memset(carry[:, :], 0.0))
            for k in range(STEPS):
                rk, ok = rows[k % 2], out[k % 2]
                same = g["same_src"][:, k * J:(k + 1) * J]
                dve.wait_ge(rows_in[k % 2], 32 * (k // 2 + 1))
                src_c, dst_c, w_c = (rk[:, :, DA + c] for c in range(3))
                nc.vector.tensor_tensor(same[:, 0:1], src_c[:, 0:1], last_key[:, :], ALU.is_equal)
                step(nc.vector.tensor_tensor(same[:, 1:J], src_c[:, 1:J], src_c[:, 0:J - 1], ALU.is_equal))
                nc.vector.tensor_scalar(cap[:, :], same, -0.5, HUGE, ALU.add, ALU.mult)
                nc.vector.tensor_copy(last_key[:, :], src_c[:, J - 1:J])
                nc.vector.tensor_copy(g["dst_sorted"][:, k * J:(k + 1) * J], dst_c)
                step(nc.vector.tensor_tensor(differs[:, :], src_c, dst_c, ALU.not_equal))
                step(nc.vector.tensor_tensor(g["w_sorted"][:, k * J:(k + 1) * J], w_c, differs[:, :], ALU.mult))
                if k >= 2:
                    dve.wait_ge(rows_out[k % 2], 32 * (k // 2))
                for f in range(DA):
                    nc.vector.tensor_tensor_scan(ok[:, :, f], cap[:, :], rk[:, :, f], carry[:, f:f + 1],
                                                 ALU.min, ALU.max)
                    last = nc.vector.tensor_tensor_scan(ok[:, :, DA + f], same, rk[:, :, f],
                                                        carry[:, DA + f:DA + f + 1], ALU.mult, ALU.add)
                last.then_inc(scans_done, 1)
                dve.wait_ge(scans_done, k + 1)
                step(nc.vector.tensor_copy(carry[:, :], ok[:, J - 1, :]))
            dve.wait_ge(pe_done, 1)
            step(nc.vector.tensor_copy(turned_carry[:, :], ps_carry[:, :]))
            step(nc.vector.tensor_copy(key_row[:, :], ps_key[:, :]))
            step(nc.vector.memset(keep[:, 0:1], 0.0))
            step(nc.vector.tensor_tensor(keep[:, 1:EP], key_row[:, 1:EP], key_row[:, 0:EP - 1], ALU.is_equal))
            step(nc.vector.tensor_copy(g["keep_run"][:, :], keep[:, :]))
            step(nc.vector.tensor_scalar(keep_cap[:, :], keep[0:DA, :], -0.5, HUGE, ALU.add, ALU.mult))
            step(nc.vector.memset(state[:, 0:1], 0.0))
            step(nc.vector.tensor_tensor_scan(state[0:DA, 1:EP], keep_cap[:, 0:EP - 1], turned_carry[0:DA, 0:EP - 1],
                                              0.0, ALU.min, ALU.max))
            step(nc.vector.tensor_tensor_scan(state[DA:2 * DA, 1:EP], keep[DA:2 * DA, 0:EP - 1],
                                              turned_carry[DA:2 * DA, 0:EP - 1], 0.0, ALU.mult, ALU.add))
            nc.vector.sem_inc(shifted, 1)
            dve.wait_ge(pe_done, 2)
            nc.vector.tensor_copy(carry_in[:, :], ps_in[:, :]).then_inc(carried, 1)

        @block.tensor
        def _(pe):
            pe.wait_ge(dve_step, 2 + 4 * STEPS)
            nc.tensor.matmul(ps_key[:, :], last_key[:, :].broadcast_to([EP, 2 * DA]), g["ident"][0:EP, 0:EP],
                             start=True, stop=True)
            nc.tensor.transpose(ps_carry[:, :], carry[:, :], g["ident"][0:EP, 0:EP]).then_inc(pe_done, 1)
            pe.wait_ge(shifted, 1)
            nc.tensor.transpose(ps_in[:, :], state[:, :], g["ident"][0:2 * DA, 0:2 * DA]).then_inc(pe_done, 1)


def locate_runs(nc, g):
    with Scope(nc) as s:
        end = s.sb("end", [P, HI], F32)
        part = s.sb("part", [P, HI], F32)
        rest = s.sb("rest", [P, HI], F32)
        test = s.sb("test", [P, HI], F32)
        part_i = s.sb("run_part_i", [P, HI], I32)
        dve_step = s.sem("dve_step")
        block = s.block()

        @block.vector
        def _(dve):
            step = Serial(dve, dve_step)
            start, deg = g["start"][:, 0:HI], g["out_deg"][:, 0:HI]
            step(nc.vector.tensor_tensor(end[:, :], start, deg, ALU.add))
            step(nc.vector.tensor_scalar(end[:, :], end[:, :], -1.0, 0.0, ALU.add, ALU.max))
            step(nc.vector.tensor_copy(g["end_i"][:, :], end[:, :]))
            step(nc.vector.tensor_scalar(part[:, :], end[:, :], 1.0 / NT, None, ALU.mult))
            step(nc.vector.tensor_copy(part_i[:, :], part[:, :]))
            step(nc.vector.tensor_copy(part[:, :], part_i[:, :]))
            step(nc.vector.scalar_tensor_tensor(rest[:, :], part[:, :], -float(NT), end[:, :], ALU.mult, ALU.add))
            step(nc.vector.tensor_scalar(test[:, :], rest[:, :], float(NT), None, ALU.is_ge))
            step(nc.vector.tensor_tensor(part[:, :], part[:, :], test[:, :], ALU.add))
            step(nc.vector.tensor_scalar(test[:, :], rest[:, :], 0.0, None, ALU.is_lt))
            step(nc.vector.tensor_tensor(part[:, :], part[:, :], test[:, :], ALU.subtract))
            step(nc.vector.tensor_copy(g["end_part_i"][:, :], part[:, :]))
            step(nc.vector.scalar_tensor_tensor(test[:, :], part[:, :], float(NT), start, ALU.mult, ALU.is_gt))
            step(nc.vector.tensor_scalar(g["has_out"][:, :], deg, 0.0, None, ALU.is_gt))
            step(nc.vector.tensor_tensor(g["spans"][:, :], test[:, :], g["has_out"][:, :], ALU.mult))


def gather_runs(nc, pool, g, scanned, carries, ends, carry_in, sem):
    for b in range(HI):
        pool.indirect_dma_start(ends[:, b, :], None, scanned[:, :],
                                bass.IndirectOffsetOnAxis(ap=g["end_i"][:, b:b + 1], axis=0)).then_inc(sem, 16)
        pool.indirect_dma_start(carry_in[:, b, :], None, carries[:, :],
                                bass.IndirectOffsetOnAxis(ap=g["end_part_i"][:, b:b + 1], axis=0)
                                ).then_inc(sem, 16)


def find_ranges(nc, g, scratch):
    Q = KB + 1
    ROWLEN = Q * P
    with Scope(nc) as s:
        least = s.sb("least", [P, NT], F32)
        greatest = s.sb("greatest", [P, NT], F32)
        count_i = s.sb("tile_count_i", [P, NT], I32)
        up = s.sb("up", [P, NT], F32)
        down = s.sb("down", [P, NT], F32)
        meets = s.sb("meets", [P, NT], F32)
        meets2 = s.sb("meets2", [P, NT], F32)
        first_t = s.sb("first_target", [P, Q], F32)
        last_t = s.sb("last_target", [P, Q], F32)
        ends = s.sb("range_ends", [P, 2, Q], F32)
        turned_sb = s.sb("ranges_turned", [Q, 2, P], F32)
        row = s.sb("range_row", [1, 2, ROWLEN], F32)
        steps = s.sb("range_steps", [1, ROWLEN], F32)
        steps_i = s.sb("range_steps_i", [1, ROWLEN], I32)
        cum = s.sb("range_cum", [1, ROWLEN], F32)
        zero = s.sb("range_zero", [1, ROWLEN], F32)
        spread = s.ps("spread", [P, 8, 512])
        consts = s.sem("consts")
        spread_ready = s.sem("spread_ready")
        dve_step = s.sem("dve_step")
        ends_ready = s.sem("ends_ready")
        turned_ready = s.sem("turned_ready")
        stored = s.sem("stored")
        rows_ready = s.sem("rows_ready")
        block = s.block()

        @block.gpsimd
        def _(pool):
            pool.iota(count_i[:, :], pattern=[[1, NT]], base=0, channel_multiplier=0).then_inc(consts, 1)
            pool.memset(zero[:, :], 0.0).then_inc(consts, 1)

        @block.tensor
        def _(pe):
            for c in range(2):
                for b in range(TB):
                    rows = P if b < TB - 1 else TLAST
                    last = nc.tensor.matmul(spread[:, 4 * c + b // 4, (b % 4) * P:(b % 4) * P + rows],
                                            g["span"][0:rows, c, b:b + 1].broadcast_to([rows, P]),
                                            g["ident"][0:rows, 0:rows], start=True, stop=True)
            last.then_inc(spread_ready, 1)
            pe.wait_ge(ends_ready, 1)
            for c in range(2):
                last = nc.tensor.transpose(spread[0:Q, 0, c * P:(c + 1) * P], ends[:, c, :], g["ident"][:, :])
            last.then_inc(turned_ready, 1)

        @block.vector
        def _(dve):
            step = Serial(dve, dve_step)
            for q in range(KB):
                step(nc.vector.tensor_scalar(first_t[:, q:q + 1], g["rowid"][:, :], float(W), float(W * P * q),
                                             ALU.mult, ALU.add))
            step(nc.vector.tensor_scalar(first_t[:, KB:Q], g["rowid"][:, :], float(P), None, ALU.mult))
            step(nc.vector.tensor_scalar(last_t[:, 0:KB], first_t[:, 0:KB], float(W - 1), None, ALU.add))
            step(nc.vector.tensor_scalar(last_t[:, KB:Q], first_t[:, KB:Q], float(P - 1), None, ALU.add))
            dve.wait_ge(consts, 2)
            step(nc.vector.tensor_scalar(up[:, :], count_i[:, :], 1.0, None, ALU.add))
            step(nc.vector.tensor_scalar(down[:, :], count_i[:, :], -1.0, float(NT), ALU.mult, ALU.add))
            dve.wait_ge(spread_ready, 1)
            for x, c in ((least, 0), (greatest, 1)):
                step(nc.vector.tensor_copy(x[:, :], spread[:, 4 * c:4 * c + 4, :].rearrange("p a b -> p (a b)")[:, 0:NT]))
            for q in range(Q):
                step(nc.vector.tensor_scalar(meets[:, :], least[:, :], last_t[:, q:q + 1], None, ALU.is_le))
                step(nc.vector.scalar_tensor_tensor(meets[:, :], greatest[:, :], first_t[:, q:q + 1], meets[:, :],
                                                    ALU.is_ge, ALU.mult))
                for x, c in ((up, 0), (down, 1)):
                    step(nc.vector.tensor_tensor_reduce(out=meets2[:, :], in0=meets[:, :], in1=x[:, :], scale=1.0,
                                                        scalar=0.0, op0=ALU.mult, op1=ALU.max,
                                                        accum_out=ends[:, c, q:q + 1]))
            dve.sem_inc(ends_ready, 1)
            dve.wait_ge(turned_ready, 1)
            nc.vector.tensor_copy(turned_sb[:, :, :], spread[0:Q, 0, 0:2 * P].rearrange("q (c p) -> q c p", c=2)
                                  ).then_inc(rows_ready, 1)
            dve.wait_ge(stored, 32)
            behind, left = row[:, 0, :], row[:, 1, :]
            step(nc.vector.tensor_tensor(steps[:, :], behind, left, ALU.add))
            step(nc.vector.tensor_scalar(steps[:, :], steps[:, :], -float(NT), 1.0, ALU.add, ALU.max))
            step(nc.vector.tensor_scalar(left, left, -1.0, float(NT), ALU.mult, ALU.add))
            step(nc.vector.tensor_scalar(left, left, float(NT - 1), None, ALU.min))
            win, blk = slice(0, NWIN), slice(KB * P, KB * P + NB)
            step(nc.vector.tensor_scalar(steps[:, win], steps[:, win], float(WGRP - 1), 683.0, ALU.add, ALU.mult))
            step(nc.vector.tensor_scalar(steps[:, blk], steps[:, blk], float(HGRP - 1), None, ALU.add))
            for part, shift in ((win, 11), (blk, 3)):
                step(nc.vector.tensor_copy(steps_i[:, part], steps[:, part]))
                step(nc.vector.tensor_single_scalar(steps_i[:, part], steps_i[:, part], shift,
                                                    ALU.arith_shift_right))
                step(nc.vector.tensor_copy(steps[:, part], steps_i[:, part]))
            step(nc.vector.tensor_scalar(cum[:, blk], steps[:, blk], -float(HGRP), float(NT), ALU.mult, ALU.add))
            step(nc.vector.tensor_tensor(left[:, blk], left[:, blk], cum[:, blk], ALU.min))
            for part, n, size, table in ((win, NWIN, WGRP, g["win_table"]), (blk, NB, HGRP, g["blk_table"])):
                step(nc.vector.tensor_tensor_scan(cum[:, part], steps[:, part], zero[:, part], 0.0, ALU.add, ALU.add))
                step(nc.vector.memset(table[:, 0:2 * n + 2], 0))
                step(nc.vector.tensor_copy(table[:, 2:2 * n + 2:2], cum[:, part]))
                step(nc.vector.tensor_tensor(cum[:, part], cum[:, part], steps[:, part], ALU.subtract))
                step(nc.vector.scalar_tensor_tensor(table[:, 1:2 * n + 1:2], cum[:, part], float(size), left[:, part],
                                                    ALU.mult, ALU.subtract))

        @block.sync
        def _(sp):
            sp.wait_ge(rows_ready, 1)
            sp.dma_start(scratch[:, :, :].rearrange("c q p -> q c p"), turned_sb[:, :, :]).then_inc(stored, 16)
            sp.wait_ge(stored, 16)
            sp.dma_start(row[:, :, :], scratch[:, :, :].rearrange("c q p -> c (q p)").unsqueeze(0)).then_inc(stored, 16)


def load_ranges(nc, table, engine, first, count, most):
    _, v = nc.values_load_multi_w_load_instructions(table[0:1, bass.ds(first * 2, 2 * count + 2)], engines=[engine],
                                                    min_val=0, max_val=most, skip_runtime_bounds_check_because=RANGES)
    return [x & ((1 << 20) - 1) for x in v[0::2]], v[1::2]


def build_adjacency(nc, g, slabs):
    MOST = NWIN * NT
    with Scope(nc) as s:
        mkey = s.sb("mkey", [EP, WGRP], F32)
        skey = s.sb("skey", [EP, WGRP], BF16)
        low = s.sb("low", [EP, 2 * P * WGRP], BF16)
        high = s.sb("high", [EP, WGRP, KEYW], BF16)
        iota_g = s.sb("iota_g", [P, P, WGRP], BF16)
        slab = [s.sb(f"slab{b}", [P, HI, SLAB], BF16) for b in range(2)]
        part = [s.ps(f"part{b}", [P, HI, W]) for b in range(2)]
        dve_step = s.sem("dve_step")
        keys_ready = s.sem("keys_ready")
        made = s.sem("made")
        used = s.sem("used")
        copied = s.sem("copied")
        stored = [s.sem(f"slab_stored{b}") for b in range(2)]
        block = s.block()

        @block.vector
        def _(dve):
            nc.vector.tensor_copy(iota_g[:, :, :], g["iota"][:, 0:P].unsqueeze(2).broadcast_to([P, P, WGRP])
                                  ).then_inc(dve_step, 1)
            dve.wait_ge(dve_step, 1)
            dve.sem_inc(made, WGRP)
            with dve.Fori(0, NWIN // WBATCH) as kb:
                before, offset = load_ranges(nc, g["win_table"], DVE, kb * WBATCH, WBATCH, MOST)
                for w in range(WBATCH):
                    with dve.Fori(before[w], before[w + 1]) as v:
                        t = nc.s_assert_within(v * WGRP - offset[w], 0, NT, skip_runtime_bounds_check_because=RANGES)
                        base = g["winbase"][0:EP, bass.ds(kb * WBATCH + w, 1)]
                        dve.wait_ge(made, v * WGRP + WGRP)
                        nc.vector.tensor_scalar(mkey[:, :], g["mkeys"][:, bass.ds(t, WGRP)], base, None, ALU.subtract)
                        nc.vector.tensor_scalar(skey[:, :], g["skeys"][:, bass.ds(t, WGRP)], base, None,
                                                ALU.subtract).then_inc(keys_ready, 1)
                        dve.wait_ge(keys_ready, v + 1)
                        dve.wait_ge(used, v * WGRP + 1)
                        lo = low[:, bass.ds((v & 1) * (P * WGRP), P * WGRP)].rearrange("p (a b) -> p a b", b=WGRP)
                        nc.vector.tensor_tensor(lo, iota_g[0:EP, :, :], skey[:, :].unsqueeze(1).broadcast_to([EP, P, WGRP]),
                                                ALU.is_equal)
                        for i in range(WGRP):
                            dve.wait_ge(used, v * WGRP + WGRP + i + 1)
                            nc.vector.tensor_scalar(high[:, i, :], g["iota"][0:EP, 0:KEYW], mkey[:, i:i + 1], None,
                                                    ALU.is_equal).then_inc(made, 1)

        @block.tensor
        def _(pe):
            pe.sem_inc(used, 2 * WGRP)
            pe.sem_inc(copied, 2)
            with pe.Fori(0, NWIN // WBATCH) as kb:
                before, _ = load_ranges(nc, g["win_table"], PE, kb * WBATCH, WBATCH, MOST)
                for w in range(WBATCH):
                    out = part[w % 2][:, :, :].rearrange("p a b -> p (a b)")
                    pe.wait_ge(copied, kb * WBATCH + w + 1)
                    nc.tensor.matmul(out, g["zerob"][0:EP, 0:P], g["zerob"][0:EP, 0:KEYW], start=True, stop=True)
                    with pe.Fori(before[w], before[w + 1]) as v:
                        for i in range(WGRP):
                            pe.wait_ge(made, v * WGRP + WGRP + i + 1)
                            nc.tensor.matmul(out, low[:, bass.DynSlice((v & 1) * (P * WGRP) + i, P, WGRP)], high[:, i, :],
                                             start=False, stop=True, skip_group_check=True).then_inc(used, 1)

        @block.scalar
        def _(act):
            with act.Fori(0, NSLAB // 2) as s2:
                for b in range(2):
                    act.wait_ge(stored[b], s2 * 16 + 1)
                    with act.Fori(0, SLAB_W // WBATCH) as k5:
                        kb = (s2 * 2 + b) * (SLAB_W // WBATCH) + k5
                        before, _ = load_ranges(nc, g["win_table"], ACTE, kb * WBATCH, WBATCH, MOST)
                        for w in range(WBATCH):
                            act.wait_ge(used, before[w + 1] * WGRP + 2 * WGRP)
                            nc.scalar.copy(slab[b][:, :, bass.ds((k5 * WBATCH + w) * W, W)],
                                           part[w % 2][:, :, :]).then_inc(copied, 1)

        @block.sync
        def _(sp):
            for b in range(2):
                sp.sem_inc(stored[b], 1)
            with sp.Fori(0, NSLAB // 2) as s2:
                for b in range(2):
                    n = s2 * 2 + b
                    sp.wait_ge(copied, n * SLAB_W + SLAB_W + 2)
                    sp.dma_start(slabs[bass.ds(n, 1), :, :].rearrange("a p c -> p (a c)"),
                                 slab[b][:, :, :].rearrange("p a b -> p (a b)")).then_inc(stored[b], 16)
            for b in range(2):
                sp.wait_ge(stored[b], 16 * (NSLAB // 2) + 1)


def sum_edge_attributes(nc, g, edge_attr_64):
    MOST = NB * NT
    HALF = HGRP // 2
    with Scope(nc) as s:
        attr = [s.sb(f"attr_half{b}", [EP, HALF, D + 1], F32) for b in range(2)]
        keys = s.sb("block_keys", [EP, HGRP], F32)
        hot = s.sb("block_hot", [EP, HGRP, P], F32)
        base = s.sb("block_base", [P, NB], F32)
        iota_f = s.sb("iota_f", [P, P], F32)
        total = [s.ps(f"block_total{b}", [P, D + 1]) for b in range(2)]
        dve_step = s.sem("dve_step")
        attr_in = [s.sem(f"attr_in{b}") for b in range(2)]
        keys_ready = s.sem("keys_ready")
        made = s.sem("made")
        used = s.sem("used")
        copied = s.sem("copied")
        block = s.block()
        rows = edge_attr_64.rearrange("(t e) f -> e t f", e=EP)
        BB = 2

        @block.sync
        def _(sp):
            sp.wait_ge(dve_step, 2)
            with sp.Fori(0, NB // BB) as i:
                before, offset = load_ranges(nc, g["blk_table"], SPE, i * BB, BB, MOST)
                for k in range(BB):
                    with sp.Fori(before[k], before[k + 1]) as v:
                        t = nc.s_assert_within(v * HGRP - offset[k], 0, NT - HGRP,
                                               skip_runtime_bounds_check_because=RANGES)
                        for b in range(2):
                            sp.wait_ge(used, v * HGRP + (b + 1) * HALF)
                            sp.dma_start(attr[b][:, :, 0:D], rows[:, bass.ds(t + b * HALF, HALF), :]
                                         ).then_inc(attr_in[b], 16)

        @block.vector
        def _(dve):
            step = Serial(dve, dve_step)
            for b in range(2):
                step(nc.vector.memset(attr[b][:, :, D:D + 1], 1.0))
            step(nc.vector.tensor_copy(iota_f[:, :], g["iota"][:, 0:P]))
            step(nc.vector.tensor_scalar(base[:, :], g["winbase"][:, 0:NB], P / 512.0, None, ALU.mult))
            dve.sem_inc(made, HGRP)
            with dve.Fori(0, NB // BB) as i:
                before, offset = load_ranges(nc, g["blk_table"], DVE, i * BB, BB, MOST)
                for k in range(BB):
                    with dve.Fori(before[k], before[k + 1]) as v:
                        t = nc.s_assert_within(v * HGRP - offset[k], 0, NT - HGRP,
                                               skip_runtime_bounds_check_because=RANGES)
                        dve.wait_ge(made, v * HGRP + HGRP)
                        nc.vector.tensor_scalar(keys[:, :], g["dkey"][:, bass.ds(t, HGRP)],
                                                base[0:EP, bass.ds(i * BB + k, 1)], None,
                                                ALU.subtract).then_inc(keys_ready, 1)
                        dve.wait_ge(keys_ready, v + 1)
                        for j in range(HGRP):
                            dve.wait_ge(used, v * HGRP + j + 1)
                            nc.vector.tensor_scalar(hot[:, j, :], iota_f[0:EP, :], keys[:, j:j + 1], None,
                                                    ALU.is_equal).then_inc(made, 1)

        @block.tensor
        def _(pe):
            pe.sem_inc(used, HGRP)
            pe.sem_inc(copied, 2)
            with pe.Fori(0, NB // BB) as i:
                before, _ = load_ranges(nc, g["blk_table"], PE, i * BB, BB, MOST)
                for k in range(BB):
                    pe.wait_ge(copied, i * BB + k + 1)
                    nc.tensor.matmul(total[k][:, :], g["zerob"][0:EP, 0:P], g["zerob"][0:EP, 0:D + 1], start=True,
                                     stop=True)
                    with pe.Fori(before[k], before[k + 1]) as v:
                        for j in range(HGRP):
                            if j % HALF == 0:
                                pe.wait_ge(attr_in[j // HALF], v * 16 + 16)
                            pe.wait_ge(made, v * HGRP + HGRP + j + 1)
                            nc.tensor.matmul(total[k][:, :], hot[:, j, :], attr[j // HALF][:, j % HALF, :], start=False,
                                             stop=True, skip_group_check=True).then_inc(used, 1)

        @block.scalar
        def _(act):
            with act.Fori(0, NB // BB) as i:
                before, _ = load_ranges(nc, g["blk_table"], ACTE, i * BB, BB, MOST)
                for k in range(BB):
                    act.wait_ge(used, before[k + 1] * HGRP + HGRP)
                    nc.scalar.copy(g["attr_sum"][:, bass.ds((i * BB + k) * (D + 1), D + 1)], total[k][:, :]
                                   ).then_inc(copied, 1)


def split_three(step, nc, out, rest, x):
    step(nc.vector.tensor_copy(out[:, :, 0:D], x))
    step(nc.vector.tensor_tensor(rest, x, out[:, :, 0:D], ALU.subtract))
    step(nc.vector.tensor_copy(out[:, :, D:2 * D], rest))
    step(nc.vector.tensor_tensor(rest, rest, out[:, :, D:2 * D], ALU.subtract))
    step(nc.vector.tensor_copy(out[:, :, 2 * D:3 * D], rest))


def sum_over_sources(nc, turn, slabs, parts, first_two, third):
    PH = 7
    PIECES = HI // PH
    with Scope(nc, turn) as s:
        piece = [s.sb(f"piece{k}", [P, PH, SLAB], BF16) for k in range(PIECES)]
        sum2 = [s.ps(f"sum2_{b}", [P, SLAB]) for b in range(2)]
        sum1 = [s.ps(f"sum1_{b}", [D, SLAB]) for b in range(2)]
        piece_in = [s.sem(f"piece_in{k}") for k in range(PIECES)]
        piece_used = s.sem("piece_used")
        copied2 = s.sem("copied2")
        copied1 = s.sem("copied1")
        block = s.block()

        @block.sync
        def _(sp):
            with sp.Fori(0, NSLAB) as n:
                for k in range(PIECES):
                    sp.wait_ge(piece_used, n * PIECES + k + 1)
                    sp.dma_start(piece[k][:, :, :].rearrange("p a b -> p (a b)"),
                                 slabs[bass.ds(n, 1), :, k * PH * SLAB:(k + 1) * PH * SLAB]
                                 .rearrange("a p c -> p (a c)")).then_inc(piece_in[k], 16)

        @block.tensor
        def _(pe):
            pe.sem_inc(piece_used, PIECES)
            pe.sem_inc(copied2, 2)
            pe.sem_inc(copied1, 2)
            with pe.Fori(0, NSLAB // 2) as i:
                for b in range(2):
                    pe.wait_ge(copied2, i * 2 + b + 1)
                    pe.wait_ge(copied1, i * 2 + b + 1)
                    for k in range(PIECES):
                        pe.wait_ge(piece_in[k], (i * 2 + b) * 16 + 16)
                        for j in range(PH):
                            hb = k * PH + j
                            ends = {"start": hb == 0, "stop": hb == HI - 1}
                            nc.tensor.matmul(sum2[b][:, :], parts[:, hb, 0:2 * D], piece[k][:, j, :], **ends)
                            last = nc.tensor.matmul(sum1[b][:, :], parts[:, hb, 2 * D:3 * D], piece[k][:, j, :], **ends)
                        last.then_inc(piece_used, 1)

        @block.scalar
        def _(act):
            with act.Fori(0, NSLAB // 2) as i:
                for b in range(2):
                    act.wait_ge(piece_used, (i * 2 + b + 2) * PIECES)
                    nc.scalar.copy(first_two[:, bass.ds((i * 2 + b) * SLAB, SLAB)], sum2[b][:, :]).then_inc(copied2, 1)

        @block.vector
        def _(dve):
            with dve.Fori(0, NSLAB // 2) as i:
                for b in range(2):
                    dve.wait_ge(piece_used, (i * 2 + b + 2) * PIECES)
                    nc.vector.tensor_copy(third[:, bass.ds((i * 2 + b) * SLAB, SLAB)], sum1[b][:, :]
                                          ).then_inc(copied1, 1)


def wide(x, width=D):
    return x.unsqueeze(2).broadcast_to([P, x.shape[1], width])


def layer_norm_relu(step, nc, act_sqrt, g, out, tmp, col):
    x = g["x"][:, :, :]
    mean, var = col[:, 0, :], col[:, 1, :]
    step(nc.vector.tensor_reduce(mean, x, AX_X, ALU.add))
    step(nc.vector.tensor_scalar(mean, mean, 1.0 / D, None, ALU.mult))
    step(nc.vector.tensor_tensor(out[:, :, :], x, wide(mean), ALU.subtract))
    step(nc.vector.tensor_tensor(tmp[:, :, :], out[:, :, :], out[:, :, :], ALU.mult))
    step(nc.vector.tensor_reduce(var, tmp[:, :, :], AX_X, ALU.add))
    step(nc.vector.tensor_scalar(var, var, 1.0 / D, 1e-5, ALU.mult, ALU.add))
    act_sqrt()
    step(nc.vector.reciprocal(var, var))
    step(nc.vector.scalar_tensor_tensor(out[:, :, :], out[:, :, :], 0.0, wide(var), ALU.max, ALU.mult))


def edge_statistics_layer(nc, g, scanned, carries, x_in, u, w1, b1, w2, b2):
    NF = 3 * DA
    with Scope(nc) as s:
        ends = s.sb("ends", [P, HI, 2 * DA], F32)
        carry_in = s.sb("run_carry", [P, HI, 2 * DA], F32)
        feats = s.sb("feats", [P, HI, NF], F32)
        feats_t = s.sb("feats_t", [NF, HI * P], F32)
        hidden = s.sb("hidden", [HID, HI * P], F32)
        off = s.sb("off", [P, HI], F32)
        inv = s.sb("inv", [P, HI], F32)
        w1_sb = s.sb("w1_sb", [NF, HID], F32)
        w2_sb = s.sb("w2_sb", [HID, D], F32)
        w1_u = s.sb("w1_u", [HID, 1], F32)
        u_col = s.sb("u_col", [HID, 1], F32)
        bias = s.sb("bias", [HID, 1], F32)
        b2_row = s.sb("b2_row", [P, D], F32)
        turned = [s.ps(f"feats_turned{b}", [NF, 4, P]) for b in range(2)]
        ps_hidden = [s.ps(f"ps_hidden{b}", [HID, 512]) for b in range(2)]
        ps_out = [s.ps(f"ps_out{b}", [P, 8, D]) for b in range(2)]
        loaded = s.sem("loaded")
        gathered = s.sem("gathered")
        dve_step = s.sem("dve_step")
        bias_ready = s.sem("bias_ready")
        feats_ready = s.sem("feats_ready")
        turned_ready = s.sem("turned_ready")
        turned_copied = s.sem("turned_copied")
        hidden_ready = s.sem("hidden_ready")
        hidden_copied = s.sem("hidden_copied")
        out_ready = s.sem("out_ready")
        added = s.sem("added")
        block = s.block()
        CH = -(-HI // 4)
        OC = -(-HI // 8)
        x, full = g["x"], (N // P) * P

        @block.sync
        def _(sp):
            sp.dma_start(w1_sb[:, :], w1[0:NF, :]).then_inc(loaded, 16)
            sp.dma_start(w1_u[:, :], w1[NF:NF + 1, :].rearrange("a h -> h a")).then_inc(loaded, 16)
            sp.dma_start(u_col[:, :], u[0:1, 0:1].broadcast_to([HID, 1])).then_inc(loaded, 16)
            sp.dma_start(bias[:, :], b1.unsqueeze(1)).then_inc(loaded, 16)
            sp.dma_start(w2_sb[:, :], w2).then_inc(loaded, 16)
            sp.dma_start(b2_row[:, :], b2.unsqueeze(0).broadcast_to([P, D])).then_inc(loaded, 16)
            sp.wait_ge(dve_step, 1)
            sp.dma_start(x[:, 0:N // P, :], x_in[0:full, :].rearrange("(b p) f -> p b f", p=P)).then_inc(loaded, 16)
            sp.dma_start(x[0:N - full, N // P, :], x_in[full:N, :]).then_inc(loaded, 16)

        @block.gpsimd
        def _(pool):
            gather_runs(nc, pool, g, scanned, carries, ends, carry_in, gathered)

        @block.vector
        def _(dve):
            step = Serial(dve, dve_step)
            step(nc.vector.memset(x[:, N // P, :], 0.0))
            step(nc.vector.tensor_scalar(off[:, :], g["spans"][:, :], -1.0, HUGE, ALU.add, ALU.mult))
            step(nc.vector.tensor_scalar(inv[:, :], g["out_deg"][:, 0:HI], 1.0, None, ALU.max))
            step(nc.vector.reciprocal(inv[:, :], inv[:, :]))
            dve.wait_ge(loaded, 8 * 16)
            nc.vector.scalar_tensor_tensor(bias[:, :], w1_u[:, :], u_col[:, 0:1], bias[:, :], ALU.mult,
                                           ALU.add).then_inc(bias_ready, 1)
            step(nc.vector.tensor_tensor(x[:, :, :], x[:, :, :], b2_row[:, :].unsqueeze(1).broadcast_to([P, HI, D]),
                                         ALU.add))
            dve.wait_ge(gathered, 16 * 2 * HI)
            total, most, mean = (feats[:, :, c * DA:(c + 1) * DA] for c in range(3))
            step(nc.vector.tensor_tensor(carry_in[:, :, :], carry_in[:, :, :], wide(g["spans"][:, :]), ALU.mult))
            step(nc.vector.tensor_tensor(total, ends[:, :, DA:], carry_in[:, :, DA:], ALU.add))
            step(nc.vector.tensor_tensor(total, total, wide(g["has_out"][:, :], DA), ALU.mult))
            step(nc.vector.tensor_tensor(mean, total, wide(inv[:, :], DA), ALU.mult))
            step(nc.vector.tensor_tensor(most, carry_in[:, :, 0:DA], wide(off[:, :], DA), ALU.add))
            step(nc.vector.tensor_tensor(most, most, ends[:, :, 0:DA], ALU.max))
            nc.vector.tensor_tensor(most, most, wide(g["has_out"][:, :], DA), ALU.mult).then_inc(feats_ready, 1)
            for c in range(OC):
                n = min(8, HI - 8 * c)
                dve.wait_ge(out_ready, c + 1)
                nc.vector.tensor_tensor(x[:, 8 * c:8 * c + n, :], x[:, 8 * c:8 * c + n, :], ps_out[c % 2][:, 0:n, :],
                                        ALU.add).then_inc(added, 1)

        @block.scalar
        def _(act):
            act.wait_ge(bias_ready, 1)
            for c in range(CH):
                n = min(4, HI - 4 * c)
                act.wait_ge(turned_ready, c + 1)
                nc.scalar.copy(feats_t[:, c * 512:c * 512 + n * P].rearrange("p (a b) -> p a b", b=P),
                               turned[c % 2][:, 0:n, :]).then_inc(turned_copied, 1)
                act.wait_ge(hidden_ready, c + 1)
                nc.scalar.activation(hidden[:, c * 512:c * 512 + n * P], ps_hidden[c % 2][:, 0:n * P], ACT.Relu,
                                     bias=bias[:, 0:1]).then_inc(hidden_copied, 1)

        @block.tensor
        def _(pe):
            pe.wait_ge(feats_ready, 1)
            for c in range(CH):
                n = min(4, HI - 4 * c)
                if c >= 2:
                    pe.wait_ge(turned_copied, c - 1)
                for a in range(n):
                    last = nc.tensor.transpose(turned[c % 2][:, a, :], feats[:, 4 * c + a, :], g["ident"][:, :])
                last.then_inc(turned_ready, 1)
                pe.wait_ge(turned_copied, c + 1)
                if c >= 2:
                    pe.wait_ge(hidden_copied, c - 1)
                nc.tensor.matmul(ps_hidden[c % 2][:, 0:n * P], w1_sb[:, :], feats_t[:, c * 512:c * 512 + n * P],
                                 start=True, stop=True).then_inc(hidden_ready, 1)
            for c in range(OC):
                n = min(8, HI - 8 * c)
                pe.wait_ge(hidden_copied, min(CH, 2 * c + 2))
                if c >= 2:
                    pe.wait_ge(added, c - 1)
                for a in range(n):
                    b = 8 * c + a
                    last = nc.tensor.matmul(ps_out[c % 2][:, a, :], hidden[:, b * P:(b + 1) * P], w2_sb[:, :],
                                            start=True, stop=True)
                last.then_inc(out_ready, 1)


def kept(nc, ctx, g):
    for name, shape, dt in (
        ("ident", [P, P], F32), ("identb", [P, P], BF16), ("below", [P, P], F32), ("belowb", [P, P], BF16),
        ("ones", [P, P], F32), ("zerob", [P, 512], BF16), ("iota", [P, 512], FP16), ("rowid", [P, 1], F32),
        ("rowid_i", [P, 1], I32), ("winbase", [P, NWIN], F32), ("mkeys", [EP, TPAD], F32), ("skeys", [EP, TPAD], F32), ("dkey", [EP, NT], F32),
        ("span", [P, 2, TB], F32), ("out_deg", [P, NB], F32), ("start", [P, NB], F32),
        ("same_src", [EP, NT], F32), ("dst_sorted", [EP, NT], I32), ("w_sorted", [EP, NT], F32),
        ("end_i", [P, HI], I32), ("end_part_i", [P, HI], I32), ("has_out", [P, HI], F32), ("spans", [P, HI], F32),
        ("x", [P, HI, D], F32), ("win_table", [1, 2 * NWIN + 2], I32), ("blk_table", [1, 2 * NB + 2], I32),
        ("attr_sum", [P, NB * (D + 1)], F32), ("keep_run", [D, EP], F32),
    ):
        g[name] = ctx.enter_context(nc.sbuf_tensor(name, shape, dt))


def kept_to_rank(nc, ctx, g):
    for name, shape, dt in (("sdw", [EP, NT, 3], F32), ("lo", [EP, NT + RG], FP16), ("hi", [EP, NT + RG], FP16),
                            ("iota_rg", [P, P, RG], FP16)):
        g[name] = ctx.enter_context(nc.sbuf_tensor(name, shape, dt))


def normalise(nc, g, turn, h, parts=None, by_degree=None):
    with Scope(nc, turn) as s:
        tmp = s.sb("norm_tmp", [P, HI, D], F32)
        scaled = s.sb("norm_scaled", [P, HI, D], F32)
        col = s.sb("norm_col", [P, 2, HI], F32)
        deg = s.sb("norm_deg", [P, 2, HI], F32)
        dve_step = s.sem("dve_step")
        var_ready = s.sem("var_ready")
        root_ready = s.sem("root_ready")
        block = s.block()

        @block.vector
        def _(dve):
            step = Serial(dve, dve_step)

            def roots():
                dve.sem_inc(var_ready, 1)
                dve.wait_ge(root_ready, 1)

            if by_degree:
                rs, factor = by_degree
                counts = g["attr_sum"][:, D:HI * (D + 1):D + 1]
                step(nc.vector.tensor_scalar(deg[:, 0, :], g["out_deg"][:, 0:HI], 1.0, None, ALU.add))
                step(nc.vector.tensor_scalar(deg[:, 1, :], counts, 1.0, None, ALU.add))
            layer_norm_relu(step, nc, roots, g, h, tmp, col)
            if by_degree:
                step(nc.vector.reciprocal(rs[:, :], rs[:, :]))
                step(nc.vector.tensor_tensor(factor[:, :], factor[:, :], deg[:, 1, :], ALU.mult))
                step(nc.vector.reciprocal(factor[:, :], factor[:, :]))
                step(nc.vector.tensor_tensor(scaled[:, :, :], h[:, :, :], wide(rs[:, :]), ALU.mult))
                split_three(step, nc, parts, tmp[:, :, :], scaled[:, :, :])
            elif parts is not None:
                split_three(step, nc, parts, tmp[:, :, :], h[:, :, :])

        @block.scalar
        def _(act):
            act.wait_ge(var_ready, 1)
            if by_degree:
                rs, factor = by_degree
                nc.scalar.activation(rs[:, :], deg[:, 0, :], ACT.Sqrt)
                nc.scalar.activation(factor[:, :], deg[:, 1, :], ACT.Sqrt)
            nc.scalar.activation(col[:, 1, :], col[:, 1, :], ACT.Sqrt).then_inc(root_ready, 1)


def convolution_layer(nc, g, slabs, w, b):
    CH = -(-HI // 4)
    with Scope(nc) as keep:
        h = keep.sb("conv_h", [P, HI, D], F32)
        parts = keep.sb("conv_parts", [P, HI, 3 * D], BF16)
        rs = keep.sb("conv_rs", [P, HI], F32)
        factor = keep.sb("conv_factor", [P, HI], F32)
        normalise(nc, g, "_conv", h, parts, (rs, factor))
        first_two = keep.sb("conv_first_two", [P, NPAD], F32)
        third = keep.sb("conv_third", [D, NPAD], F32)
        sum_over_sources(nc, "_conv", slabs, parts, first_two, third)
        with Scope(nc) as s:
            w_ab = s.sb("w_ab", [D, 2 * D], F32)
            w_b2 = s.sb("w_b2", [P, D], F32)
            b_row = s.sb("conv_b_row", [P, D], F32)
            ht = s.sb("conv_ht", [D, 2, 512], F32)
            mix = s.sb("conv_mix", [P, 4, D], F32)
            turned = [s.ps(f"conv_turned{k}", [D, 512]) for k in range(2)]
            own = [s.ps(f"conv_own{k}", [P, 4, 2 * D]) for k in range(2)]
            summed = [s.ps(f"conv_summed{k}", [P, 4, D]) for k in range(2)]
            loaded = s.sem("loaded")
            turned_ready = s.sem("turned_ready")
            turned_copied = s.sem("turned_copied")
            ready = s.sem("products_ready")
            added = s.sem("added")
            dve_step = s.sem("dve_step")
            block = s.block()
            x = g["x"]

            @block.sync
            def _(sp):
                sp.dma_start(w_ab[:, 0:D], w[0:D, :]).then_inc(loaded, 16)
                sp.dma_start(w_ab[:, D:2 * D], w[D:2 * D, :]).then_inc(loaded, 16)
                sp.dma_start(w_b2[0:D, :], w[D:2 * D, :]).then_inc(loaded, 16)
                sp.dma_start(w_b2[D:2 * D, :], w[D:2 * D, :]).then_inc(loaded, 16)
                sp.dma_start(b_row[:, :], b.unsqueeze(0).broadcast_to([P, D])).then_inc(loaded, 16)

            @block.tensor
            def _(pe):
                def turn(c):
                    if c >= 2:
                        pe.wait_ge(turned_copied, c - 1)
                    for a in range(min(4, HI - 4 * c)):
                        last = nc.tensor.transpose(turned[c % 2][:, a * P:(a + 1) * P], h[:, 4 * c + a, :],
                                                   g["ident"][:, :])
                    last.then_inc(turned_ready, 1)

                turn(0)
                pe.wait_ge(loaded, 5 * 16)
                for c in range(CH):
                    if c + 1 < CH:
                        turn(c + 1)
                    pe.wait_ge(turned_copied, c + 1)
                    if c >= 2:
                        pe.wait_ge(added, c - 1)
                    for a in range(min(4, HI - 4 * c)):
                        nodes = slice((4 * c + a) * P, (4 * c + a + 1) * P)
                        nc.tensor.matmul(own[c % 2][:, a, :], ht[:, c % 2, a * P:(a + 1) * P], w_ab[:, :],
                                         start=True, stop=True)
                        nc.tensor.matmul(summed[c % 2][:, a, :], first_two[:, nodes], w_b2[:, :], start=True,
                                         stop=False)
                        last = nc.tensor.matmul(summed[c % 2][:, a, :], third[:, nodes], w_b2[0:D, :],
                                                start=False, stop=True)
                    last.then_inc(ready, 1)

            @block.scalar
            def _(act):
                for c in range(CH):
                    n = min(4, HI - 4 * c) * P
                    act.wait_ge(turned_ready, c + 1)
                    if c >= 2:
                        act.wait_ge(ready, c - 1)
                    nc.scalar.copy(ht[:, c % 2, 0:n], turned[c % 2][:, 0:n]).then_inc(turned_copied, 1)

            @block.vector
            def _(dve):
                step = Serial(dve, dve_step)
                dve.wait_ge(loaded, 5 * 16)
                step(nc.vector.tensor_tensor(x[:, :, :], x[:, :, :], b_row[:, :].unsqueeze(1).broadcast_to([P, HI, D]),
                                             ALU.add))
                for c in range(CH):
                    n = min(4, HI - 4 * c)
                    blocks = slice(4 * c, 4 * c + n)
                    m = mix[:, 0:n, :]
                    dve.wait_ge(ready, c + 1)
                    step(nc.vector.tensor_tensor(m, own[c % 2][:, 0:n, D:2 * D], wide(rs[:, blocks]), ALU.mult))
                    step(nc.vector.tensor_tensor(m, m, summed[c % 2][:, 0:n, :], ALU.add))
                    step(nc.vector.tensor_tensor(m, m, wide(factor[:, blocks]), ALU.mult))
                    nc.vector.tensor_tensor(m, m, own[c % 2][:, 0:n, 0:D], ALU.add).then_inc(added, 1)
                    dve.wait_ge(added, c + 1)
                    step(nc.vector.tensor_tensor(x[:, blocks, :], x[:, blocks, :], m, ALU.add))


def scan_messages(nc, g, table, scanned, carries):
    J = 50
    STEPS = NT // J
    with Scope(nc) as s:
        index = [s.sb(f"gather_index{b}", [EP, J], I32) for b in range(2)]
        got = [s.sb(f"gathered_rows{b}", [EP, J, D], F32) for b in range(2)]
        out = [s.sb(f"message_sums{b}", [EP, J, D], F32) for b in range(2)]
        carry = s.sb("sum_carry", [EP, D], F32)
        state = s.sb("sum_state", [D, EP], F32)
        turned_carry = s.sb("sum_turned_carry", [D, EP], F32)
        carry_in = s.sb("sum_carry_in", [EP, D], F32)
        ps_carry = s.ps("ps_sum_carry", [D, EP])
        ps_in = s.ps("ps_sum_in", [EP, D])
        index_ready = s.sem("index_ready")
        gathered = [s.sem(f"gathered{b}") for b in range(2)]
        index_used = s.sem("index_used")
        weighted = s.sem("weighted")
        scans_done = s.sem("scans_done")
        carry_ready = s.sem("carry_ready")
        sums_out = [s.sem(f"sums_out{b}") for b in range(2)]
        pool_turns = s.sem("pool_turns")
        dve_step = s.sem("dve_step")
        pe_done = s.sem("pe_done")
        carried = s.sem("carried")
        block = s.block()
        dst_v = scanned[:, :].rearrange("(p j) c -> p (j c)", p=EP)

        @block.gpsimd
        def _(pool):
            pool.sem_inc(scans_done, 2)
            pool.sem_inc(index_used, 2)
            with pool.Fori(0, STEPS // 2) as i:
                for b in range(2):
                    pool.wait_ge(index_ready, 2 * i + b + 1)
                    pool.wait_ge(scans_done, 2 * i + b + 1)
                    pool.sem_inc(pool_turns, 1)
                    for j in range(J):
                        pool.indirect_dma_start(got[b][:, j, :], None, table[:, :],
                                                bass.IndirectOffsetOnAxis(ap=index[b][:, j:j + 1], axis=0)
                                                ).then_inc(gathered[b], 16)

        @block.scalar
        def _(act):
            with act.Fori(0, STEPS // 2) as i:
                for b in range(2):
                    act.wait_ge(index_used, 2 * i + b + 1)
                    nc.scalar.copy(index[b][:, :], g["dst_sorted"][:, bass.ds((2 * i + b) * J, J)]
                                   ).then_inc(index_ready, 1)

        @block.vector
        def _(dve):
            nc.vector.memset(carry[:, :], 0.0).then_inc(carry_ready, 1)
            with dve.Fori(0, STEPS // 2) as i:
                for b in range(2):
                    n = 2 * i + b
                    dve.wait_ge(gathered[b], 16 * J * (i + 1))
                    dve.sem_inc(index_used, 1)
                    w = g["w_sorted"][:, bass.ds(n * J, J)]
                    nc.vector.tensor_tensor(got[b][:, :, :], got[b][:, :, :], w.unsqueeze(2).broadcast_to([EP, J, D]),
                                            ALU.mult).then_inc(weighted, 1)
                    dve.wait_ge(weighted, n + 1)
                    dve.wait_ge(carry_ready, n + 1)
                    dve.wait_ge(sums_out[b], 32 * i + 1)
                    for f in range(D):
                        last = nc.vector.tensor_tensor_scan(out[b][:, :, f], g["same_src"][:, bass.ds(n * J, J)],
                                                            got[b][:, :, f], carry[:, f:f + 1], ALU.mult, ALU.add)
                    last.then_inc(scans_done, 1)
                    dve.wait_ge(scans_done, n + 3)
                    nc.vector.tensor_copy(carry[:, :], out[b][:, J - 1, :]).then_inc(carry_ready, 1)
            step = Serial(dve, dve_step)
            dve.wait_ge(pe_done, 1)
            step(nc.vector.tensor_copy(turned_carry[:, :], ps_carry[:, :]))
            step(nc.vector.memset(state[:, 0:1], 0.0))
            step(nc.vector.tensor_tensor_scan(state[:, 1:EP], g["keep_run"][:, 0:EP - 1], turned_carry[:, 0:EP - 1],
                                              0.0, ALU.mult, ALU.add))
            dve.wait_ge(pe_done, 2)
            nc.vector.tensor_copy(carry_in[:, :], ps_in[:, :]).then_inc(carried, 1)

        @block.tensor
        def _(pe):
            pe.wait_ge(carry_ready, STEPS + 1)
            nc.tensor.transpose(ps_carry[:, :], carry[:, :], g["ident"][0:EP, 0:EP]).then_inc(pe_done, 1)
            pe.wait_ge(dve_step, 3)
            nc.tensor.transpose(ps_in[:, :], state[:, :], g["ident"][0:D, 0:D]).then_inc(pe_done, 1)

        @block.sync
        def _(sp):
            for b in range(2):
                sp.sem_inc(sums_out[b], 1)
            with sp.Fori(0, STEPS // 2) as i:
                for b in range(2):
                    n = 2 * i + b
                    sp.wait_ge(scans_done, n + 3)
                    two_parts(sp, dst_v[:, bass.ds(n * J * D, J * D)], out[b][:, :, :].rearrange("p j f -> p (j f)"),
                              sums_out[b])
            for b in range(2):
                sp.wait_ge(sums_out[b], 16 * STEPS + 1)
            sp.wait_ge(carried, 1)
            sp.dma_start(carries[:, :], carry_in[:, :]).then_inc(sums_out[0], 16)
            sp.wait_ge(sums_out[0], 16 * STEPS + 17)


def weighted_layer(nc, g, table, scanned, carries, eps):
    with Scope(nc) as keep:
        h = keep.sb("weighted_h", [P, HI, D], F32)
        normalise(nc, g, "_weighted", h)
        with Scope(nc) as s:
            stored = s.sem("table_stored")
            block = s.block()

            @block.sync
            def _(sp):
                sp.dma_start(table[:, :].rearrange("(b p) f -> p b f", p=P), h[:, :, :]).then_inc(stored, 16)
                sp.wait_ge(stored, 16)

        scan_messages(nc, g, table, scanned, carries)
        with Scope(nc) as s:
            ends = s.sb("message_ends", [P, HI, D], F32)
            carry_in = s.sb("message_carry", [P, HI, D], F32)
            factor = s.sb("one_eps", [P, 1], F32)
            loaded = s.sem("loaded")
            gathered = s.sem("gathered")
            dve_step = s.sem("dve_step")
            block = s.block()
            x = g["x"]

            @block.sync
            def _(sp):
                sp.dma_start(factor[:, :], eps.unsqueeze(0).broadcast_to([P, 1])).then_inc(loaded, 16)

            @block.gpsimd
            def _(pool):
                gather_runs(nc, pool, g, scanned, carries, ends, carry_in, gathered)

            @block.vector
            def _(dve):
                step = Serial(dve, dve_step)
                dve.wait_ge(loaded, 16)
                step(nc.vector.tensor_scalar(factor[:, :], factor[:, :], 1.0, None, ALU.add))
                step(nc.vector.scalar_tensor_tensor(x[:, :, :], h[:, :, :], factor[:, 0:1], x[:, :, :], ALU.mult,
                                                    ALU.add))
                dve.wait_ge(gathered, 16 * 2 * HI)
                step(nc.vector.tensor_tensor(carry_in[:, :, :], carry_in[:, :, :], wide(g["spans"][:, :]), ALU.mult))
                step(nc.vector.tensor_tensor(ends[:, :, :], ends[:, :, :], carry_in[:, :, :], ALU.add))
                step(nc.vector.tensor_tensor(ends[:, :, :], ends[:, :, :], wide(g["has_out"][:, :]), ALU.mult))
                step(nc.vector.tensor_tensor(x[:, :, :], x[:, :, :], ends[:, :, :], ALU.add))


def split_features(nc, parts, h):
    with Scope(nc) as s:
        rest = s.sb("split_rest", [P, HI, D], F32)
        dve_step = s.sem("dve_step")
        block = s.block()

        @block.vector
        def _(dve):
            split_three(Serial(dve, dve_step), nc, parts, rest[:, :, :], h[:, :, :])


def turn_weights(nc, g, t, w_msg, b_msg, w_ih, w_hh, b_ih, b_hh, wd, ws2, we, w_in, w_hid):
    with Scope(nc, f"_round{t}") as s:
        msg = s.sb("msg_nat", [P, 4 * D + 1], F32)
        inp = s.sb("in_nat", [P, 2, P], F32)
        hid = s.sb("hid_nat", [P, 3, D + 1], F32)
        bias = s.sb("hid_bias", [P, 1], F32)
        turned = [s.ps(f"weights_turned{k}", [P, 2, P]) for k in range(4)]
        cleared = s.sem("cleared")
        loaded = s.sem("loaded")
        nat_ready = s.sem("nat_ready")
        turned_ready = s.sem("turned_ready")
        copied = s.sem("copied")
        block = s.block()
        G = 2 * D

        @block.sync
        def _(sp):
            sp.dma_start(msg[:, 0:2 * D], w_msg[t, :, 0:2 * D]).then_inc(loaded, 16)
            sp.dma_start(msg[:, 2 * D:4 * D], w_msg[t, :, D:3 * D]).then_inc(loaded, 16)
            sp.dma_start(msg[:, 4 * D:4 * D + 1], b_msg[t, :].unsqueeze(1)).then_inc(loaded, 16)
            sp.dma_start(inp[:, 0, :], w_ih[t, 0:G, :]).then_inc(loaded, 16)
            sp.dma_start(inp[0:D, 1, :], w_ih[t, G:3 * D, :]).then_inc(loaded, 16)
            sp.dma_start(hid[:, 0, 0:D], w_hh[t, 0:G, :]).then_inc(loaded, 16)
            sp.dma_start(hid[:, 0, D:D + 1], b_hh[t, 0:G].unsqueeze(1)).then_inc(loaded, 16)
            sp.dma_start(bias[:, :], b_ih[t, 0:G].unsqueeze(1)).then_inc(loaded, 16)
            sp.dma_start(hid[0:D, 2, 0:D], w_hh[t, G:3 * D, :]).then_inc(loaded, 16)
            sp.dma_start(hid[0:D, 2, D:D + 1], b_hh[t, G:3 * D].unsqueeze(1)).then_inc(loaded, 16)
            sp.wait_ge(cleared, 1)
            sp.dma_start(hid[0:D, 1, D:D + 1], b_ih[t, G:3 * D].unsqueeze(1)).then_inc(loaded, 16)

        @block.vector
        def _(dve):
            nc.vector.memset(hid[:, 1, :], 0.0).then_inc(cleared, 1)
            dve.wait_ge(loaded, 11 * 16)
            nc.vector.tensor_tensor(hid[:, 0, D:D + 1], hid[:, 0, D:D + 1], bias[:, :], ALU.add).then_inc(nat_ready, 1)
            dve.wait_ge(turned_ready, 1)
            nc.vector.tensor_copy(wd[:, :], turned[0][0:D, 0, :])
            nc.vector.tensor_copy(ws2[:, :], turned[0][:, 1, :])
            nc.vector.tensor_copy(we[:, :], turned[1][0:D + 1, 0, :])
            nc.vector.tensor_copy(w_in[:, 0:G], turned[1][:, 1, :])
            nc.vector.tensor_copy(w_in[:, G:3 * D], turned[2][:, 0, 0:D])
            nc.vector.tensor_copy(w_hid[:, 0:G], turned[2][0:D + 1, 1, :])
            nc.vector.tensor_copy(w_hid[:, G:3 * D], turned[3][0:D + 1, 0, 0:D])
            nc.vector.tensor_copy(w_hid[:, 3 * D:4 * D], turned[3][0:D + 1, 1, 0:D]).then_inc(copied, 1)

        @block.tensor
        def _(pe):
            pe.wait_ge(nat_ready, 1)
            ident, half = g["ident"][:, :], g["ident"][0:D, 0:D]
            nc.tensor.transpose(turned[0][0:D, 0, :], msg[:, 0:D], ident)
            nc.tensor.transpose(turned[0][:, 1, :], msg[:, D:3 * D], ident)
            nc.tensor.transpose(turned[1][0:D + 1, 0, :], msg[:, 3 * D:4 * D + 1], ident)
            nc.tensor.transpose(turned[1][:, 1, :], inp[:, 0, :], ident)
            nc.tensor.transpose(turned[2][:, 0, 0:D], inp[0:D, 1, :], half)
            nc.tensor.transpose(turned[2][0:D + 1, 1, :], hid[:, 0, :], ident)
            nc.tensor.transpose(turned[3][0:D + 1, 0, 0:D], hid[0:D, 1, :], half)
            nc.tensor.transpose(turned[3][0:D + 1, 1, 0:D], hid[0:D, 2, :], half).then_inc(turned_ready, 1)


def gated_update(nc, g, t, h, first_two, third, wd, ws2, we, w_in, w_hid):
    CH = -(-HI // 4)
    PAIRS = -(-HI // 2)
    with Scope(nc, f"_round{t}") as s:
        scaled = s.sb("scaled_h", [P, 2, 4, D], F32)
        ht = s.sb("gru_ht", [D + 1, 2, 512], F32)
        ct = s.sb("gru_ct", [D, 2, 512], F32)
        et = s.sb("gru_et", [D + 1, 2, 512], F32)
        at = s.sb("gru_at", [P, 2, 512], F32)
        rz = s.sb("gru_rz", [P, 2, 2, 2 * D], F32)
        new = s.sb("gru_new", [P, 2, 2, D], F32)
        diff = s.sb("gru_diff", [P, 2, D], F32)
        ps_h = s.ps("ps_ht", [D, 4, P])
        ps_c = s.ps("ps_ct", [D, 4, P])
        ps_e = s.ps("ps_et", [D + 1, 4, P])
        ps_a = s.ps("ps_at", [P, 512])
        gates = [s.ps(f"ps_gates{k}", [P, 2, 4 * D]) for k in range(4)]
        scaled_ready = s.sem("scaled_ready")
        turned_ready = s.sem("turned_ready")
        copied_act = s.sem("copied_act")
        copied_dve = s.sem("copied_dve")
        sum_ready = s.sem("sum_ready")
        sum_copied = s.sem("sum_copied")
        gates_ready = s.sem("gates_ready")
        rz_ready = s.sem("rz_ready")
        pre_ready = s.sem("pre_ready")
        new_ready = s.sem("new_ready")
        updated = s.sem("updated")
        dve_step = s.sem("dve_step")
        ones_ready = s.sem("ones_ready")
        block = s.block()

        def blocks(c):
            return min(4, HI - 4 * c)

        def pairs(c):
            return range(2 * c, min(2 * c + 2, PAIRS))

        def paired(p):
            return min(2, HI - 2 * p)

        @block.tensor
        def _(pe):
            def turn(c):
                pe.wait_ge(scaled_ready, c + 1)
                if c:
                    pe.wait_ge(copied_act, c)
                    pe.wait_ge(copied_dve, c)
                for a in range(blocks(c)):
                    b = 4 * c + a
                    nc.tensor.transpose(ps_h[:, a, :], h[:, b, :], g["ident"][:, :])
                    nc.tensor.transpose(ps_e[:, a, :], g["attr_sum"][:, b * (D + 1):(b + 1) * (D + 1)],
                                        g["ident"][:, :])
                    last = nc.tensor.transpose(ps_c[:, a, :], scaled[:, c % 2, a, :], g["ident"][:, :])
                last.then_inc(turned_ready, 1)

            turn(0)
            pe.wait_ge(ones_ready, 1)
            for c in range(CH):
                if c + 1 < CH:
                    turn(c + 1)
                n = blocks(c) * P
                nodes = slice(c * 512, c * 512 + n)
                pe.wait_ge(copied_act, c + 1)
                pe.wait_ge(copied_dve, c + 1)
                if c:
                    pe.wait_ge(sum_copied, c)
                nc.tensor.matmul(ps_a[:, 0:n], wd[:, :], ct[:, c % 2, 0:n], start=True, stop=False)
                nc.tensor.matmul(ps_a[:, 0:n], ws2[:, :], first_two[:, nodes], start=False, stop=False)
                nc.tensor.matmul(ps_a[:, 0:n], ws2[0:D, :], third[:, nodes], start=False, stop=False)
                nc.tensor.matmul(ps_a[:, 0:n], we[:, :], et[:, c % 2, 0:n], start=False, stop=True
                                 ).then_inc(sum_ready, 1)
                pe.wait_ge(sum_copied, c + 1)
                for p in pairs(c):
                    if p >= 4:
                        pe.wait_ge(pre_ready, p - 3)
                    for k in range(paired(p)):
                        col = (2 * (p % 2) + k) * P
                        nc.tensor.matmul(gates[p % 4][:, k, :], ht[:, c % 2, col:col + P], w_hid[:, :], start=True,
                                         stop=True)
                        last = nc.tensor.matmul(gates[p % 4][:, k, 0:3 * D], at[:, c % 2, col:col + P], w_in[:, :],
                                                start=False, stop=True, skip_group_check=True)
                    last.then_inc(gates_ready, 1)

        @block.scalar
        def _(act):
            def copy(c):
                n = blocks(c)
                act.wait_ge(turned_ready, c + 1)
                if c >= 2:
                    act.wait_ge(gates_ready, 2 * c - 2)
                for out, bank, rows in ((ht, ps_h, D), (et, ps_e, D + 1)):
                    last = nc.scalar.copy(out[0:rows, c % 2, 0:n * P].rearrange("p (a b) -> p a b", b=P), bank[:, 0:n, :])
                last.then_inc(copied_act, 1)

            def gate(p):
                act.wait_ge(gates_ready, p + 1)
                if p >= 2:
                    act.wait_ge(updated, p - 1)
                nc.scalar.activation(rz[:, p % 2, 0:paired(p), :], gates[p % 4][:, 0:paired(p), 0:2 * D], ACT.Sigmoid
                                     ).then_inc(rz_ready, 1)

            def tanh(p):
                act.wait_ge(pre_ready, p + 1)
                state = new[:, p % 2, 0:paired(p), :]
                nc.scalar.activation(state, state, ACT.Tanh).then_inc(new_ready, 1)

            copy(0)
            for c in range(CH):
                if c + 1 < CH:
                    copy(c + 1)
                for p in pairs(c):
                    gate(p)
                    if p:
                        tanh(p - 1)
            tanh(PAIRS - 1)

        @block.vector
        def _(dve):
            step = Serial(dve, dve_step)
            for b in range(2):
                last = nc.vector.memset(ht[D:D + 1, b, :], 1.0)
            last.then_inc(ones_ready, 1)
            counts = g["attr_sum"][:, D:NB * (D + 1):D + 1]

            def scale(c):
                n = blocks(c)
                if c >= 2:
                    dve.wait_ge(turned_ready, c - 1)
                nc.vector.tensor_tensor(scaled[:, c % 2, 0:n, :], h[:, 4 * c:4 * c + n, :],
                                        wide(counts[:, 4 * c:4 * c + n]), ALU.mult).then_inc(scaled_ready, 1)

            def copy(c):
                n = blocks(c)
                dve.wait_ge(turned_ready, c + 1)
                if c >= 2:
                    dve.wait_ge(sum_ready, c - 1)
                nc.vector.tensor_copy(ct[:, c % 2, 0:n * P].rearrange("p (a b) -> p a b", b=P), ps_c[:, 0:n, :]
                                      ).then_inc(copied_dve, 1)

            def before_tanh(p):
                n = paired(p)
                pre = new[:, p % 2, 0:n, :]
                dve.wait_ge(rz_ready, p + 1)
                step(nc.vector.tensor_tensor(pre, rz[:, p % 2, 0:n, 0:D], gates[p % 4][:, 0:n, 3 * D:4 * D], ALU.mult))
                nc.vector.tensor_tensor(pre, pre, gates[p % 4][:, 0:n, 2 * D:3 * D], ALU.add).then_inc(pre_ready, 1)

            def update(p):
                n = paired(p)
                state, d = h[:, 2 * p:2 * p + n, :], diff[:, 0:n, :]
                dve.wait_ge(new_ready, p + 1)
                step(nc.vector.tensor_tensor(d, state, new[:, p % 2, 0:n, :], ALU.subtract))
                step(nc.vector.tensor_tensor(d, d, rz[:, p % 2, 0:n, D:2 * D], ALU.mult))
                nc.vector.tensor_tensor(state, d, new[:, p % 2, 0:n, :], ALU.add).then_inc(updated, 1)
                dve.wait_ge(updated, p + 1)

            scale(0)
            copy(0)
            for c in range(CH):
                if c + 1 < CH:
                    scale(c + 1)
                dve.wait_ge(sum_ready, c + 1)
                if c >= 2:
                    dve.wait_ge(gates_ready, 2 * c - 2)
                n = blocks(c) * P
                nc.vector.tensor_copy(at[:, c % 2, 0:n], ps_a[:, 0:n]).then_inc(sum_copied, 1)
                if c + 1 < CH:
                    copy(c + 1)
                for p in pairs(c):
                    before_tanh(p)
                    if p:
                        update(p - 1)
            update(PAIRS - 1)


def gated_layer(nc, g, slabs, w_msg, b_msg, w_ih, w_hh, b_ih, b_hh, out):
    with Scope(nc) as keep:
        h = keep.sb("gated_h", [P, HI, D], F32)
        parts = keep.sb("gated_parts", [P, HI, 3 * D], BF16)
        wd = keep.sb("wd", [D, P], F32)
        ws2 = keep.sb("ws2", [P, P], F32)
        we = keep.sb("we", [D + 1, P], F32)
        w_in = keep.sb("w_in", [P, 3 * D], F32)
        w_hid = keep.sb("w_hid", [D + 1, 4 * D], F32)
        weights = (wd, ws2, we, w_in, w_hid)
        normalise(nc, g, "_gated", h, parts)
        for t in range(2):
            turn_weights(nc, g, t, w_msg, b_msg, w_ih, w_hh, b_ih, b_hh, *weights)
            with Scope(nc, f"_round{t}") as s:
                first_two = s.sb("gated_first_two", [P, NPAD], F32)
                third = s.sb("gated_third", [D, NPAD], F32)
                sum_over_sources(nc, f"_round{t}", slabs, parts, first_two, third)
                gated_update(nc, g, t, h, first_two, third, *weights)
            if t == 0:
                split_features(nc, parts, h)
        with Scope(nc) as s:
            ready = s.sem("result_ready")
            stored = s.sem("result_stored")
            block = s.block()
            x, full = g["x"], (N // P) * P

            @block.vector
            def _(dve):
                nc.vector.tensor_tensor(x[:, :, :], x[:, :, :], h[:, :, :], ALU.add).then_inc(ready, 1)

            @block.sync
            def _(sp):
                sp.wait_ge(ready, 1)
                sp.dma_start(out[0:full, :].rearrange("(b p) f -> p b f", p=P), x[:, 0:N // P, :]).then_inc(stored, 16)
                sp.dma_start(out[full:N, :], x[0:N - full, N // P, :]).then_inc(stored, 16)
                sp.wait_ge(stored, 32)


def gnn_kernel(nc, x, src, dst, edge_attr_32, edge_attr_64, edge_weight, u, w1, b1, w2, b2, conv_w, conv_b, eps,
               w_msg, b_msg, w_ih, w_hh, b_ih, b_hh, out):
    g = {}
    Scope.spent.clear()
    slabs = nc.dram_tensor("slabs", [NSLAB, P, HI * SLAB], BF16)
    scratch = nc.dram_tensor("range_rows", [2, KB + 1, P], F32)
    sorted_rows = nc.dram_tensor("sorted_rows", [E, ROW], F32)
    scanned = nc.dram_tensor("scanned", [E, D], F32)
    carries = nc.dram_tensor("carries", [EP, D], F32)
    table = nc.dram_tensor("feature_table", [HI * P, D], F32)
    with ExitStack() as ctx:
        kept(nc, ctx, g)
        with ExitStack() as to_rank:
            kept_to_rank(nc, to_rank, g)
            prepare_keys(nc, g, src, dst, edge_weight)
            count_sources(nc, g)
            rank_and_scatter(nc, g, edge_attr_32, sorted_rows)
        scan_sorted(nc, g, sorted_rows, scanned, carries)
        locate_runs(nc, g)
        edge_statistics_layer(nc, g, scanned, carries, x, u, w1, b1, w2, b2)
        find_ranges(nc, g, scratch)
        build_adjacency(nc, g, slabs)
        sum_edge_attributes(nc, g, edge_attr_64)
        convolution_layer(nc, g, slabs, conv_w, conv_b)
        clear_spent(nc)
        weighted_layer(nc, g, table, scanned, carries, eps)
        gated_layer(nc, g, slabs, w_msg, b_msg, w_ih, w_hh, b_ih, b_hh, out)


_INS = ['x', 'src', 'dst', 'edge_attr_32', 'edge_attr_64', 'edge_weight', 'L0_gnn_u', 'L0_gnn_W1', 'L0_gnn_b1',
        'L0_gnn_W2', 'L0_gnn_b2', 'L1_gnn_W', 'L1_gnn_b', 'L2_gnn_eps', 'L3_gnn_w_msg', 'L3_gnn_b_msg',
        'L3_gnn_w_ih', 'L3_gnn_w_hh', 'L3_gnn_b_ih', 'L3_gnn_b_hh']
_OUTS = [((N, D), 'float32')]


def kernel(**inputs):
    import numpy as _np
    import concourse.bacc as _bacc
    from concourse import mybir as _mybir
    from concourse.bass_utils import run_bass_kernel_spmd as _run

    nc = _bacc.Bacc("TRN2", target_bir_lowering=False, num_devices=1)
    arrays, args = {}, []
    for name in _INS:
        a = _np.ascontiguousarray(inputs[name])
        arrays[f"in_{name}_dram"] = a
        args.append(nc.dram_tensor(f"in_{name}_dram", a.shape, _mybir.dt.from_np(a.dtype), kind="ExternalInput").ap())
    for i, (shape, dtype) in enumerate(_OUTS):
        dt = _mybir.dt.from_np(_np.dtype(dtype))
        args.append(nc.dram_tensor(f"out_{i}_dram", shape, dt, kind="ExternalOutput").ap())
    gnn_kernel(nc, *args)
    r = _run(nc, [arrays], core_ids=[0])
    return r.results[0]["out_0_dram"]
```

```python
from contextlib import ExitStack

import concourse.bass as bass
from concourse import mybir
from concourse.alu_op_type import AluOpType as ALU

F32 = mybir.dt.float32
BF16 = mybir.dt.bfloat16
FP16 = mybir.dt.float16
I32 = mybir.dt.int32
ACT = mybir.ActivationFunctionType
AX_X = mybir.AxisListType.X
PE, DVE, ACTE = mybir.EngineType.PE, mybir.EngineType.DVE, mybir.EngineType.Activation
SPE = mybir.EngineType.SP

P = 128
N = 6250
E = 200000
EP = 125
NT = E // EP
D = 64
DA = 32
HID = 128
HI = -(-N // P)
W = 8
KEYW = HI * W
NWIN = 800
WGRP = 3
SLAB_W = 40
NSLAB = NWIN // SLAB_W
SLAB = SLAB_W * W
NPAD = NWIN * W
NB = NPAD // P
HGRP = 16
TPAD = NT + WGRP
RU = 16
RG = RU // 2
WT = NWIN * RU // NT
QUAD = 4
NG = NT // RG
ROW = DA + 3
TB = -(-NT // P)
TLAST = NT - (TB - 1) * P
KB = -(-NWIN // P)
HUGE = 3.0e38
KEY_SCALE = 1.0 / 8
RANGES = "the ranges are worked out within the tiles"


class Scope(ExitStack):

    spent = []
    made = 0

    def __init__(self, nc, turn=""):
        super().__init__()
        self.nc, self.turn = nc, turn

    def sb(self, name, shape, dt):
        return self.enter_context(self.nc.sbuf_tensor(name + self.turn, shape, dt))

    def ps(self, name, shape, dt=F32):
        return self.enter_context(self.nc.psum_tensor(name + self.turn, shape, dt))

    def sem(self, name):
        Scope.made += 1
        handle = self.nc.alloc_semaphore(f"{name}_{Scope.made}")
        self.spent.append(handle)
        return handle

    def block(self):
        return self.enter_context(self.nc.Block())


class Serial:

    def __init__(self, eng, sem):
        self.eng, self.sem, self.n = eng, sem, 0

    def __call__(self, ins):
        self.n += 1
        ins.then_inc(self.sem, 1)
        self.eng.wait_ge(self.sem, self.n)


def clear_spent(nc):
    nc.clear_and_free_semaphores(Scope.spent)
    Scope.spent.clear()
    nc.all_engine_barrier()


def two_parts(queue, out, in_, sem):
    queue.dma_start(out[0:112], in_[0:112]).then_inc(sem, 16)
    queue.dma_start(out[112:EP], in_[112:EP]).then_inc(sem, 16)


def prepare_keys(nc, g, src, dst, edge_weight):
    with Scope(nc) as s:
        raw_i = s.sb("raw_i", [EP, 2, NT], I32)
        raw_w = s.sb("raw_w", [EP, NT], F32)
        part_i = s.sb("part_i", [EP, NT], I32)
        tile_i = s.sb("tile_i", [P, 2, TB, EP], I32)
        tile_f = s.sb("tile_f", [P, 2, TB, EP], F32)
        key_i = s.sb("key_i", [EP, 4, NT], I32)
        count_i = s.sb("count_i", [P, NWIN], I32)
        turned = s.ps("turned", [P, 8, 512])
        loaded = s.sem("loaded")
        consts = s.sem("consts")
        dve_step = s.sem("dve_step")
        tiles_float = s.sem("tiles_float")
        turned_ready = s.sem("turned_ready")
        turned_used = s.sem("turned_used")
        block = s.block()
        @block.sync
        def _(sp):
            sp.dma_start(raw_i[:, 0, :], src.rearrange("(p j) -> p j", p=EP)).then_inc(loaded, 16)
            sp.dma_start(raw_i[:, 1, :], dst.rearrange("(p j) -> p j", p=EP)).then_inc(loaded, 16)
            sp.dma_start(raw_w[:, :], edge_weight.rearrange("(p j) -> p j", p=EP)).then_inc(loaded, 16)

        @block.scalar
        def _(act):
            for n, x in enumerate((src, dst)):
                rows = x.rearrange("(t e) -> t e", e=EP)
                full = (TB - 1) * P
                act.dma_start(tile_i[:, n, 0:TB - 1, :],
                              rows[0:full, :].rearrange("(b t) e -> t b e", t=P)).then_inc(loaded, 16)
                act.dma_start(tile_i[0:TLAST, n, TB - 1, :], rows[full:NT, :]).then_inc(loaded, 16)

        @block.gpsimd
        def _(pool):
            pool.iota(count_i[:, :], pattern=[[1, NWIN]], base=0, channel_multiplier=0).then_inc(consts, 1)
            pool.iota(g["rowid_i"][:, :], pattern=[[0, 1]], base=0, channel_multiplier=1).then_inc(consts, 1)
            pool.memset(g["ident"][:, :], 0.0).then_inc(consts, 1)
            pool.memset(g["below"][:, :], 1.0).then_inc(consts, 1)
            pool.memset(g["ones"][:, :], 1.0).then_inc(consts, 1)
            pool.wait_ge(consts, 5)
            pool.affine_select(out=g["ident"][:, :], in_=g["ident"][:, :], compare_op=ALU.not_equal, fill=1.0,
                               base=0, pattern=[[-1, P]], channel_multiplier=1).then_inc(consts, 1)
            pool.affine_select(out=g["below"][:, :], in_=g["below"][:, :], compare_op=ALU.is_gt, fill=0.0,
                               base=0, pattern=[[1, P]], channel_multiplier=-1).then_inc(consts, 1)
            pool.tensor_copy(g["iota"][:, :], count_i[:, 0:512]).then_inc(consts, 1)
            pool.tensor_copy(g["rowid"][:, :], g["rowid_i"][:, :]).then_inc(consts, 1)
            pool.memset(g["mkeys"][:, NT:TPAD], -1.0).then_inc(consts, 1)
            pool.memset(g["lo_tiles"][:, NT:TPAD], 0.0).then_inc(consts, 1)

        @block.tensor
        def _(pe):
            pe.wait_ge(tiles_float, 4)
            pe.wait_ge(consts, 11)
            for n in range(2):
                for b in range(TB):
                    rows = P if b < TB - 1 else TLAST
                    last = nc.tensor.transpose(turned[0:EP, 4 * n + b // 4, (b % 4) * P:(b % 4) * P + rows],
                                               tile_f[0:rows, n, b, :], g["ident"][0:rows, 0:rows])
                last.then_inc(turned_ready, 1)

        @block.vector
        def _(dve):
            step = Serial(dve, dve_step)
            dve.wait_ge(loaded, 7 * 16)
            for n in range(2):
                nc.vector.tensor_copy(tile_f[:, n, 0:TB - 1, :], tile_i[:, n, 0:TB - 1, :]).then_inc(tiles_float, 1)
                nc.vector.tensor_copy(tile_f[0:TLAST, n, TB - 1, :],
                                      tile_i[0:TLAST, n, TB - 1, :]).then_inc(tiles_float, 1)
            dve.wait_ge(consts, 11)
            nc.vector.memset(g["zerob"][:, :], 0.0).then_inc(dve_step, 1)
            nc.vector.tensor_copy(g["identb"][:, :], g["ident"][:, :]).then_inc(dve_step, 1)
            nc.vector.tensor_copy(g["belowb"][:, :], g["below"][:, :]).then_inc(dve_step, 1)
            nc.vector.tensor_scalar(g["winbase"][:, :], count_i[:, :], 512.0, None, ALU.mult).then_inc(dve_step, 1)
            nc.vector.tensor_copy(g["sdw"][:, :, 0], raw_i[:, 0, :]).then_inc(dve_step, 1)
            nc.vector.tensor_copy(g["sdw"][:, :, 1], raw_i[:, 1, :]).then_inc(dve_step, 1)
            nc.vector.tensor_copy(g["sdw"][:, :, 2], raw_w[:, :]).then_inc(dve_step, 1)
            step.n = 7
            step(nc.vector.tensor_single_scalar(part_i[:, :], raw_i[:, 0, :], P - 1, ALU.bitwise_and))
            step(nc.vector.tensor_copy(g["lo"][:, 0:NT], part_i[:, :]))
            step(nc.vector.tensor_single_scalar(part_i[:, :], raw_i[:, 0, :], 7, ALU.arith_shift_right))
            step(nc.vector.tensor_copy(g["hi"][:, 0:NT], part_i[:, :]))
            step(nc.vector.memset(g["lo"][:, NT:NT + RG], 0.0))
            step(nc.vector.memset(g["hi"][:, NT:NT + RG], 0.0))
            step(nc.vector.tensor_copy(g["iota_rg"][:, :, :], g["iota"][:, 0:P].unsqueeze(2).broadcast_to([P, P, RG])))
            dve.wait_ge(tiles_float, 4)
            for op, c in ((ALU.min, 0), (ALU.max, 1)):
                step(nc.vector.tensor_reduce(g["span"][:, c, 0:TB - 1], tile_f[:, 1, 0:TB - 1, :], AX_X, op))
                step(nc.vector.tensor_reduce(g["span"][0:TLAST, c, TB - 1:TB], tile_f[0:TLAST, 1, TB - 1:TB, :],
                                             AX_X, op))
            for n in range(2):
                dve.wait_ge(turned_ready, n + 1)
                flat = turned[0:EP, 4 * n:4 * n + 4, :].rearrange("p a b -> p (a b)")
                if n:
                    step(nc.vector.tensor_copy(g["dkey"][:, 0:NT], flat[:, 0:NT]))
                step(nc.vector.tensor_copy(key_i[:, n, :], flat[:, 0:NT]))
            s_i, d_i, u_i, v_i = (key_i[:, n, :] for n in range(4))
            step(nc.vector.tensor_single_scalar(u_i, d_i, 3, ALU.arith_shift_right))
            step(nc.vector.tensor_single_scalar(v_i, d_i, W - 1, ALU.bitwise_and))
            step(nc.vector.tensor_single_scalar(d_i, s_i, 7, ALU.arith_shift_right))
            step(nc.vector.scalar_tensor_tensor(raw_w[:, :], d_i, float(W), v_i, ALU.mult, ALU.add))
            step(nc.vector.scalar_tensor_tensor(g["mkeys"][:, 0:NT], u_i, 512.0, raw_w[:, :], ALU.mult, ALU.add))
            step(nc.vector.tensor_single_scalar(v_i, s_i, P - 1, ALU.bitwise_and))
            step(nc.vector.tensor_scalar(g["lo_tiles"][:, 0:NT], v_i, KEY_SCALE, None, ALU.mult))


def one_hots(nc, g, out_lo, out_hi, n):
    def keys(x, width):
        return x[:, bass.ds(n * RG, RG)].unsqueeze(1).broadcast_to([EP, width, RG])
    nc.vector.tensor_tensor(out_lo, g["iota_rg"][0:EP, :, :], keys(g["lo"], P), ALU.is_equal)
    return nc.vector.tensor_tensor(out_hi, g["iota_rg"][0:EP, 0:HI, :], keys(g["hi"], HI), ALU.is_equal)


def count_sources(nc, g):
    with Scope(nc) as s:
        oh_lo = s.sb("hist_lo", [EP, 2, P, RG], BF16)
        oh_hi = s.sb("hist_hi", [EP, 2, HI, RG], BF16)
        totals = s.sb("totals", [P, HI], F32)
        upto = s.sb("upto", [P, HI], F32)
        zeros = s.sb("zeros", [P, HI], F32)
        hist = s.ps("hist", [P, HI])
        sums = s.ps("sums", [P, 2, HI])
        oh_ready = s.sem("oh_ready")
        oh_used = s.sem("oh_used")
        sums_ready = s.sem("sums_ready")
        dve_step = s.sem("dve_step")
        block = s.block()
        @block.vector
        def _(dve):
            step = Serial(dve, dve_step)
            step(nc.vector.memset(zeros[:, :], 0.0))
            with dve.Fori(0, NG // 2) as i:
                for h in range(2):
                    dve.wait_ge(oh_used, 2 * i + h + 1)
                    one_hots(nc, g, oh_lo[:, h], oh_hi[:, h], 2 * i + h).then_inc(oh_ready, 1)
            dve.wait_ge(oh_used, NG + 2)
            step(nc.vector.tensor_copy(g["out_deg"][:, 0:HI], hist[:, :]))
            step(nc.vector.memset(g["out_deg"][:, HI:NB], 0.0))
            dve.wait_ge(sums_ready, 1)
            step(nc.vector.tensor_copy(totals[:, :], sums[:, 1, :]))
            step(nc.vector.tensor_tensor_scan(upto[:, :], totals[:, :], zeros[:, :], 0.0, ALU.add, ALU.add))
            step(nc.vector.tensor_tensor(upto[:, :], upto[:, :], totals[:, :], ALU.subtract))
            step(nc.vector.tensor_tensor(g["start"][:, 0:HI], sums[:, 0, :], upto[:, :], ALU.add))

        @block.tensor
        def _(pe):
            pe.sem_inc(oh_used, 2)
            nc.tensor.matmul(hist[:, :], g["zerob"][:, 0:P], g["zerob"][:, 0:HI], start=True, stop=True)
            with pe.Fori(0, NG // 2) as i:
                for h in range(2):
                    pe.wait_ge(oh_ready, 2 * i + h + 1)
                    for u in range(RG):
                        last = nc.tensor.matmul(hist[:, :], oh_lo[:, h, :, u], oh_hi[:, h, :, u], start=False,
                                                stop=True, skip_group_check=True)
                    last.then_inc(oh_used, 1)
            pe.wait_ge(dve_step, 2)
            nc.tensor.matmul(sums[:, 0, :], g["below"][:, :], g["out_deg"][:, 0:HI], start=True, stop=True)
            nc.tensor.matmul(sums[:, 1, :], g["ones"][:, :], g["out_deg"][:, 0:HI], start=True,
                             stop=True).then_inc(sums_ready, 1)


def rank_and_build(nc, g, edge_attr_32, sorted_rows, slabs):
    with Scope(nc) as s:
        oh_lo = s.sb("oh_lo", [EP, 2, P, RG], BF16)
        oh_hi = s.sb("oh_hi", [EP, 2, HI, RG], BF16)
        lo_rows_b = s.sb("lo_rows_b", [P, 2, 2, QUAD, EP], BF16)
        lo_rows_f = s.sb("lo_rows_f", [P, 2, 2, QUAD, EP], F32)
        earlier = s.sb("earlier", [EP, 2, 2, QUAD, EP], BF16)
        counts = s.sb("counts", [P, 2, HI], F32)
        picked = s.sb("picked", [EP, 2, RG, HI], BF16)
        place = s.sb("place", [EP, 2, RG], F32)
        place_i = s.sb("place_i", [EP, 2, RG], I32)
        attr = s.sb("attr", [EP, 2, RG, DA], F32)
        rows = s.sb("rows", [EP, 2, RG, ROW], F32)
        low = s.sb("low", [EP, 2 * P * WGRP], BF16)
        high = s.sb("high", [EP, 2 * WGRP * KEYW], BF16)
        window_keys = s.sb("window_keys", [EP, 2 * WGRP], FP16)
        iota_g = s.sb("iota_g", [P, KEYW, WGRP], FP16)
        slab = s.sb("slab", [P, HI, 2 * SLAB], BF16)
        turned = s.ps("turned_lo", [P, 2, QUAD, P], BF16)
        part = [s.ps(f"part{b}", [P, HI, W]) for b in range(2)]
        same0 = s.ps("same0", [EP, QUAD * EP])
        same1 = s.ps("same1", [EP, QUAD * EP])
        count_rows = [s.ps(f"count_rows{b}", [EP, 2, HI]) for b in range(2)]
        running = s.ps("running", [P, HI])
        oh_ready = s.sem("oh_ready")
        turned_ready = s.sem("turned_ready")
        lo_rows_ready = s.sem("lo_rows_ready")
        same_ready = s.sem("same_ready")
        earlier_ready = s.sem("earlier_ready")
        counts_ready = s.sem("counts_ready")
        count_rows_ready = s.sem("count_rows_ready")
        updated = s.sem("updated")
        placed = s.sem("placed")
        places_ready = s.sem("places_ready")
        rows_ready = s.sem("rows_ready")
        attr0 = s.sem("attr0")
        attr1 = s.sem("attr1")
        scattered0 = s.sem("scattered0")
        scattered1 = s.sem("scattered1")
        pool_turns = s.sem("pool_turns")
        iota_ready = s.sem("iota_ready")
        keys_ready = s.sem("keys_ready")
        made = s.sem("made")
        used = s.sem("used")
        copied = s.sem("copied")
        slab_free = s.sem("slab_free")
        stored = [s.sem(f"slab_stored{b}") for b in range(2)]
        block = s.block()
        same = (same0, same1)
        MOST = NWIN * NT
        RING = 2 * SLAB_W // WT
        attr_in, scattered = (attr0, attr1), (scattered0, scattered1)
        attrs = edge_attr_32.rearrange("(p j) c -> p (j c)", p=EP)
        ALL = 16 * RG

        @block.sync
        def _(sp):
            sp.sem_inc(slab_free, RING)
            with sp.Fori(0, NG // 2 // RING) as r:
                for k in range(2):
                    with sp.Fori(0, RING // 2) as m:
                        i = r * RING + k * (RING // 2) + m
                        for h in range(2):
                            sp.wait_ge(rows_ready, 2 * i + h + 1)
                            sp.dma_start(attr[:, h].rearrange("p j c -> p (j c)"),
                                         attrs[:, bass.ds((2 * i + h) * RG * DA, RG * DA)]).then_inc(attr_in[h], 16)
                    n = r * 2 + k
                    sp.wait_ge(copied, n * SLAB_W + SLAB_W + 2)
                    sp.dma_start(slabs[bass.ds(n, 1), :, :].rearrange("a p (h c) -> p (a h) c", c=SLAB),
                                 slab[:, :, k * SLAB:(k + 1) * SLAB]).then_inc(stored[k], 16)
                    sp.wait_ge(stored[k], r * 16 + 16)
                    sp.sem_inc(slab_free, RING // 2)

        @block.gpsimd
        def _(pool):
            with pool.Fori(0, NG // 2) as i:
                for h in range(2):
                    pool.wait_ge(places_ready, 2 * i + h + 1)
                    pool.wait_ge(rows_ready, 2 * i + h + 3)
                    pool.sem_inc(pool_turns, 1)
                    for u in range(RG):
                        pool.indirect_dma_start(sorted_rows[:, :],
                                                bass.IndirectOffsetOnAxis(ap=place_i[:, h, u:u + 1], axis=0),
                                                rows[:, h, u, :], None).then_inc(scattered[h], 16)
            for h in range(2):
                pool.wait_ge(scattered[h], ALL * NG // 2)

        @block.vector
        def _(dve):
            def lo_hi(n, h):
                one_hots(nc, g, oh_lo[:, h], oh_hi[:, h], n).then_inc(oh_ready, 1)

            def mask(n, h):
                for q in range(2):
                    dve.wait_ge(same_ready, 2 * n + q + 1)
                    nc.vector.tensor_tensor(earlier[:, h, q], same[q][:, :].rearrange("p (u e) -> p u e", u=QUAD),
                                            g["belowb"][0:EP, 0:EP].unsqueeze(1).broadcast_to([EP, QUAD, EP]),
                                            ALU.mult).then_inc(earlier_ready, 1)

            def pick(n, h, u):
                if u % 2 == 0:
                    dve.wait_ge(count_rows_ready, n * RG + u + 3)
                nc.vector.tensor_tensor_reduce(out=picked[:, h, u, :], in0=count_rows[u // 2 % 2][:, u % 2, :],
                                               in1=oh_hi[:, h, :, u], scale=1.0, scalar=0.0, op0=ALU.mult,
                                               op1=ALU.add, accum_out=place[:, h, u:u + 1]).then_inc(placed, 1)

            def window(i, j, before, offset):
                base = g["winbase"][0:EP, bass.ds(i * WT + j, 1)]
                with dve.Fori(before[j], before[j + 1]) as v:
                    t = nc.s_assert_within(v * WGRP - offset[j], 0, NT, skip_runtime_bounds_check_because=RANGES)
                    slot = v & 1
                    keys = window_keys[:, bass.ds(slot * WGRP, WGRP)]
                    dve.wait_ge(used, v + 1)
                    nc.vector.tensor_scalar(keys, g["mkeys"][:, bass.ds(t, WGRP)], base, KEY_SCALE,
                                            ALU.subtract, ALU.mult).then_inc(keys_ready, 1)
                    nc.vector.tensor_tensor(
                        low[:, bass.ds(slot * (P * WGRP), P * WGRP)].rearrange("p (a b) -> p a b", b=WGRP),
                        iota_g[0:EP, 0:P, :],
                        g["lo_tiles"][:, bass.ds(t, WGRP)].unsqueeze(1).broadcast_to([EP, P, WGRP]), ALU.is_equal)
                    dve.wait_ge(keys_ready, v + 1)
                    nc.vector.tensor_tensor(
                        high[:, bass.ds(slot * (WGRP * KEYW), WGRP * KEYW)].rearrange("p (a b) -> p a b", b=WGRP),
                        iota_g[0:EP, :, :], keys.unsqueeze(1).broadcast_to([EP, KEYW, WGRP]), ALU.is_equal
                    ).then_inc(made, 1)

            nc.vector.tensor_scalar(iota_g[:, :, :], g["iota"][:, 0:KEYW].unsqueeze(2).broadcast_to([P, KEYW, WGRP]),
                                    KEY_SCALE, None, ALU.mult).then_inc(iota_ready, 1)
            dve.wait_ge(iota_ready, 1)
            dve.sem_inc(placed, 4)
            lo_hi(0, 0)
            mask(0, 0)
            def turn(i, first):
                before, offset = load_ranges(nc, g["win_table"], DVE, i * WT, WT, MOST)
                for h in range(2):
                    n = 2 * i + h
                    dve.wait_ge(count_rows_ready, n * RG + 1)
                    dve.wait_ge(placed, n * RG + 4)
                    lo_hi(n + 1, 1 - h)
                    for u in range(RG):
                        if u % 2 == 0:
                            window(i, (h * RG + u) // 2, before, offset)
                        pick(n, h, u)
                        if u == 5:
                            mask(n + 1, 1 - h)
                    dve.wait_ge(placed, n * RG + RG + 4)
                    if not first:
                        dve.wait_ge(scattered[h], ALL * i)
                    nc.vector.tensor_copy(place_i[:, h, :], place[:, h, :]).then_inc(places_ready, 1)

            turn(0, True)
            with dve.Fori(1, NG // 2) as i:
                turn(i, False)

        @block.scalar
        def _(act):
            act.sem_inc(rows_ready, 2)

            def lo_rows(n, h, q):
                act.wait_ge(turned_ready, n + 1)
                nc.scalar.copy(lo_rows_b[:, h, q], turned[:, q, :, 0:EP])
                nc.scalar.copy(lo_rows_f[:, h, q], turned[:, q, :, 0:EP]).then_inc(lo_rows_ready, 1)

            def window(k, j, before):
                act.wait_ge(used, before[j + 1] + 2)
                nc.scalar.copy(slab[:, :, bass.ds(k * (WT * W) + j * W, W)], part[j % 2][:, :, :]
                               ).then_inc(copied, 1)

            nc.scalar.copy(counts[:, 0, :], g["start"][:, 0:HI]).then_inc(counts_ready, 1)
            for q in range(2):
                lo_rows(0, 0, q)
            def turn(i, k, first):
                before, _ = load_ranges(nc, g["win_table"], ACTE, i * WT, WT, MOST)
                act.wait_ge(slab_free, i + 1)
                for h in range(2):
                    n = 2 * i + h
                    for u in range(RG):
                        act.wait_ge(updated, n * RG + u + 1)
                        nc.scalar.copy(counts[:, (u + 1) % 2, :], running[:, :]).then_inc(counts_ready, 1)
                        if u in (1, 3):
                            lo_rows(n + 1, 1 - h, u // 2)
                        if u == 5:
                            act.wait_ge(attr_in[h], 16 * (i + 1))
                            if not first:
                                act.wait_ge(scattered[h], ALL * i)
                            nc.scalar.copy(rows[:, h, :, 0:DA], attr[:, h])
                            nc.scalar.copy(rows[:, h, :, DA:ROW],
                                           g["sdw"][:, bass.ds(n * RG, RG), :]).then_inc(rows_ready, 1)
                        if u % 2 and h * RG + u > 1:
                            window(k, (h * RG + u) // 2 - 1, before)
                window(k, WT - 1, before)

            turn(0, 0, True)
            with act.Fori(1, RING) as k:
                turn(k, k, False)
            with act.Fori(1, NG // 2 // RING) as r:
                with act.Fori(0, RING) as k:
                    turn(r * RING + k, k, False)

        @block.tensor
        def _(pe):
            pe.sem_inc(count_rows_ready, 1)

            def turn(n, h):
                pe.wait_ge(oh_ready, n + 1)
                for q in range(2):
                    for u in range(QUAD):
                        last = nc.tensor.transpose(turned[:, q, u, 0:EP],
                                                   oh_lo[:, h, :, q * QUAD + u], g["identb"][0:EP, 0:EP])
                last.then_inc(turned_ready, 1)

            def compare(n, h):
                for q in range(2):
                    pe.wait_ge(lo_rows_ready, 2 * n + q + 1)
                    for u in range(QUAD):
                        x = lo_rows_b[:, h, q, u, :]
                        last = nc.tensor.matmul(same[q][:, u * EP:(u + 1) * EP], x, x, start=True, stop=True)
                    last.then_inc(same_ready, 1)

            def chain(n, h, u):
                q, v = divmod(u, QUAD)
                if v == 0:
                    pe.wait_ge(earlier_ready, 2 * n + q + 1)
                pe.wait_ge(counts_ready, n * RG + u + 1)
                nc.tensor.matmul(running[:, :], oh_lo[:, h, :, u], oh_hi[:, h, :, u], start=False, stop=True,
                                 skip_group_check=True).then_inc(updated, 1)
                if u % 2 == 0:
                    pe.wait_ge(placed, n * RG + u + 2)
                out = count_rows[u // 2 % 2][:, u % 2, :]
                nc.tensor.matmul(out, lo_rows_f[:, h, q, v, :], counts[:, u % 2, :], start=True, stop=False)
                nc.tensor.matmul(out, earlier[:, h, q, v, :], oh_hi[:, h, :, u], start=False,
                                 stop=True).then_inc(count_rows_ready, 1)

            def window(i, j, before):
                out = part[j % 2][:, :, :].rearrange("p a b -> p (a b)")
                pe.wait_ge(copied, i * WT + j + 1)
                nc.tensor.matmul(out, g["zerob"][0:EP, 0:P], g["zerob"][0:EP, 0:KEYW], start=True, stop=True)
                with pe.Fori(before[j], before[j + 1]) as v:
                    slot = v & 1
                    pe.wait_ge(made, v + 1)
                    for k in range(WGRP):
                        last = nc.tensor.matmul(out, low[:, bass.DynSlice(slot * (P * WGRP) + k, P, WGRP)],
                                                high[:, bass.DynSlice(slot * (WGRP * KEYW) + k, KEYW, WGRP)],
                                                start=False, stop=True, skip_group_check=True)
                    last.then_inc(used, 1)

            pe.sem_inc(used, 2)
            pe.sem_inc(copied, 2)
            nc.tensor.matmul(running[:, :], g["ident"][:, :], g["start"][:, 0:HI], start=True, stop=True)
            turn(0, 0)
            compare(0, 0)
            with pe.Fori(0, NG // 2) as i:
                before, _ = load_ranges(nc, g["win_table"], PE, i * WT, WT, MOST)
                for h in range(2):
                    n = 2 * i + h
                    turn(n + 1, 1 - h)
                    for u in range(RG):
                        if u == 5:
                            compare(n + 1, 1 - h)
                        chain(n, h, u)
                        if u % 2:
                            window(i, (h * RG + u) // 2, before)


def scan_sorted(nc, g, sorted_rows, scanned, carries):
    J = 160
    STEPS = NT // J
    with Scope(nc) as s:
        rows = [s.sb(f"scan_rows{b}", [EP, J, ROW], F32) for b in range(2)]
        out = [s.sb(f"scan_out{b}", [EP, J, 2 * DA], F32) for b in range(2)]
        cap = s.sb("cap", [EP, J], F32)
        differs = s.sb("differs", [EP, J], F32)
        last_key = s.sb("last_key", [EP, 1], F32)
        carry = s.sb("carry", [EP, 2 * DA], F32)
        state = s.sb("state", [2 * DA, EP], F32)
        turned_carry = s.sb("turned_carry", [2 * DA, EP], F32)
        key_row = s.sb("key_row", [2 * DA, EP], F32)
        keep = s.sb("keep", [2 * DA, EP], F32)
        keep_cap = s.sb("keep_cap", [DA, EP], F32)
        carry_in = s.sb("carry_in", [EP, 2 * DA], F32)
        ps_carry = s.ps("ps_carry", [2 * DA, EP])
        ps_key = s.ps("ps_key", [2 * DA, EP])
        ps_in = s.ps("ps_in", [EP, 2 * DA])
        rows_in = [s.sem(f"rows_in{b}") for b in range(2)]
        rows_out = [s.sem(f"rows_out{b}") for b in range(2)]
        dve_step = s.sem("dve_step")
        scans_done = s.sem("scans_done")
        pe_done = s.sem("pe_done")
        shifted = s.sem("shifted")
        carried = s.sem("carried")
        block = s.block()
        src_v = sorted_rows[:, :].rearrange("(p j) c -> p j c", p=EP)
        dst_v = scanned[:, :].rearrange("(p j) c -> p j c", p=EP)

        @block.sync
        def _(sp):
            for k in range(STEPS):
                if k >= 2:
                    sp.wait_ge(scans_done, k - 1)
                two_parts(sp, rows[k % 2][:, :, :], src_v[:, k * J:(k + 1) * J, :], rows_in[k % 2])

        @block.scalar
        def _(act):
            for k in range(STEPS):
                act.wait_ge(scans_done, k + 1)
                two_parts(act, dst_v[:, k * J:(k + 1) * J, :], out[k % 2][:, :, :], rows_out[k % 2])
            act.wait_ge(carried, 1)
            act.dma_start(carries[:, :], carry_in[:, :]).then_inc(rows_out[0], 16)
            act.wait_ge(rows_out[0], 16 * (STEPS + 1))
            act.wait_ge(rows_out[1], 16 * STEPS)

        @block.vector
        def _(dve):
            step = Serial(dve, dve_step)
            step(nc.vector.memset(last_key[:, :], -1.0))
            step(nc.vector.memset(carry[:, :], 0.0))
            for k in range(STEPS):
                rk, ok = rows[k % 2], out[k % 2]
                same = g["same_src"][:, k * J:(k + 1) * J]
                dve.wait_ge(rows_in[k % 2], 32 * (k // 2 + 1))
                src_c, dst_c, w_c = (rk[:, :, DA + c] for c in range(3))
                nc.vector.tensor_tensor(same[:, 0:1], src_c[:, 0:1], last_key[:, :], ALU.is_equal)
                step(nc.vector.tensor_tensor(same[:, 1:J], src_c[:, 1:J], src_c[:, 0:J - 1], ALU.is_equal))
                nc.vector.tensor_scalar(cap[:, :], same, -0.5, HUGE, ALU.add, ALU.mult)
                nc.vector.tensor_copy(last_key[:, :], src_c[:, J - 1:J])
                nc.vector.tensor_copy(g["dst_sorted"][:, k * J:(k + 1) * J], dst_c)
                step(nc.vector.tensor_tensor(differs[:, :], src_c, dst_c, ALU.not_equal))
                step(nc.vector.tensor_tensor(g["w_sorted"][:, k * J:(k + 1) * J], w_c, differs[:, :], ALU.mult))
                if k >= 2:
                    dve.wait_ge(rows_out[k % 2], 32 * (k // 2))
                for f in range(DA):
                    nc.vector.tensor_tensor_scan(ok[:, :, f], cap[:, :], rk[:, :, f], carry[:, f:f + 1],
                                                 ALU.min, ALU.max)
                    last = nc.vector.tensor_tensor_scan(ok[:, :, DA + f], same, rk[:, :, f],
                                                        carry[:, DA + f:DA + f + 1], ALU.mult, ALU.add)
                last.then_inc(scans_done, 1)
                dve.wait_ge(scans_done, k + 1)
                step(nc.vector.tensor_copy(carry[:, :], ok[:, J - 1, :]))
            dve.wait_ge(pe_done, 1)
            step(nc.vector.tensor_copy(turned_carry[:, :], ps_carry[:, :]))
            step(nc.vector.tensor_copy(key_row[:, :], ps_key[:, :]))
            step(nc.vector.memset(keep[:, 0:1], 0.0))
            step(nc.vector.tensor_tensor(keep[:, 1:EP], key_row[:, 1:EP], key_row[:, 0:EP - 1], ALU.is_equal))
            step(nc.vector.tensor_copy(g["keep_run"][:, :], keep[:, :]))
            step(nc.vector.tensor_scalar(keep_cap[:, :], keep[0:DA, :], -0.5, HUGE, ALU.add, ALU.mult))
            step(nc.vector.memset(state[:, 0:1], 0.0))
            step(nc.vector.tensor_tensor_scan(state[0:DA, 1:EP], keep_cap[:, 0:EP - 1], turned_carry[0:DA, 0:EP - 1],
                                              0.0, ALU.min, ALU.max))
            step(nc.vector.tensor_tensor_scan(state[DA:2 * DA, 1:EP], keep[DA:2 * DA, 0:EP - 1],
                                              turned_carry[DA:2 * DA, 0:EP - 1], 0.0, ALU.mult, ALU.add))
            nc.vector.sem_inc(shifted, 1)
            dve.wait_ge(pe_done, 2)
            nc.vector.tensor_copy(carry_in[:, :], ps_in[:, :]).then_inc(carried, 1)

        @block.tensor
        def _(pe):
            pe.wait_ge(dve_step, 2 + 4 * STEPS)
            nc.tensor.matmul(ps_key[:, :], last_key[:, :].broadcast_to([EP, 2 * DA]), g["ident"][0:EP, 0:EP],
                             start=True, stop=True)
            nc.tensor.transpose(ps_carry[:, :], carry[:, :], g["ident"][0:EP, 0:EP]).then_inc(pe_done, 1)
            pe.wait_ge(shifted, 1)
            nc.tensor.transpose(ps_in[:, :], state[:, :], g["ident"][0:2 * DA, 0:2 * DA]).then_inc(pe_done, 1)


def locate_runs(nc, g):
    with Scope(nc) as s:
        end = s.sb("end", [P, HI], F32)
        part = s.sb("part", [P, HI], F32)
        rest = s.sb("rest", [P, HI], F32)
        test = s.sb("test", [P, HI], F32)
        part_i = s.sb("run_part_i", [P, HI], I32)
        dve_step = s.sem("dve_step")
        block = s.block()

        @block.vector
        def _(dve):
            step = Serial(dve, dve_step)
            start, deg = g["start"][:, 0:HI], g["out_deg"][:, 0:HI]
            step(nc.vector.tensor_tensor(end[:, :], start, deg, ALU.add))
            step(nc.vector.tensor_scalar(end[:, :], end[:, :], -1.0, 0.0, ALU.add, ALU.max))
            step(nc.vector.tensor_copy(g["end_i"][:, :], end[:, :]))
            step(nc.vector.tensor_scalar(part[:, :], end[:, :], 1.0 / NT, None, ALU.mult))
            step(nc.vector.tensor_copy(part_i[:, :], part[:, :]))
            step(nc.vector.tensor_copy(part[:, :], part_i[:, :]))
            step(nc.vector.scalar_tensor_tensor(rest[:, :], part[:, :], -float(NT), end[:, :], ALU.mult, ALU.add))
            step(nc.vector.tensor_scalar(test[:, :], rest[:, :], float(NT), None, ALU.is_ge))
            step(nc.vector.tensor_tensor(part[:, :], part[:, :], test[:, :], ALU.add))
            step(nc.vector.tensor_scalar(test[:, :], rest[:, :], 0.0, None, ALU.is_lt))
            step(nc.vector.tensor_tensor(part[:, :], part[:, :], test[:, :], ALU.subtract))
            step(nc.vector.tensor_copy(g["end_part_i"][:, :], part[:, :]))
            step(nc.vector.scalar_tensor_tensor(test[:, :], part[:, :], float(NT), start, ALU.mult, ALU.is_gt))
            step(nc.vector.tensor_scalar(g["has_out"][:, :], deg, 0.0, None, ALU.is_gt))
            step(nc.vector.tensor_tensor(g["spans"][:, :], test[:, :], g["has_out"][:, :], ALU.mult))


def gather_runs(nc, pool, g, scanned, carries, ends, carry_in, sem):
    for b in range(HI):
        pool.indirect_dma_start(ends[:, b, :], None, scanned[:, :],
                                bass.IndirectOffsetOnAxis(ap=g["end_i"][:, b:b + 1], axis=0)).then_inc(sem, 16)
        pool.indirect_dma_start(carry_in[:, b, :], None, carries[:, :],
                                bass.IndirectOffsetOnAxis(ap=g["end_part_i"][:, b:b + 1], axis=0)
                                ).then_inc(sem, 16)


def find_ranges(nc, g, scratch):
    Q = KB + 1
    ROWLEN = Q * P
    with Scope(nc) as s:
        least = s.sb("least", [P, NT], F32)
        greatest = s.sb("greatest", [P, NT], F32)
        count_i = s.sb("tile_count_i", [P, NT], I32)
        up = s.sb("up", [P, NT], F32)
        down = s.sb("down", [P, NT], F32)
        meets = s.sb("meets", [P, NT], F32)
        meets2 = s.sb("meets2", [P, NT], F32)
        first_t = s.sb("first_target", [P, Q], F32)
        last_t = s.sb("last_target", [P, Q], F32)
        ends = s.sb("range_ends", [P, 2, Q], F32)
        turned_sb = s.sb("ranges_turned", [Q, 2, P], F32)
        row = s.sb("range_row", [1, 2, ROWLEN], F32)
        steps = s.sb("range_steps", [1, ROWLEN], F32)
        steps_i = s.sb("range_steps_i", [1, ROWLEN], I32)
        cum = s.sb("range_cum", [1, ROWLEN], F32)
        zero = s.sb("range_zero", [1, ROWLEN], F32)
        spread = s.ps("spread", [P, 8, 512])
        consts = s.sem("consts")
        spread_ready = s.sem("spread_ready")
        dve_step = s.sem("dve_step")
        ends_ready = s.sem("ends_ready")
        turned_ready = s.sem("turned_ready")
        stored = s.sem("stored")
        rows_ready = s.sem("rows_ready")
        block = s.block()

        @block.gpsimd
        def _(pool):
            pool.iota(count_i[:, :], pattern=[[1, NT]], base=0, channel_multiplier=0).then_inc(consts, 1)
            pool.memset(zero[:, :], 0.0).then_inc(consts, 1)

        @block.tensor
        def _(pe):
            for c in range(2):
                for b in range(TB):
                    rows = P if b < TB - 1 else TLAST
                    last = nc.tensor.matmul(spread[:, 4 * c + b // 4, (b % 4) * P:(b % 4) * P + rows],
                                            g["span"][0:rows, c, b:b + 1].broadcast_to([rows, P]),
                                            g["ident"][0:rows, 0:rows], start=True, stop=True)
            last.then_inc(spread_ready, 1)
            pe.wait_ge(ends_ready, 1)
            for c in range(2):
                last = nc.tensor.transpose(spread[0:Q, 0, c * P:(c + 1) * P], ends[:, c, :], g["ident"][:, :])
            last.then_inc(turned_ready, 1)

        @block.vector
        def _(dve):
            step = Serial(dve, dve_step)
            for q in range(KB):
                step(nc.vector.tensor_scalar(first_t[:, q:q + 1], g["rowid"][:, :], float(W), float(W * P * q),
                                             ALU.mult, ALU.add))
            step(nc.vector.tensor_scalar(first_t[:, KB:Q], g["rowid"][:, :], float(P), None, ALU.mult))
            step(nc.vector.tensor_scalar(last_t[:, 0:KB], first_t[:, 0:KB], float(W - 1), None, ALU.add))
            step(nc.vector.tensor_scalar(last_t[:, KB:Q], first_t[:, KB:Q], float(P - 1), None, ALU.add))
            dve.wait_ge(consts, 2)
            step(nc.vector.tensor_scalar(up[:, :], count_i[:, :], 1.0, None, ALU.add))
            step(nc.vector.tensor_scalar(down[:, :], count_i[:, :], -1.0, float(NT), ALU.mult, ALU.add))
            dve.wait_ge(spread_ready, 1)
            for x, c in ((least, 0), (greatest, 1)):
                step(nc.vector.tensor_copy(x[:, :], spread[:, 4 * c:4 * c + 4, :].rearrange("p a b -> p (a b)")[:, 0:NT]))
            for q in range(Q):
                step(nc.vector.tensor_scalar(meets[:, :], least[:, :], last_t[:, q:q + 1], None, ALU.is_le))
                step(nc.vector.scalar_tensor_tensor(meets[:, :], greatest[:, :], first_t[:, q:q + 1], meets[:, :],
                                                    ALU.is_ge, ALU.mult))
                for x, c in ((up, 0), (down, 1)):
                    step(nc.vector.tensor_tensor_reduce(out=meets2[:, :], in0=meets[:, :], in1=x[:, :], scale=1.0,
                                                        scalar=0.0, op0=ALU.mult, op1=ALU.max,
                                                        accum_out=ends[:, c, q:q + 1]))
            dve.sem_inc(ends_ready, 1)
            dve.wait_ge(turned_ready, 1)
            nc.vector.tensor_copy(turned_sb[:, :, :], spread[0:Q, 0, 0:2 * P].rearrange("q (c p) -> q c p", c=2)
                                  ).then_inc(rows_ready, 1)
            dve.wait_ge(stored, 32)
            behind, left = row[:, 0, :], row[:, 1, :]
            step(nc.vector.tensor_tensor(steps[:, :], behind, left, ALU.add))
            step(nc.vector.tensor_scalar(steps[:, :], steps[:, :], -float(NT), 1.0, ALU.add, ALU.max))
            step(nc.vector.tensor_scalar(left, left, -1.0, float(NT), ALU.mult, ALU.add))
            step(nc.vector.tensor_scalar(left, left, float(NT - 1), None, ALU.min))
            win, blk = slice(0, NWIN), slice(KB * P, KB * P + NB)
            step(nc.vector.tensor_scalar(steps[:, win], steps[:, win], float(WGRP - 1), 683.0, ALU.add, ALU.mult))
            step(nc.vector.tensor_scalar(steps[:, blk], steps[:, blk], float(HGRP - 1), None, ALU.add))
            for part, shift in ((win, 11), (blk, 4)):
                step(nc.vector.tensor_copy(steps_i[:, part], steps[:, part]))
                step(nc.vector.tensor_single_scalar(steps_i[:, part], steps_i[:, part], shift,
                                                    ALU.arith_shift_right))
                step(nc.vector.tensor_copy(steps[:, part], steps_i[:, part]))
            step(nc.vector.tensor_scalar(cum[:, blk], steps[:, blk], -float(HGRP), float(NT), ALU.mult, ALU.add))
            step(nc.vector.tensor_tensor(left[:, blk], left[:, blk], cum[:, blk], ALU.min))
            for part, n, size, table in ((win, NWIN, WGRP, g["win_table"]), (blk, NB, HGRP, g["blk_table"])):
                step(nc.vector.tensor_tensor_scan(cum[:, part], steps[:, part], zero[:, part], 0.0, ALU.add, ALU.add))
                step(nc.vector.memset(table[:, 0:2 * n + 2], 0))
                step(nc.vector.tensor_copy(table[:, 2:2 * n + 2:2], cum[:, part]))
                step(nc.vector.tensor_tensor(cum[:, part], cum[:, part], steps[:, part], ALU.subtract))
                step(nc.vector.scalar_tensor_tensor(table[:, 1:2 * n + 1:2], cum[:, part], float(size), left[:, part],
                                                    ALU.mult, ALU.subtract))

        @block.sync
        def _(sp):
            sp.wait_ge(rows_ready, 1)
            sp.dma_start(scratch[:, :, :].rearrange("c q p -> q c p"), turned_sb[:, :, :]).then_inc(stored, 16)
            sp.wait_ge(stored, 16)
            sp.dma_start(row[:, :, :], scratch[:, :, :].rearrange("c q p -> c (q p)").unsqueeze(0)).then_inc(stored, 16)


def load_ranges(nc, table, engine, first, count, most):
    _, v = nc.values_load_multi_w_load_instructions(table[0:1, bass.ds(first * 2, 2 * count + 2)], engines=[engine],
                                                    min_val=0, max_val=most, skip_runtime_bounds_check_because=RANGES)
    return [x & ((1 << 20) - 1) for x in v[0::2]], v[1::2]


def split_three(step, nc, out, rest, x):
    step(nc.vector.memset(out[:, :, 3 * D:3 * D + 1], 1.0))
    step(nc.vector.tensor_copy(out[:, :, 0:D], x))
    step(nc.vector.tensor_tensor(rest, x, out[:, :, 0:D], ALU.subtract))
    step(nc.vector.tensor_copy(out[:, :, D:2 * D], rest))
    step(nc.vector.tensor_tensor(rest, rest, out[:, :, D:2 * D], ALU.subtract))
    step(nc.vector.tensor_copy(out[:, :, 2 * D:3 * D], rest))


def sum_over_sources(nc, turn, slabs, parts, first_two, third):
    PH = 7
    PIECES = HI // PH
    with Scope(nc, turn) as s:
        piece = [s.sb(f"piece{k}", [P, PH, SLAB], BF16) for k in range(PIECES)]
        sum2 = [s.ps(f"sum2_{b}", [P, SLAB]) for b in range(2)]
        sum1 = [s.ps(f"sum1_{b}", [D + 1, SLAB]) for b in range(2)]
        piece_in = [s.sem(f"piece_in{k}") for k in range(PIECES)]
        piece_used = s.sem("piece_used")
        copied2 = s.sem("copied2")
        copied1 = s.sem("copied1")
        block = s.block()

        @block.sync
        def _(sp):
            with sp.Fori(0, NSLAB) as n:
                for k in range(PIECES):
                    sp.wait_ge(piece_used, n * PIECES + k + 1)
                    sp.dma_start(piece[k][:, :, :].rearrange("p a b -> p (a b)"),
                                 slabs[bass.ds(n, 1), :, k * PH * SLAB:(k + 1) * PH * SLAB]
                                 .rearrange("a p c -> p (a c)")).then_inc(piece_in[k], 16)

        @block.tensor
        def _(pe):
            pe.sem_inc(piece_used, PIECES)
            pe.sem_inc(copied2, 2)
            pe.sem_inc(copied1, 2)
            with pe.Fori(0, NSLAB // 2) as i:
                for b in range(2):
                    pe.wait_ge(copied2, i * 2 + b + 1)
                    pe.wait_ge(copied1, i * 2 + b + 1)
                    for k in range(PIECES):
                        pe.wait_ge(piece_in[k], (i * 2 + b) * 16 + 16)
                        for j in range(PH):
                            hb = k * PH + j
                            ends = {"start": hb == 0, "stop": hb == HI - 1}
                            nc.tensor.matmul(sum2[b][:, :], parts[:, hb, 0:2 * D], piece[k][:, j, :], **ends)
                            last = nc.tensor.matmul(sum1[b][:, :], parts[:, hb, 2 * D:3 * D + 1], piece[k][:, j, :], **ends)
                        last.then_inc(piece_used, 1)

        @block.scalar
        def _(act):
            with act.Fori(0, NSLAB // 2) as i:
                for b in range(2):
                    act.wait_ge(piece_used, (i * 2 + b + 2) * PIECES)
                    nc.scalar.copy(first_two[:, bass.ds((i * 2 + b) * SLAB, SLAB)], sum2[b][:, :]).then_inc(copied2, 1)

        @block.vector
        def _(dve):
            with dve.Fori(0, NSLAB // 2) as i:
                for b in range(2):
                    dve.wait_ge(piece_used, (i * 2 + b + 2) * PIECES)
                    nc.vector.tensor_copy(third[:, bass.ds((i * 2 + b) * SLAB, SLAB)], sum1[b][:, :]
                                          ).then_inc(copied1, 1)


def wide(x, width=D):
    return x.unsqueeze(2).broadcast_to([P, x.shape[1], width])


def layer_norm_relu(step, nc, act_sqrt, g, out, tmp, col):
    x = g["x"][:, :, :]
    mean, var = col[:, 0, :], col[:, 1, :]
    step(nc.vector.tensor_reduce(mean, x, AX_X, ALU.add))
    step(nc.vector.tensor_scalar(mean, mean, 1.0 / D, None, ALU.mult))
    step(nc.vector.tensor_tensor(out[:, :, :], x, wide(mean), ALU.subtract))
    step(nc.vector.tensor_tensor(tmp[:, :, :], out[:, :, :], out[:, :, :], ALU.mult))
    step(nc.vector.tensor_reduce(var, tmp[:, :, :], AX_X, ALU.add))
    step(nc.vector.tensor_scalar(var, var, 1.0 / D, 1e-5, ALU.mult, ALU.add))
    act_sqrt()
    step(nc.vector.reciprocal(var, var))
    step(nc.vector.scalar_tensor_tensor(out[:, :, :], out[:, :, :], 0.0, wide(var), ALU.max, ALU.mult))


def edge_statistics_layer(nc, g, scanned, carries, x_in, u, w1, b1, w2, b2):
    NF = 3 * DA
    with Scope(nc) as s:
        ends = s.sb("ends", [P, HI, 2 * DA], F32)
        carry_in = s.sb("run_carry", [P, HI, 2 * DA], F32)
        feats = s.sb("feats", [P, HI, NF], F32)
        feats_t = s.sb("feats_t", [NF, HI * P], F32)
        hidden = s.sb("hidden", [HID, HI * P], F32)
        off = s.sb("off", [P, HI], F32)
        inv = s.sb("inv", [P, HI], F32)
        w1_sb = s.sb("w1_sb", [NF, HID], F32)
        w2_sb = s.sb("w2_sb", [HID, D], F32)
        w1_u = s.sb("w1_u", [HID, 1], F32)
        u_col = s.sb("u_col", [HID, 1], F32)
        bias = s.sb("bias", [HID, 1], F32)
        b2_row = s.sb("b2_row", [P, D], F32)
        turned = [s.ps(f"feats_turned{b}", [NF, 4, P]) for b in range(2)]
        ps_hidden = [s.ps(f"ps_hidden{b}", [HID, 512]) for b in range(2)]
        ps_out = [s.ps(f"ps_out{b}", [P, 8, D]) for b in range(2)]
        loaded = s.sem("loaded")
        gathered = s.sem("gathered")
        dve_step = s.sem("dve_step")
        bias_ready = s.sem("bias_ready")
        feats_ready = s.sem("feats_ready")
        turned_ready = s.sem("turned_ready")
        turned_copied = s.sem("turned_copied")
        hidden_ready = s.sem("hidden_ready")
        hidden_copied = s.sem("hidden_copied")
        out_ready = s.sem("out_ready")
        added = s.sem("added")
        block = s.block()
        CH = -(-HI // 4)
        OC = -(-HI // 8)
        x, full = g["x"], (N // P) * P

        @block.sync
        def _(sp):
            sp.dma_start(w1_sb[:, :], w1[0:NF, :]).then_inc(loaded, 16)
            sp.dma_start(w1_u[:, :], w1[NF:NF + 1, :].rearrange("a h -> h a")).then_inc(loaded, 16)
            sp.dma_start(u_col[:, :], u[0:1, 0:1].broadcast_to([HID, 1])).then_inc(loaded, 16)
            sp.dma_start(bias[:, :], b1.unsqueeze(1)).then_inc(loaded, 16)
            sp.dma_start(w2_sb[:, :], w2).then_inc(loaded, 16)
            sp.dma_start(b2_row[:, :], b2.unsqueeze(0).broadcast_to([P, D])).then_inc(loaded, 16)
            sp.wait_ge(dve_step, 1)
            sp.dma_start(x[:, 0:N // P, :], x_in[0:full, :].rearrange("(b p) f -> p b f", p=P)).then_inc(loaded, 16)
            sp.dma_start(x[0:N - full, N // P, :], x_in[full:N, :]).then_inc(loaded, 16)

        @block.gpsimd
        def _(pool):
            gather_runs(nc, pool, g, scanned, carries, ends, carry_in, gathered)

        @block.vector
        def _(dve):
            step = Serial(dve, dve_step)
            step(nc.vector.memset(x[:, N // P, :], 0.0))
            step(nc.vector.tensor_scalar(off[:, :], g["spans"][:, :], -1.0, HUGE, ALU.add, ALU.mult))
            step(nc.vector.tensor_scalar(inv[:, :], g["out_deg"][:, 0:HI], 1.0, None, ALU.max))
            step(nc.vector.reciprocal(inv[:, :], inv[:, :]))
            dve.wait_ge(loaded, 8 * 16)
            nc.vector.scalar_tensor_tensor(bias[:, :], w1_u[:, :], u_col[:, 0:1], bias[:, :], ALU.mult,
                                           ALU.add).then_inc(bias_ready, 1)
            step(nc.vector.tensor_tensor(x[:, :, :], x[:, :, :], b2_row[:, :].unsqueeze(1).broadcast_to([P, HI, D]),
                                         ALU.add))
            dve.wait_ge(gathered, 16 * 2 * HI)
            total, most, mean = (feats[:, :, c * DA:(c + 1) * DA] for c in range(3))
            step(nc.vector.tensor_tensor(carry_in[:, :, :], carry_in[:, :, :], wide(g["spans"][:, :]), ALU.mult))
            step(nc.vector.tensor_tensor(total, ends[:, :, DA:], carry_in[:, :, DA:], ALU.add))
            step(nc.vector.tensor_tensor(total, total, wide(g["has_out"][:, :], DA), ALU.mult))
            step(nc.vector.tensor_tensor(mean, total, wide(inv[:, :], DA), ALU.mult))
            step(nc.vector.tensor_tensor(most, carry_in[:, :, 0:DA], wide(off[:, :], DA), ALU.add))
            step(nc.vector.tensor_tensor(most, most, ends[:, :, 0:DA], ALU.max))
            nc.vector.tensor_tensor(most, most, wide(g["has_out"][:, :], DA), ALU.mult).then_inc(feats_ready, 1)
            for c in range(OC):
                n = min(8, HI - 8 * c)
                dve.wait_ge(out_ready, c + 1)
                nc.vector.tensor_tensor(x[:, 8 * c:8 * c + n, :], x[:, 8 * c:8 * c + n, :], ps_out[c % 2][:, 0:n, :],
                                        ALU.add).then_inc(added, 1)

        @block.scalar
        def _(act):
            act.wait_ge(bias_ready, 1)
            for c in range(CH):
                n = min(4, HI - 4 * c)
                act.wait_ge(turned_ready, c + 1)
                nc.scalar.copy(feats_t[:, c * 512:c * 512 + n * P].rearrange("p (a b) -> p a b", b=P),
                               turned[c % 2][:, 0:n, :]).then_inc(turned_copied, 1)
                act.wait_ge(hidden_ready, c + 1)
                nc.scalar.activation(hidden[:, c * 512:c * 512 + n * P], ps_hidden[c % 2][:, 0:n * P], ACT.Relu,
                                     bias=bias[:, 0:1]).then_inc(hidden_copied, 1)

        @block.tensor
        def _(pe):
            pe.wait_ge(feats_ready, 1)
            for c in range(CH):
                n = min(4, HI - 4 * c)
                if c >= 2:
                    pe.wait_ge(turned_copied, c - 1)
                for a in range(n):
                    last = nc.tensor.transpose(turned[c % 2][:, a, :], feats[:, 4 * c + a, :], g["ident"][:, :])
                last.then_inc(turned_ready, 1)
                pe.wait_ge(turned_copied, c + 1)
                if c >= 2:
                    pe.wait_ge(hidden_copied, c - 1)
                nc.tensor.matmul(ps_hidden[c % 2][:, 0:n * P], w1_sb[:, :], feats_t[:, c * 512:c * 512 + n * P],
                                 start=True, stop=True).then_inc(hidden_ready, 1)
            for c in range(OC):
                n = min(8, HI - 8 * c)
                pe.wait_ge(hidden_copied, min(CH, 2 * c + 2))
                if c >= 2:
                    pe.wait_ge(added, c - 1)
                for a in range(n):
                    b = 8 * c + a
                    last = nc.tensor.matmul(ps_out[c % 2][:, a, :], hidden[:, b * P:(b + 1) * P], w2_sb[:, :],
                                            start=True, stop=True)
                last.then_inc(out_ready, 1)


def kept(nc, ctx, g):
    for name, shape, dt in (
        ("ident", [P, P], F32), ("identb", [P, P], BF16), ("below", [P, P], F32), ("belowb", [P, P], BF16),
        ("ones", [P, P], F32), ("zerob", [P, 512], BF16), ("iota", [P, 512], FP16), ("rowid", [P, 1], F32),
        ("rowid_i", [P, 1], I32), ("dkey", [EP, NT], F32),
        ("span", [P, 2, TB], F32), ("out_deg", [P, NB], F32), ("start", [P, NB], F32),
        ("same_src", [EP, NT], F32), ("dst_sorted", [EP, NT], I32), ("w_sorted", [EP, NT], F32),
        ("end_i", [P, HI], I32), ("end_part_i", [P, HI], I32), ("has_out", [P, HI], F32), ("spans", [P, HI], F32),
        ("x", [P, HI, D], F32), ("win_table", [1, 2 * NWIN + 2], I32), ("blk_table", [1, 2 * NB + 2], I32),
        ("keep_run", [D, EP], F32),
    ):
        g[name] = ctx.enter_context(nc.sbuf_tensor(name, shape, dt))


def kept_to_rank(nc, ctx, g):
    for name, shape, dt in (("winbase", [P, NWIN], F32), ("mkeys", [EP, TPAD], F32), ("lo_tiles", [EP, TPAD], BF16),
                            ("sdw", [EP, NT, 3], F32), ("lo", [EP, NT + RG], FP16), ("hi", [EP, NT + RG], FP16),
                            ("iota_rg", [P, P, RG], FP16)):
        g[name] = ctx.enter_context(nc.sbuf_tensor(name, shape, dt))


def normalise(nc, g, turn, h, parts=None, by_degree=None):
    with Scope(nc, turn) as s:
        tmp = s.sb("norm_tmp", [P, HI, D], F32)
        scaled = s.sb("norm_scaled", [P, HI, D], F32)
        col = s.sb("norm_col", [P, 2, HI], F32)
        dve_step = s.sem("dve_step")
        var_ready = s.sem("var_ready")
        root_ready = s.sem("root_ready")
        block = s.block()

        @block.vector
        def _(dve):
            step = Serial(dve, dve_step)

            def roots():
                dve.sem_inc(var_ready, 1)
                dve.wait_ge(root_ready, 1)

            if by_degree is not None:
                step(nc.vector.tensor_scalar(by_degree[:, :], g["out_deg"][:, 0:HI], 1.0, None, ALU.add))
            layer_norm_relu(step, nc, roots, g, h, tmp, col)
            if by_degree is not None:
                step(nc.vector.reciprocal(by_degree[:, :], by_degree[:, :]))
                step(nc.vector.tensor_tensor(scaled[:, :, :], h[:, :, :], wide(by_degree[:, :]), ALU.mult))
                split_three(step, nc, parts, tmp[:, :, :], scaled[:, :, :])
            elif parts is not None:
                split_three(step, nc, parts, tmp[:, :, :], h[:, :, :])

        @block.scalar
        def _(act):
            act.wait_ge(var_ready, 1)
            if by_degree is not None:
                nc.scalar.activation(by_degree[:, :], by_degree[:, :], ACT.Sqrt)
            nc.scalar.activation(col[:, 1, :], col[:, 1, :], ACT.Sqrt).then_inc(root_ready, 1)


def convolution_layer(nc, g, slabs, w, b):
    CH = -(-HI // 4)
    with Scope(nc) as keep:
        h = keep.sb("conv_h", [P, HI, D], F32)
        parts = keep.sb("conv_parts", [P, HI, 3 * D + 1], BF16)
        rs = keep.sb("conv_rs", [P, HI], F32)
        normalise(nc, g, "_conv", h, parts, rs)
        first_two = keep.sb("conv_first_two", [P, NPAD], F32)
        third = keep.sb("conv_third", [D + 1, NPAD], F32)
        sum_over_sources(nc, "_conv", slabs, parts, first_two, third)
        with Scope(nc) as s:
            w_ab = s.sb("w_ab", [D, 2 * D], F32)
            w_b2 = s.sb("w_b2", [P, D + 1], F32)
            w_b1 = s.sb("w_b1", [D + 1, D + 1], F32)
            deg = s.sb("conv_deg", [P, 2, 4], F32)
            factor = s.sb("conv_factor", [P, 2, 4], F32)
            b_row = s.sb("conv_b_row", [P, D], F32)
            ht = s.sb("conv_ht", [D, 2, 512], F32)
            mix = s.sb("conv_mix", [P, 4, D], F32)
            turned = [s.ps(f"conv_turned{k}", [D, 512]) for k in range(2)]
            own = [s.ps(f"conv_own{k}", [P, 4, 2 * D]) for k in range(2)]
            summed = [s.ps(f"conv_summed{k}", [P, 4, D + 1]) for k in range(2)]
            loaded = s.sem("loaded")
            turned_ready = s.sem("turned_ready")
            turned_copied = s.sem("turned_copied")
            ready = s.sem("products_ready")
            cleared = s.sem("cleared")
            deg_ready = s.sem("deg_ready")
            root_ready = s.sem("root_ready")
            added = s.sem("added")
            dve_step = s.sem("dve_step")
            block = s.block()
            x = g["x"]

            @block.sync
            def _(sp):
                sp.dma_start(w_ab[:, 0:D], w[0:D, :]).then_inc(loaded, 16)
                sp.dma_start(w_ab[:, D:2 * D], w[D:2 * D, :]).then_inc(loaded, 16)
                sp.wait_ge(cleared, 4)
                sp.dma_start(w_b2[0:D, 0:D], w[D:2 * D, :]).then_inc(loaded, 16)
                sp.dma_start(w_b2[D:2 * D, 0:D], w[D:2 * D, :]).then_inc(loaded, 16)
                sp.dma_start(w_b1[0:D, 0:D], w[D:2 * D, :]).then_inc(loaded, 16)
                sp.dma_start(b_row[:, :], b.unsqueeze(0).broadcast_to([P, D])).then_inc(loaded, 16)

            @block.tensor
            def _(pe):
                def turn(c):
                    if c >= 2:
                        pe.wait_ge(turned_copied, c - 1)
                    for a in range(min(4, HI - 4 * c)):
                        last = nc.tensor.transpose(turned[c % 2][:, a * P:(a + 1) * P], h[:, 4 * c + a, :],
                                                   g["ident"][:, :])
                    last.then_inc(turned_ready, 1)

                turn(0)
                pe.wait_ge(loaded, 6 * 16)
                for c in range(CH):
                    if c + 1 < CH:
                        turn(c + 1)
                    pe.wait_ge(turned_copied, c + 1)
                    if c >= 2:
                        pe.wait_ge(added, c - 1)
                    for a in range(min(4, HI - 4 * c)):
                        nodes = slice((4 * c + a) * P, (4 * c + a + 1) * P)
                        nc.tensor.matmul(own[c % 2][:, a, :], ht[:, c % 2, a * P:(a + 1) * P], w_ab[:, :],
                                         start=True, stop=True)
                        nc.tensor.matmul(summed[c % 2][:, a, :], first_two[:, nodes], w_b2[:, :], start=True,
                                         stop=False)
                        last = nc.tensor.matmul(summed[c % 2][:, a, :], third[:, nodes], w_b1[:, :],
                                                start=False, stop=True)
                    last.then_inc(ready, 1)

            @block.scalar
            def _(act):
                def copy(c):
                    n = min(4, HI - 4 * c) * P
                    act.wait_ge(turned_ready, c + 1)
                    if c >= 2:
                        act.wait_ge(ready, c - 1)
                    nc.scalar.copy(ht[:, c % 2, 0:n], turned[c % 2][:, 0:n]).then_inc(turned_copied, 1)

                copy(0)
                for c in range(CH):
                    if c + 1 < CH:
                        copy(c + 1)
                    n = min(4, HI - 4 * c)
                    act.wait_ge(deg_ready, c + 1)
                    nc.scalar.activation(factor[:, c % 2, 0:n], deg[:, c % 2, 0:n], ACT.Sqrt).then_inc(root_ready, 1)

            @block.vector
            def _(dve):
                step = Serial(dve, dve_step)
                nc.vector.memset(w_b2[:, D:D + 1], 0.0).then_inc(cleared, 1)
                nc.vector.memset(w_b1[0:D, D:D + 1], 0.0).then_inc(cleared, 1)
                nc.vector.memset(w_b1[D:D + 1, 0:D], 0.0).then_inc(cleared, 1)
                nc.vector.memset(w_b1[D:D + 1, D:D + 1], 1.0).then_inc(cleared, 1)
                dve.wait_ge(loaded, 6 * 16)
                step(nc.vector.tensor_tensor(x[:, :, :], x[:, :, :], b_row[:, :].unsqueeze(1).broadcast_to([P, HI, D]),
                                             ALU.add))
                for c in range(CH):
                    n = min(4, HI - 4 * c)
                    blocks = slice(4 * c, 4 * c + n)
                    m = mix[:, 0:n, :]
                    dve.wait_ge(ready, c + 1)
                    d, f = deg[:, c % 2, 0:n], factor[:, c % 2, 0:n]
                    nc.vector.tensor_scalar(d, summed[c % 2][:, 0:n, D], 1.0, None, ALU.add).then_inc(deg_ready, 1)
                    step(nc.vector.tensor_tensor(m, own[c % 2][:, 0:n, D:2 * D], wide(rs[:, blocks]), ALU.mult))
                    step(nc.vector.tensor_tensor(m, m, summed[c % 2][:, 0:n, 0:D], ALU.add))
                    dve.wait_ge(root_ready, c + 1)
                    step(nc.vector.tensor_tensor(f, f, d, ALU.mult))
                    step(nc.vector.reciprocal(f, f))
                    step(nc.vector.tensor_tensor(m, m, wide(f), ALU.mult))
                    nc.vector.tensor_tensor(m, m, own[c % 2][:, 0:n, 0:D], ALU.add).then_inc(added, 1)
                    dve.wait_ge(added, c + 1)
                    step(nc.vector.tensor_tensor(x[:, blocks, :], x[:, blocks, :], m, ALU.add))


def scan_messages(nc, g, table, scanned, carries, edge_attr_64):
    MOST = NB * NT
    HALF = HGRP // 2
    J = NT // NB
    STEPS = NT // J
    with Scope(nc) as s:
        index = [s.sb(f"gather_index{b}", [EP, J], I32) for b in range(2)]
        got = [s.sb(f"gathered_rows{b}", [EP, J, D], F32) for b in range(2)]
        out = [s.sb(f"message_sums{b}", [EP, J, D], F32) for b in range(2)]
        carry = s.sb("sum_carry", [EP, D], F32)
        state = s.sb("sum_state", [D, EP], F32)
        turned_carry = s.sb("sum_turned_carry", [D, EP], F32)
        carry_in = s.sb("sum_carry_in", [EP, D], F32)
        attr = [s.sb(f"attr_half{b}", [EP, HALF, D + 1], F32) for b in range(2)]
        keys = s.sb("block_keys", [EP, HGRP], F32)
        hot = s.sb("block_hot", [EP, HGRP, P], F32)
        base = s.sb("block_base", [P, NB], F32)
        iota_f = s.sb("iota_f", [P, P], F32)
        total = [s.ps(f"block_total{b}", [P, D + 1]) for b in range(2)]
        ps_carry = s.ps("ps_sum_carry", [D, EP])
        ps_in = s.ps("ps_sum_in", [EP, D])
        index_ready = s.sem("index_ready")
        gathered = [s.sem(f"gathered{b}") for b in range(2)]
        weighted = s.sem("weighted")
        scans_done = s.sem("scans_done")
        carry_ready = s.sem("carry_ready")
        sums_out = [s.sem(f"sums_out{b}") for b in range(2)]
        pool_turns = s.sem("pool_turns")
        dve_step = s.sem("dve_step")
        pe_done = s.sem("pe_done")
        carried = s.sem("carried")
        consts = s.sem("block_consts")
        attr_in = [s.sem(f"attr_in{b}") for b in range(2)]
        keys_ready = s.sem("keys_ready")
        made = s.sem("made")
        used = s.sem("used")
        copied = s.sem("copied")
        block = s.block()
        dst_v = scanned[:, :].rearrange("(p j) c -> p (j c)", p=EP)
        attr_rows = edge_attr_64.rearrange("(t e) f -> e t f", e=EP)

        @block.gpsimd
        def _(pool):
            pool.sem_inc(scans_done, 2)
            with pool.Fori(0, STEPS // 2) as i:
                for b in range(2):
                    pool.wait_ge(scans_done, 2 * i + b + 1)
                    pool.tensor_copy(index[b][:, :], g["dst_sorted"][:, bass.ds((2 * i + b) * J, J)]
                                     ).then_inc(index_ready, 1)
                    pool.wait_ge(index_ready, 2 * i + b + 1)
                    pool.sem_inc(pool_turns, 1)
                    for j in range(J):
                        pool.indirect_dma_start(got[b][:, j, :], None, table[:, :],
                                                bass.IndirectOffsetOnAxis(ap=index[b][:, j:j + 1], axis=0)
                                                ).then_inc(gathered[b], 16)

        @block.scalar
        def _(act):
            with act.Fori(0, STEPS // 2) as i:
                before, _ = load_ranges(nc, g["blk_table"], ACTE, i * 2, 2, MOST)
                for b in range(2):
                    act.wait_ge(used, before[b + 1] * HGRP + HGRP)
                    nc.scalar.copy(g["attr_sum"][:, bass.ds((i * 2 + b) * (D + 1), D + 1)], total[b][:, :]
                                   ).then_inc(copied, 1)

        @block.vector
        def _(dve):
            for b in range(2):
                nc.vector.memset(attr[b][:, :, D:D + 1], 1.0).then_inc(consts, 1)
            nc.vector.tensor_copy(iota_f[:, :], g["iota"][:, 0:P]).then_inc(consts, 1)
            nc.vector.tensor_scalar(base[:, :], g["iota"][:, 0:NB], float(P), None, ALU.mult).then_inc(consts, 1)
            nc.vector.memset(carry[:, :], 0.0).then_inc(carry_ready, 1)
            dve.wait_ge(consts, 4)
            dve.sem_inc(made, HGRP)
            with dve.Fori(0, STEPS // 2) as i:
                before, offset = load_ranges(nc, g["blk_table"], DVE, i * 2, 2, MOST)
                for b in range(2):
                    with dve.Fori(before[b], before[b + 1]) as v:
                        t = nc.s_assert_within(v * HGRP - offset[b], 0, NT - HGRP,
                                               skip_runtime_bounds_check_because=RANGES)
                        dve.wait_ge(made, v * HGRP + HGRP)
                        nc.vector.tensor_scalar(keys[:, :], g["dkey"][:, bass.ds(t, HGRP)],
                                                base[0:EP, bass.ds(i * 2 + b, 1)], None,
                                                ALU.subtract).then_inc(keys_ready, 1)
                        dve.wait_ge(keys_ready, v + 1)
                        for j in range(HGRP):
                            dve.wait_ge(used, v * HGRP + j + 1)
                            nc.vector.tensor_scalar(hot[:, j, :], iota_f[0:EP, :], keys[:, j:j + 1], None,
                                                    ALU.is_equal).then_inc(made, 1)
                    n = 2 * i + b
                    dve.wait_ge(gathered[b], 16 * J * (i + 1))
                    w = g["w_sorted"][:, bass.ds(n * J, J)]
                    nc.vector.tensor_tensor(got[b][:, :, :], got[b][:, :, :], w.unsqueeze(2).broadcast_to([EP, J, D]),
                                            ALU.mult).then_inc(weighted, 1)
                    dve.wait_ge(weighted, n + 1)
                    dve.wait_ge(carry_ready, n + 1)
                    dve.wait_ge(sums_out[b], 32 * i + 1)
                    for f in range(D):
                        last = nc.vector.tensor_tensor_scan(out[b][:, :, f], g["same_src"][:, bass.ds(n * J, J)],
                                                            got[b][:, :, f], carry[:, f:f + 1], ALU.mult, ALU.add)
                    last.then_inc(scans_done, 1)
                    dve.wait_ge(scans_done, n + 3)
                    nc.vector.tensor_copy(carry[:, :], out[b][:, J - 1, :]).then_inc(carry_ready, 1)
            step = Serial(dve, dve_step)
            dve.wait_ge(pe_done, 1)
            step(nc.vector.tensor_copy(turned_carry[:, :], ps_carry[:, :]))
            step(nc.vector.memset(state[:, 0:1], 0.0))
            step(nc.vector.tensor_tensor_scan(state[:, 1:EP], g["keep_run"][:, 0:EP - 1], turned_carry[:, 0:EP - 1],
                                              0.0, ALU.mult, ALU.add))
            dve.wait_ge(pe_done, 2)
            nc.vector.tensor_copy(carry_in[:, :], ps_in[:, :]).then_inc(carried, 1)

        @block.tensor
        def _(pe):
            pe.sem_inc(used, HGRP)
            pe.sem_inc(copied, 2)
            with pe.Fori(0, STEPS // 2) as i:
                before, _ = load_ranges(nc, g["blk_table"], PE, i * 2, 2, MOST)
                for b in range(2):
                    pe.wait_ge(copied, i * 2 + b + 1)
                    nc.tensor.matmul(total[b][:, :], g["zerob"][0:EP, 0:P], g["zerob"][0:EP, 0:D + 1], start=True,
                                     stop=True)
                    with pe.Fori(before[b], before[b + 1]) as v:
                        for j in range(HGRP):
                            if j % HALF == 0:
                                pe.wait_ge(attr_in[j // HALF], v * 16 + 16)
                            pe.wait_ge(made, v * HGRP + HGRP + j + 1)
                            nc.tensor.matmul(total[b][:, :], hot[:, j, :], attr[j // HALF][:, j % HALF, :],
                                             start=False, stop=True, skip_group_check=True).then_inc(used, 1)
            pe.wait_ge(carry_ready, STEPS + 1)
            nc.tensor.transpose(ps_carry[:, :], carry[:, :], g["ident"][0:EP, 0:EP]).then_inc(pe_done, 1)
            pe.wait_ge(dve_step, 3)
            nc.tensor.transpose(ps_in[:, :], state[:, :], g["ident"][0:D, 0:D]).then_inc(pe_done, 1)

        @block.sync
        def _(sp):
            for b in range(2):
                sp.sem_inc(sums_out[b], 1)
            sp.wait_ge(consts, 2)
            with sp.Fori(0, STEPS // 2) as i:
                before, offset = load_ranges(nc, g["blk_table"], SPE, i * 2, 2, MOST)
                for b in range(2):
                    n = 2 * i + b
                    with sp.Fori(before[b], before[b + 1]) as v:
                        t = nc.s_assert_within(v * HGRP - offset[b], 0, NT - HGRP,
                                               skip_runtime_bounds_check_because=RANGES)
                        for k in range(2):
                            sp.wait_ge(used, v * HGRP + (k + 1) * HALF)
                            sp.dma_start(attr[k][:, :, 0:D], attr_rows[:, bass.ds(t + k * HALF, HALF), :]
                                         ).then_inc(attr_in[k], 16)
                    sp.wait_ge(scans_done, n + 3)
                    two_parts(sp, dst_v[:, bass.ds(n * J * D, J * D)], out[b][:, :, :].rearrange("p j f -> p (j f)"),
                              sums_out[b])
            for b in range(2):
                sp.wait_ge(sums_out[b], 16 * STEPS + 1)
            sp.wait_ge(carried, 1)
            sp.dma_start(carries[:, :], carry_in[:, :]).then_inc(sums_out[0], 16)
            sp.wait_ge(sums_out[0], 16 * STEPS + 17)


def weighted_layer(nc, g, table, scanned, carries, eps, edge_attr_64):
    with Scope(nc) as keep:
        h = keep.sb("weighted_h", [P, HI, D], F32)
        normalise(nc, g, "_weighted", h)
        with Scope(nc) as s:
            stored = s.sem("table_stored")
            block = s.block()

            @block.sync
            def _(sp):
                sp.dma_start(table[:, :].rearrange("(b p) f -> p b f", p=P), h[:, :, :]).then_inc(stored, 16)
                sp.wait_ge(stored, 16)

        scan_messages(nc, g, table, scanned, carries, edge_attr_64)
        with Scope(nc) as s:
            ends = s.sb("message_ends", [P, HI, D], F32)
            carry_in = s.sb("message_carry", [P, HI, D], F32)
            factor = s.sb("one_eps", [P, 1], F32)
            loaded = s.sem("loaded")
            gathered = s.sem("gathered")
            dve_step = s.sem("dve_step")
            block = s.block()
            x = g["x"]

            @block.sync
            def _(sp):
                sp.dma_start(factor[:, :], eps.unsqueeze(0).broadcast_to([P, 1])).then_inc(loaded, 16)

            @block.gpsimd
            def _(pool):
                gather_runs(nc, pool, g, scanned, carries, ends, carry_in, gathered)

            @block.vector
            def _(dve):
                step = Serial(dve, dve_step)
                dve.wait_ge(loaded, 16)
                step(nc.vector.tensor_scalar(factor[:, :], factor[:, :], 1.0, None, ALU.add))
                step(nc.vector.scalar_tensor_tensor(x[:, :, :], h[:, :, :], factor[:, 0:1], x[:, :, :], ALU.mult,
                                                    ALU.add))
                dve.wait_ge(gathered, 16 * 2 * HI)
                step(nc.vector.tensor_tensor(carry_in[:, :, :], carry_in[:, :, :], wide(g["spans"][:, :]), ALU.mult))
                step(nc.vector.tensor_tensor(ends[:, :, :], ends[:, :, :], carry_in[:, :, :], ALU.add))
                step(nc.vector.tensor_tensor(ends[:, :, :], ends[:, :, :], wide(g["has_out"][:, :]), ALU.mult))
                step(nc.vector.tensor_tensor(x[:, :, :], x[:, :, :], ends[:, :, :], ALU.add))


def split_features(nc, parts, h):
    with Scope(nc) as s:
        rest = s.sb("split_rest", [P, HI, D], F32)
        dve_step = s.sem("dve_step")
        block = s.block()

        @block.vector
        def _(dve):
            split_three(Serial(dve, dve_step), nc, parts, rest[:, :, :], h[:, :, :])


def turn_weights(nc, g, t, w_msg, b_msg, w_ih, w_hh, b_ih, b_hh, wd, ws2, we, w_in, w_hid):
    with Scope(nc, f"_round{t}") as s:
        msg = s.sb("msg_nat", [P, 4 * D + 1], F32)
        inp = s.sb("in_nat", [P, 2, P], F32)
        hid = s.sb("hid_nat", [P, 3, D + 1], F32)
        bias = s.sb("hid_bias", [P, 1], F32)
        turned = [s.ps(f"weights_turned{k}", [P, 2, P]) for k in range(4)]
        cleared = s.sem("cleared")
        loaded = s.sem("loaded")
        nat_ready = s.sem("nat_ready")
        turned_ready = s.sem("turned_ready")
        copied = s.sem("copied")
        block = s.block()
        G = 2 * D

        @block.sync
        def _(sp):
            sp.dma_start(msg[:, 0:2 * D], w_msg[t, :, 0:2 * D]).then_inc(loaded, 16)
            sp.dma_start(msg[:, 2 * D:4 * D], w_msg[t, :, D:3 * D]).then_inc(loaded, 16)
            sp.dma_start(msg[:, 4 * D:4 * D + 1], b_msg[t, :].unsqueeze(1)).then_inc(loaded, 16)
            sp.dma_start(inp[:, 0, :], w_ih[t, 0:G, :]).then_inc(loaded, 16)
            sp.dma_start(inp[0:D, 1, :], w_ih[t, G:3 * D, :]).then_inc(loaded, 16)
            sp.dma_start(hid[:, 0, 0:D], w_hh[t, 0:G, :]).then_inc(loaded, 16)
            sp.dma_start(hid[:, 0, D:D + 1], b_hh[t, 0:G].unsqueeze(1)).then_inc(loaded, 16)
            sp.dma_start(bias[:, :], b_ih[t, 0:G].unsqueeze(1)).then_inc(loaded, 16)
            sp.dma_start(hid[0:D, 2, 0:D], w_hh[t, G:3 * D, :]).then_inc(loaded, 16)
            sp.dma_start(hid[0:D, 2, D:D + 1], b_hh[t, G:3 * D].unsqueeze(1)).then_inc(loaded, 16)
            sp.wait_ge(cleared, 1)
            sp.dma_start(hid[0:D, 1, D:D + 1], b_ih[t, G:3 * D].unsqueeze(1)).then_inc(loaded, 16)

        @block.vector
        def _(dve):
            nc.vector.memset(hid[:, 1, :], 0.0).then_inc(cleared, 1)
            dve.wait_ge(loaded, 11 * 16)
            nc.vector.tensor_tensor(hid[:, 0, D:D + 1], hid[:, 0, D:D + 1], bias[:, :], ALU.add).then_inc(nat_ready, 1)
            dve.wait_ge(turned_ready, 1)
            nc.vector.tensor_copy(wd[:, :], turned[0][0:D, 0, :])
            nc.vector.tensor_copy(ws2[:, :], turned[0][:, 1, :])
            nc.vector.tensor_copy(we[:, :], turned[1][0:D + 1, 0, :])
            nc.vector.tensor_copy(w_in[:, 0:G], turned[1][:, 1, :])
            nc.vector.tensor_copy(w_in[:, G:3 * D], turned[2][:, 0, 0:D])
            nc.vector.tensor_copy(w_hid[:, 0:G], turned[2][0:D + 1, 1, :])
            nc.vector.tensor_copy(w_hid[:, G:3 * D], turned[3][0:D + 1, 0, 0:D])
            nc.vector.tensor_copy(w_hid[:, 3 * D:4 * D], turned[3][0:D + 1, 1, 0:D]).then_inc(copied, 1)

        @block.tensor
        def _(pe):
            pe.wait_ge(nat_ready, 1)
            ident, half = g["ident"][:, :], g["ident"][0:D, 0:D]
            nc.tensor.transpose(turned[0][0:D, 0, :], msg[:, 0:D], ident)
            nc.tensor.transpose(turned[0][:, 1, :], msg[:, D:3 * D], ident)
            nc.tensor.transpose(turned[1][0:D + 1, 0, :], msg[:, 3 * D:4 * D + 1], ident)
            nc.tensor.transpose(turned[1][:, 1, :], inp[:, 0, :], ident)
            nc.tensor.transpose(turned[2][:, 0, 0:D], inp[0:D, 1, :], half)
            nc.tensor.transpose(turned[2][0:D + 1, 1, :], hid[:, 0, :], ident)
            nc.tensor.transpose(turned[3][0:D + 1, 0, 0:D], hid[0:D, 1, :], half)
            nc.tensor.transpose(turned[3][0:D + 1, 1, 0:D], hid[0:D, 2, :], half).then_inc(turned_ready, 1)


def gated_update(nc, g, t, h, first_two, third, wd, ws2, we, w_in, w_hid):
    CH = -(-HI // 4)
    PAIRS = -(-HI // 2)
    with Scope(nc, f"_round{t}") as s:
        scaled = s.sb("scaled_h", [P, 2, 4, D], F32)
        ht = s.sb("gru_ht", [D + 1, 2, 512], F32)
        ct = s.sb("gru_ct", [D, 2, 512], F32)
        et = s.sb("gru_et", [D + 1, 2, 512], F32)
        at = s.sb("gru_at", [P, 2, 512], F32)
        rz = s.sb("gru_rz", [P, 2, 2, 2 * D], F32)
        new = s.sb("gru_new", [P, 2, 2, D], F32)
        diff = s.sb("gru_diff", [P, 2, D], F32)
        ps_h = s.ps("ps_ht", [D, 4, P])
        ps_c = s.ps("ps_ct", [D, 4, P])
        ps_e = s.ps("ps_et", [D + 1, 4, P])
        ps_a = s.ps("ps_at", [P, 512])
        gates = [s.ps(f"ps_gates{k}", [P, 2, 4 * D]) for k in range(4)]
        scaled_ready = s.sem("scaled_ready")
        turned_ready = s.sem("turned_ready")
        copied_act = s.sem("copied_act")
        copied_dve = s.sem("copied_dve")
        sum_ready = s.sem("sum_ready")
        sum_copied = s.sem("sum_copied")
        gates_ready = s.sem("gates_ready")
        rz_ready = s.sem("rz_ready")
        pre_ready = s.sem("pre_ready")
        new_ready = s.sem("new_ready")
        updated = s.sem("updated")
        dve_step = s.sem("dve_step")
        ones_ready = s.sem("ones_ready")
        block = s.block()

        def blocks(c):
            return min(4, HI - 4 * c)

        def pairs(c):
            return range(2 * c, min(2 * c + 2, PAIRS))

        def paired(p):
            return min(2, HI - 2 * p)

        @block.tensor
        def _(pe):
            def turn(c):
                pe.wait_ge(scaled_ready, c + 1)
                if c:
                    pe.wait_ge(copied_act, c)
                    pe.wait_ge(copied_dve, c)
                for a in range(blocks(c)):
                    b = 4 * c + a
                    nc.tensor.transpose(ps_h[:, a, :], h[:, b, :], g["ident"][:, :])
                    nc.tensor.transpose(ps_e[:, a, :], g["attr_sum"][:, b * (D + 1):(b + 1) * (D + 1)],
                                        g["ident"][:, :])
                    last = nc.tensor.transpose(ps_c[:, a, :], scaled[:, c % 2, a, :], g["ident"][:, :])
                last.then_inc(turned_ready, 1)

            turn(0)
            pe.wait_ge(ones_ready, 1)
            for c in range(CH):
                if c + 1 < CH:
                    turn(c + 1)
                n = blocks(c) * P
                nodes = slice(c * 512, c * 512 + n)
                pe.wait_ge(copied_act, c + 1)
                pe.wait_ge(copied_dve, c + 1)
                if c:
                    pe.wait_ge(sum_copied, c)
                nc.tensor.matmul(ps_a[:, 0:n], wd[:, :], ct[:, c % 2, 0:n], start=True, stop=False)
                nc.tensor.matmul(ps_a[:, 0:n], ws2[:, :], first_two[:, nodes], start=False, stop=False)
                nc.tensor.matmul(ps_a[:, 0:n], ws2[0:D, :], third[0:D, nodes], start=False, stop=False)
                nc.tensor.matmul(ps_a[:, 0:n], we[:, :], et[:, c % 2, 0:n], start=False, stop=True
                                 ).then_inc(sum_ready, 1)
                pe.wait_ge(sum_copied, c + 1)
                for p in pairs(c):
                    if p >= 4:
                        pe.wait_ge(pre_ready, p - 3)
                    for k in range(paired(p)):
                        col = (2 * (p % 2) + k) * P
                        nc.tensor.matmul(gates[p % 4][:, k, :], ht[:, c % 2, col:col + P], w_hid[:, :], start=True,
                                         stop=True)
                        last = nc.tensor.matmul(gates[p % 4][:, k, 0:3 * D], at[:, c % 2, col:col + P], w_in[:, :],
                                                start=False, stop=True, skip_group_check=True)
                    last.then_inc(gates_ready, 1)

        @block.scalar
        def _(act):
            def copy(c):
                n = blocks(c)
                act.wait_ge(turned_ready, c + 1)
                if c >= 2:
                    act.wait_ge(gates_ready, 2 * c - 2)
                for out, bank, rows in ((ht, ps_h, D), (et, ps_e, D + 1)):
                    last = nc.scalar.copy(out[0:rows, c % 2, 0:n * P].rearrange("p (a b) -> p a b", b=P), bank[:, 0:n, :])
                last.then_inc(copied_act, 1)

            def gate(p):
                act.wait_ge(gates_ready, p + 1)
                if p >= 2:
                    act.wait_ge(updated, p - 1)
                nc.scalar.activation(rz[:, p % 2, 0:paired(p), :], gates[p % 4][:, 0:paired(p), 0:2 * D], ACT.Sigmoid
                                     ).then_inc(rz_ready, 1)

            def tanh(p):
                act.wait_ge(pre_ready, p + 1)
                state = new[:, p % 2, 0:paired(p), :]
                nc.scalar.activation(state, state, ACT.Tanh).then_inc(new_ready, 1)

            copy(0)
            for c in range(CH):
                if c + 1 < CH:
                    copy(c + 1)
                for p in pairs(c):
                    gate(p)
                    if p:
                        tanh(p - 1)
            tanh(PAIRS - 1)

        @block.vector
        def _(dve):
            step = Serial(dve, dve_step)
            for b in range(2):
                last = nc.vector.memset(ht[D:D + 1, b, :], 1.0)
            last.then_inc(ones_ready, 1)
            counts = g["attr_sum"][:, D:NB * (D + 1):D + 1]

            def scale(c):
                n = blocks(c)
                if c >= 2:
                    dve.wait_ge(turned_ready, c - 1)
                nc.vector.tensor_tensor(scaled[:, c % 2, 0:n, :], h[:, 4 * c:4 * c + n, :],
                                        wide(counts[:, 4 * c:4 * c + n]), ALU.mult).then_inc(scaled_ready, 1)

            def copy(c):
                n = blocks(c)
                dve.wait_ge(turned_ready, c + 1)
                if c >= 2:
                    dve.wait_ge(sum_ready, c - 1)
                nc.vector.tensor_copy(ct[:, c % 2, 0:n * P].rearrange("p (a b) -> p a b", b=P), ps_c[:, 0:n, :]
                                      ).then_inc(copied_dve, 1)

            def before_tanh(p):
                n = paired(p)
                pre = new[:, p % 2, 0:n, :]
                dve.wait_ge(rz_ready, p + 1)
                step(nc.vector.tensor_tensor(pre, rz[:, p % 2, 0:n, 0:D], gates[p % 4][:, 0:n, 3 * D:4 * D], ALU.mult))
                nc.vector.tensor_tensor(pre, pre, gates[p % 4][:, 0:n, 2 * D:3 * D], ALU.add).then_inc(pre_ready, 1)

            def update(p):
                n = paired(p)
                state, d = h[:, 2 * p:2 * p + n, :], diff[:, 0:n, :]
                dve.wait_ge(new_ready, p + 1)
                step(nc.vector.tensor_tensor(d, state, new[:, p % 2, 0:n, :], ALU.subtract))
                step(nc.vector.tensor_tensor(d, d, rz[:, p % 2, 0:n, D:2 * D], ALU.mult))
                nc.vector.tensor_tensor(state, d, new[:, p % 2, 0:n, :], ALU.add).then_inc(updated, 1)
                dve.wait_ge(updated, p + 1)

            scale(0)
            copy(0)
            for c in range(CH):
                if c + 1 < CH:
                    scale(c + 1)
                dve.wait_ge(sum_ready, c + 1)
                if c >= 2:
                    dve.wait_ge(gates_ready, 2 * c - 2)
                n = blocks(c) * P
                nc.vector.tensor_copy(at[:, c % 2, 0:n], ps_a[:, 0:n]).then_inc(sum_copied, 1)
                if c + 1 < CH:
                    copy(c + 1)
                for p in pairs(c):
                    before_tanh(p)
                    if p:
                        update(p - 1)
            update(PAIRS - 1)


def gated_layer(nc, g, slabs, w_msg, b_msg, w_ih, w_hh, b_ih, b_hh, out):
    with Scope(nc) as keep:
        h = keep.sb("gated_h", [P, HI, D], F32)
        parts = keep.sb("gated_parts", [P, HI, 3 * D + 1], BF16)
        wd = keep.sb("wd", [D, P], F32)
        ws2 = keep.sb("ws2", [P, P], F32)
        we = keep.sb("we", [D + 1, P], F32)
        w_in = keep.sb("w_in", [P, 3 * D], F32)
        w_hid = keep.sb("w_hid", [D + 1, 4 * D], F32)
        weights = (wd, ws2, we, w_in, w_hid)
        normalise(nc, g, "_gated", h, parts)
        for t in range(2):
            turn_weights(nc, g, t, w_msg, b_msg, w_ih, w_hh, b_ih, b_hh, *weights)
            with Scope(nc, f"_round{t}") as s:
                first_two = s.sb("gated_first_two", [P, NPAD], F32)
                third = s.sb("gated_third", [D + 1, NPAD], F32)
                sum_over_sources(nc, f"_round{t}", slabs, parts, first_two, third)
                gated_update(nc, g, t, h, first_two, third, *weights)
            if t == 0:
                split_features(nc, parts, h)
        with Scope(nc) as s:
            ready = s.sem("result_ready")
            stored = s.sem("result_stored")
            block = s.block()
            x, full = g["x"], (N // P) * P

            @block.vector
            def _(dve):
                nc.vector.tensor_tensor(x[:, :, :], x[:, :, :], h[:, :, :], ALU.add).then_inc(ready, 1)

            @block.sync
            def _(sp):
                sp.wait_ge(ready, 1)
                sp.dma_start(out[0:full, :].rearrange("(b p) f -> p b f", p=P), x[:, 0:N // P, :]).then_inc(stored, 16)
                sp.dma_start(out[full:N, :], x[0:N - full, N // P, :]).then_inc(stored, 16)
                sp.wait_ge(stored, 32)


def gnn_kernel(nc, x, src, dst, edge_attr_32, edge_attr_64, edge_weight, u, w1, b1, w2, b2, conv_w, conv_b, eps,
               w_msg, b_msg, w_ih, w_hh, b_ih, b_hh, out):
    g = {}
    Scope.spent.clear()
    slabs = nc.dram_tensor("slabs", [NSLAB, P, HI * SLAB], BF16)
    scratch = nc.dram_tensor("range_rows", [2, KB + 1, P], F32)
    sorted_rows = nc.dram_tensor("sorted_rows", [E, ROW], F32)
    scanned = nc.dram_tensor("scanned", [E, D], F32)
    carries = nc.dram_tensor("carries", [EP, D], F32)
    table = nc.dram_tensor("feature_table", [HI * P, D], F32)
    with ExitStack() as ctx:
        kept(nc, ctx, g)
        with ExitStack() as to_rank:
            kept_to_rank(nc, to_rank, g)
            prepare_keys(nc, g, src, dst, edge_weight)
            count_sources(nc, g)
            find_ranges(nc, g, scratch)
            rank_and_build(nc, g, edge_attr_32, sorted_rows, slabs)
        scan_sorted(nc, g, sorted_rows, scanned, carries)
        locate_runs(nc, g)
        edge_statistics_layer(nc, g, scanned, carries, x, u, w1, b1, w2, b2)
        convolution_layer(nc, g, slabs, conv_w, conv_b)
        clear_spent(nc)
        g["attr_sum"] = ctx.enter_context(nc.sbuf_tensor("attr_sum", [P, NB * (D + 1)], F32))
        weighted_layer(nc, g, table, scanned, carries, eps, edge_attr_64)
        gated_layer(nc, g, slabs, w_msg, b_msg, w_ih, w_hh, b_ih, b_hh, out)


_INS = ['x', 'src', 'dst', 'edge_attr_32', 'edge_attr_64', 'edge_weight', 'L0_gnn_u', 'L0_gnn_W1', 'L0_gnn_b1',
        'L0_gnn_W2', 'L0_gnn_b2', 'L1_gnn_W', 'L1_gnn_b', 'L2_gnn_eps', 'L3_gnn_w_msg', 'L3_gnn_b_msg',
        'L3_gnn_w_ih', 'L3_gnn_w_hh', 'L3_gnn_b_ih', 'L3_gnn_b_hh']
_OUTS = [((N, D), 'float32')]


def kernel(**inputs):
    import numpy as _np
    import concourse.bacc as _bacc
    from concourse import mybir as _mybir
    from concourse.bass_utils import run_bass_kernel_spmd as _run

    nc = _bacc.Bacc("TRN2", target_bir_lowering=False, num_devices=1)
    arrays, args = {}, []
    for name in _INS:
        a = _np.ascontiguousarray(inputs[name])
        arrays[f"in_{name}_dram"] = a
        args.append(nc.dram_tensor(f"in_{name}_dram", a.shape, _mybir.dt.from_np(a.dtype), kind="ExternalInput").ap())
    for i, (shape, dtype) in enumerate(_OUTS):
        dt = _mybir.dt.from_np(_np.dtype(dtype))
        args.append(nc.dram_tensor(f"out_{i}_dram", shape, dt, kind="ExternalOutput").ap())
    gnn_kernel(nc, *args)
    r = _run(nc, [arrays], core_ids=[0])
    return r.results[0]["out_0_dram"]
```

```python
from contextlib import ExitStack

import concourse.bass as bass
from concourse import mybir
from concourse.alu_op_type import AluOpType as ALU

F32 = mybir.dt.float32
BF16 = mybir.dt.bfloat16
FP16 = mybir.dt.float16
I32 = mybir.dt.int32
ACT = mybir.ActivationFunctionType
AX_X = mybir.AxisListType.X
PE, DVE, ACTE = mybir.EngineType.PE, mybir.EngineType.DVE, mybir.EngineType.Activation
SPE = mybir.EngineType.SP

P = 128
N = 6250
E = 200000
EP = 125
NT = E // EP
D = 64
DA = 32
HID = 128
HI = -(-N // P)
W = 8
KEYW = HI * W
NWIN = 800
WGRP = 4
SLAB_W = 40
NSLAB = NWIN // SLAB_W
SLAB = SLAB_W * W
SPAN = 2 * SLAB
NPAD = NWIN * W
NB = NPAD // P
HGRP = 16
TPAD = NT + WGRP
RU = 16
RG = RU // 2
WT = NWIN * RU // NT
QUAD = 4
NG = NT // RG
ROW = DA + 3
TB = -(-NT // P)
TLAST = NT - (TB - 1) * P
KB = -(-NWIN // P)
HUGE = 3.0e38
KEY_SCALE = 1.0 / 8
RANGES = "the ranges are worked out within the tiles"


class Scope(ExitStack):

    spent = []
    made = 0

    def __init__(self, nc, turn=""):
        super().__init__()
        self.nc, self.turn = nc, turn

    def sb(self, name, shape, dt):
        return self.enter_context(self.nc.sbuf_tensor(name + self.turn, shape, dt))

    def ps(self, name, shape, dt=F32):
        return self.enter_context(self.nc.psum_tensor(name + self.turn, shape, dt))

    def sem(self, name):
        Scope.made += 1
        handle = self.nc.alloc_semaphore(f"{name}_{Scope.made}")
        self.spent.append(handle)
        return handle

    def block(self):
        return self.enter_context(self.nc.Block())


class Serial:

    def __init__(self, eng, sem):
        self.eng, self.sem, self.n = eng, sem, 0

    def __call__(self, ins):
        self.n += 1
        ins.then_inc(self.sem, 1)
        self.eng.wait_ge(self.sem, self.n)


def clear_spent(nc):
    nc.clear_and_free_semaphores(Scope.spent)
    Scope.spent.clear()
    nc.all_engine_barrier()


def two_parts(queue, out, in_, sem):
    queue.dma_start(out[0:112], in_[0:112]).then_inc(sem, 16)
    queue.dma_start(out[112:EP], in_[112:EP]).then_inc(sem, 16)


def prepare_keys(nc, g, src, dst, edge_weight):
    with Scope(nc) as s:
        raw_i = s.sb("raw_i", [EP, 2, NT], I32)
        raw_w = s.sb("raw_w", [EP, NT], F32)
        part_i = s.sb("part_i", [EP, NT], I32)
        tile_i = s.sb("tile_i", [P, 2, TB, EP], I32)
        tile_f = s.sb("tile_f", [P, 2, TB, EP], F32)
        key_i = s.sb("key_i", [EP, 4, NT], I32)
        count_i = s.sb("count_i", [P, NWIN], I32)
        turned = s.ps("turned", [P, 8, 512])
        loaded = s.sem("loaded")
        consts = s.sem("consts")
        dve_step = s.sem("dve_step")
        tiles_float = s.sem("tiles_float")
        turned_ready = s.sem("turned_ready")
        turned_used = s.sem("turned_used")
        block = s.block()
        @block.sync
        def _(sp):
            sp.dma_start(raw_i[:, 0, :], src.rearrange("(p j) -> p j", p=EP)).then_inc(loaded, 16)
            sp.dma_start(raw_i[:, 1, :], dst.rearrange("(p j) -> p j", p=EP)).then_inc(loaded, 16)
            sp.dma_start(raw_w[:, :], edge_weight.rearrange("(p j) -> p j", p=EP)).then_inc(loaded, 16)

        @block.scalar
        def _(act):
            for n, x in enumerate((src, dst)):
                rows = x.rearrange("(t e) -> t e", e=EP)
                full = (TB - 1) * P
                act.dma_start(tile_i[:, n, 0:TB - 1, :],
                              rows[0:full, :].rearrange("(b t) e -> t b e", t=P)).then_inc(loaded, 16)
                act.dma_start(tile_i[0:TLAST, n, TB - 1, :], rows[full:NT, :]).then_inc(loaded, 16)

        @block.gpsimd
        def _(pool):
            pool.iota(count_i[:, :], pattern=[[1, NWIN]], base=0, channel_multiplier=0).then_inc(consts, 1)
            pool.iota(g["rowid_i"][:, :], pattern=[[0, 1]], base=0, channel_multiplier=1).then_inc(consts, 1)
            pool.memset(g["ident"][:, :], 0.0).then_inc(consts, 1)
            pool.memset(g["below"][:, :], 1.0).then_inc(consts, 1)
            pool.memset(g["ones"][:, :], 1.0).then_inc(consts, 1)
            pool.wait_ge(consts, 5)
            pool.affine_select(out=g["ident"][:, :], in_=g["ident"][:, :], compare_op=ALU.not_equal, fill=1.0,
                               base=0, pattern=[[-1, P]], channel_multiplier=1).then_inc(consts, 1)
            pool.affine_select(out=g["below"][:, :], in_=g["below"][:, :], compare_op=ALU.is_gt, fill=0.0,
                               base=0, pattern=[[1, P]], channel_multiplier=-1).then_inc(consts, 1)
            pool.tensor_copy(g["iota"][:, :], count_i[:, 0:512]).then_inc(consts, 1)
            pool.tensor_copy(g["rowid"][:, :], g["rowid_i"][:, :]).then_inc(consts, 1)
            pool.memset(g["mkeys"][:, NT:TPAD], -1.0).then_inc(consts, 1)
            pool.memset(g["lo_tiles"][:, NT:TPAD], 0.0).then_inc(consts, 1)

        @block.tensor
        def _(pe):
            pe.wait_ge(tiles_float, 4)
            pe.wait_ge(consts, 11)
            for n in range(2):
                for b in range(TB):
                    rows = P if b < TB - 1 else TLAST
                    last = nc.tensor.transpose(turned[0:EP, 4 * n + b // 4, (b % 4) * P:(b % 4) * P + rows],
                                               tile_f[0:rows, n, b, :], g["ident"][0:rows, 0:rows])
                last.then_inc(turned_ready, 1)

        @block.vector
        def _(dve):
            step = Serial(dve, dve_step)
            dve.wait_ge(loaded, 7 * 16)
            for n in range(2):
                nc.vector.tensor_copy(tile_f[:, n, 0:TB - 1, :], tile_i[:, n, 0:TB - 1, :]).then_inc(tiles_float, 1)
                nc.vector.tensor_copy(tile_f[0:TLAST, n, TB - 1, :],
                                      tile_i[0:TLAST, n, TB - 1, :]).then_inc(tiles_float, 1)
            dve.wait_ge(consts, 11)
            nc.vector.memset(g["zerob"][:, :], 0.0).then_inc(dve_step, 1)
            nc.vector.tensor_copy(g["identb"][:, :], g["ident"][:, :]).then_inc(dve_step, 1)
            nc.vector.tensor_copy(g["belowb"][:, :], g["below"][:, :]).then_inc(dve_step, 1)
            nc.vector.tensor_scalar(g["winbase"][:, :], count_i[:, :], 512.0, None, ALU.mult).then_inc(dve_step, 1)
            nc.vector.tensor_copy(g["sdw"][:, :, 0], raw_i[:, 0, :]).then_inc(dve_step, 1)
            nc.vector.tensor_copy(g["sdw"][:, :, 1], raw_i[:, 1, :]).then_inc(dve_step, 1)
            nc.vector.tensor_copy(g["sdw"][:, :, 2], raw_w[:, :]).then_inc(dve_step, 1)
            step.n = 7
            step(nc.vector.tensor_single_scalar(part_i[:, :], raw_i[:, 0, :], P - 1, ALU.bitwise_and))
            step(nc.vector.tensor_copy(g["lo"][:, 0:NT], part_i[:, :]))
            step(nc.vector.tensor_single_scalar(part_i[:, :], raw_i[:, 0, :], 7, ALU.arith_shift_right))
            step(nc.vector.tensor_copy(g["hi"][:, 0:NT], part_i[:, :]))
            step(nc.vector.memset(g["lo"][:, NT:NT + RG], 0.0))
            step(nc.vector.memset(g["hi"][:, NT:NT + RG], 0.0))
            step(nc.vector.tensor_copy(g["iota_rg"][:, :, :], g["iota"][:, 0:P].unsqueeze(2).broadcast_to([P, P, RG])))
            dve.wait_ge(tiles_float, 4)
            for op, c in ((ALU.min, 0), (ALU.max, 1)):
                step(nc.vector.tensor_reduce(g["span"][:, c, 0:TB - 1], tile_f[:, 1, 0:TB - 1, :], AX_X, op))
                step(nc.vector.tensor_reduce(g["span"][0:TLAST, c, TB - 1:TB], tile_f[0:TLAST, 1, TB - 1:TB, :],
                                             AX_X, op))
            for n in range(2):
                dve.wait_ge(turned_ready, n + 1)
                flat = turned[0:EP, 4 * n:4 * n + 4, :].rearrange("p a b -> p (a b)")
                if n:
                    step(nc.vector.tensor_copy(g["dkey"][:, 0:NT], flat[:, 0:NT]))
                step(nc.vector.tensor_copy(key_i[:, n, :], flat[:, 0:NT]))
            s_i, d_i, u_i, v_i = (key_i[:, n, :] for n in range(4))
            step(nc.vector.tensor_single_scalar(u_i, d_i, 3, ALU.arith_shift_right))
            step(nc.vector.tensor_single_scalar(v_i, d_i, W - 1, ALU.bitwise_and))
            step(nc.vector.tensor_single_scalar(d_i, s_i, 7, ALU.arith_shift_right))
            step(nc.vector.scalar_tensor_tensor(raw_w[:, :], d_i, float(W), v_i, ALU.mult, ALU.add))
            step(nc.vector.scalar_tensor_tensor(g["mkeys"][:, 0:NT], u_i, 512.0, raw_w[:, :], ALU.mult, ALU.add))
            step(nc.vector.tensor_single_scalar(v_i, s_i, P - 1, ALU.bitwise_and))
            step(nc.vector.tensor_scalar(g["lo_tiles"][:, 0:NT], v_i, KEY_SCALE, None, ALU.mult))


def one_hots(nc, g, out_lo, out_hi, n):
    def keys(x, width):
        return x[:, bass.ds(n * RG, RG)].unsqueeze(1).broadcast_to([EP, width, RG])
    nc.vector.tensor_tensor(out_lo, g["iota_rg"][0:EP, :, :], keys(g["lo"], P), ALU.is_equal)
    return nc.vector.tensor_tensor(out_hi, g["iota_rg"][0:EP, 0:HI, :], keys(g["hi"], HI), ALU.is_equal)


def count_sources(nc, g):
    with Scope(nc) as s:
        oh_lo = s.sb("hist_lo", [EP, 2, P, RG], BF16)
        oh_hi = s.sb("hist_hi", [EP, 2, HI, RG], BF16)
        totals = s.sb("totals", [P, HI], F32)
        upto = s.sb("upto", [P, HI], F32)
        zeros = s.sb("zeros", [P, HI], F32)
        hist = s.ps("hist", [P, HI])
        sums = s.ps("sums", [P, 2, HI])
        oh_ready = s.sem("oh_ready")
        oh_used = s.sem("oh_used")
        sums_ready = s.sem("sums_ready")
        dve_step = s.sem("dve_step")
        block = s.block()
        @block.vector
        def _(dve):
            step = Serial(dve, dve_step)
            step(nc.vector.memset(zeros[:, :], 0.0))
            with dve.Fori(0, NG // 2) as i:
                for h in range(2):
                    dve.wait_ge(oh_used, 2 * i + h + 1)
                    one_hots(nc, g, oh_lo[:, h], oh_hi[:, h], 2 * i + h).then_inc(oh_ready, 1)
            dve.wait_ge(oh_used, NG + 2)
            step(nc.vector.tensor_copy(g["out_deg"][:, 0:HI], hist[:, :]))
            step(nc.vector.memset(g["out_deg"][:, HI:NB], 0.0))
            dve.wait_ge(sums_ready, 1)
            step(nc.vector.tensor_copy(totals[:, :], sums[:, 1, :]))
            step(nc.vector.tensor_tensor_scan(upto[:, :], totals[:, :], zeros[:, :], 0.0, ALU.add, ALU.add))
            step(nc.vector.tensor_tensor(upto[:, :], upto[:, :], totals[:, :], ALU.subtract))
            step(nc.vector.tensor_tensor(g["start"][:, 0:HI], sums[:, 0, :], upto[:, :], ALU.add))

        @block.tensor
        def _(pe):
            pe.sem_inc(oh_used, 2)
            nc.tensor.matmul(hist[:, :], g["zerob"][:, 0:P], g["zerob"][:, 0:HI], start=True, stop=True)
            with pe.Fori(0, NG // 2) as i:
                for h in range(2):
                    pe.wait_ge(oh_ready, 2 * i + h + 1)
                    for u in range(RG):
                        last = nc.tensor.matmul(hist[:, :], oh_lo[:, h, :, u], oh_hi[:, h, :, u], start=False,
                                                stop=True, skip_group_check=True)
                    last.then_inc(oh_used, 1)
            pe.wait_ge(dve_step, 2)
            nc.tensor.matmul(sums[:, 0, :], g["below"][:, :], g["out_deg"][:, 0:HI], start=True, stop=True)
            nc.tensor.matmul(sums[:, 1, :], g["ones"][:, :], g["out_deg"][:, 0:HI], start=True,
                             stop=True).then_inc(sums_ready, 1)


def rank_and_build(nc, g, edge_attr_32, sorted_rows, slabs):
    with Scope(nc) as s:
        oh_lo = s.sb("oh_lo", [EP, 2, P, RG], BF16)
        oh_hi = s.sb("oh_hi", [EP, 2, HI, RG], BF16)
        lo_rows_b = s.sb("lo_rows_b", [P, 2, 2, QUAD, EP], BF16)
        lo_rows_f = s.sb("lo_rows_f", [P, 2, 2, QUAD, EP], F32)
        earlier = s.sb("earlier", [EP, 2, 2, QUAD, EP], BF16)
        counts = s.sb("counts", [P, 2, HI], F32)
        picked = s.sb("picked", [EP, 2, RG, HI], BF16)
        place = s.sb("place", [EP, 2, RG], F32)
        place_i = s.sb("place_i", [EP, 2, RG], I32)
        attr = s.sb("attr", [EP, 2, RG, DA], F32)
        rows = s.sb("rows", [EP, 2, RG, ROW], F32)
        low = s.sb("low", [EP, 2 * P * WGRP], BF16)
        high = s.sb("high", [EP, 2 * WGRP * KEYW], BF16)
        window_keys = s.sb("window_keys", [EP, 2 * WGRP], FP16)
        iota_g = s.sb("iota_g", [P, KEYW, WGRP], FP16)
        slab = s.sb("slab", [P, HI, 2 * SLAB], BF16)
        turned = s.ps("turned_lo", [P, 2, QUAD, P], BF16)
        part = [s.ps(f"part{b}", [P, HI, W]) for b in range(2)]
        same0 = s.ps("same0", [EP, QUAD * EP])
        same1 = s.ps("same1", [EP, QUAD * EP])
        count_rows = [s.ps(f"count_rows{b}", [EP, 2, HI]) for b in range(2)]
        running = s.ps("running", [P, HI])
        oh_ready = s.sem("oh_ready")
        turned_ready = s.sem("turned_ready")
        lo_rows_ready = s.sem("lo_rows_ready")
        same_ready = s.sem("same_ready")
        earlier_ready = s.sem("earlier_ready")
        counts_ready = s.sem("counts_ready")
        count_rows_ready = s.sem("count_rows_ready")
        updated = s.sem("updated")
        placed = s.sem("placed")
        places_ready = s.sem("places_ready")
        rows_ready = s.sem("rows_ready")
        attr0 = s.sem("attr0")
        attr1 = s.sem("attr1")
        scattered0 = s.sem("scattered0")
        scattered1 = s.sem("scattered1")
        pool_turns = s.sem("pool_turns")
        iota_ready = s.sem("iota_ready")
        keys_ready = s.sem("keys_ready")
        made = s.sem("made")
        used = s.sem("used")
        copied = s.sem("copied")
        slab_free = s.sem("slab_free")
        stored = [s.sem(f"slab_stored{b}") for b in range(2)]
        block = s.block()
        same = (same0, same1)
        MOST = NWIN * NT
        RING = 2 * SLAB_W // WT
        attr_in, scattered = (attr0, attr1), (scattered0, scattered1)
        attrs = edge_attr_32.rearrange("(p j) c -> p (j c)", p=EP)
        ALL = 16 * RG

        @block.sync
        def _(sp):
            sp.sem_inc(slab_free, RING)
            with sp.Fori(0, NG // 2 // RING) as r:
                for k in range(2):
                    with sp.Fori(0, RING // 2) as m:
                        i = r * RING + k * (RING // 2) + m
                        for h in range(2):
                            sp.wait_ge(rows_ready, 2 * i + h + 1)
                            sp.dma_start(attr[:, h].rearrange("p j c -> p (j c)"),
                                         attrs[:, bass.ds((2 * i + h) * RG * DA, RG * DA)]).then_inc(attr_in[h], 16)
                    n = r * 2 + k
                    sp.wait_ge(copied, n * SLAB_W + SLAB_W + 2)
                    sp.dma_start(slabs[bass.ds(r, 1), :, :].rearrange("a p (h c) -> p (a h) c", c=SPAN)
                                 [:, :, k * SLAB:(k + 1) * SLAB],
                                 slab[:, :, k * SLAB:(k + 1) * SLAB]).then_inc(stored[k], 16)
                    sp.wait_ge(stored[k], r * 16 + 16)
                    sp.sem_inc(slab_free, RING // 2)

        @block.gpsimd
        def _(pool):
            with pool.Fori(0, NG // 2) as i:
                for h in range(2):
                    pool.wait_ge(places_ready, 2 * i + h + 1)
                    pool.wait_ge(rows_ready, 2 * i + h + 3)
                    pool.sem_inc(pool_turns, 1)
                    for u in range(RG):
                        pool.indirect_dma_start(sorted_rows[:, :],
                                                bass.IndirectOffsetOnAxis(ap=place_i[:, h, u:u + 1], axis=0),
                                                rows[:, h, u, :], None).then_inc(scattered[h], 16)
            for h in range(2):
                pool.wait_ge(scattered[h], ALL * NG // 2)

        @block.vector
        def _(dve):
            def lo_hi(n, h):
                one_hots(nc, g, oh_lo[:, h], oh_hi[:, h], n).then_inc(oh_ready, 1)

            def mask(n, h):
                for q in range(2):
                    dve.wait_ge(same_ready, 2 * n + q + 1)
                    nc.vector.tensor_tensor(earlier[:, h, q], same[q][:, :].rearrange("p (u e) -> p u e", u=QUAD),
                                            g["belowb"][0:EP, 0:EP].unsqueeze(1).broadcast_to([EP, QUAD, EP]),
                                            ALU.mult).then_inc(earlier_ready, 1)

            def pick(n, h, u):
                if u % 2 == 0:
                    dve.wait_ge(count_rows_ready, n * RG + u + 3)
                nc.vector.tensor_tensor_reduce(out=picked[:, h, u, :], in0=count_rows[u // 2 % 2][:, u % 2, :],
                                               in1=oh_hi[:, h, :, u], scale=1.0, scalar=0.0, op0=ALU.mult,
                                               op1=ALU.add, accum_out=place[:, h, u:u + 1]).then_inc(placed, 1)

            def window(i, j, before, offset):
                base = g["winbase"][0:EP, bass.ds(i * WT + j, 1)]
                with dve.Fori(before[j], before[j + 1]) as v:
                    t = nc.s_assert_within(v * WGRP - offset[j], 0, NT, skip_runtime_bounds_check_because=RANGES)
                    slot = v & 1
                    keys = window_keys[:, bass.ds(slot * WGRP, WGRP)]
                    dve.wait_ge(used, v + 1)
                    nc.vector.tensor_scalar(keys, g["mkeys"][:, bass.ds(t, WGRP)], base, KEY_SCALE,
                                            ALU.subtract, ALU.mult).then_inc(keys_ready, 1)
                    nc.vector.tensor_tensor(
                        low[:, bass.ds(slot * (P * WGRP), P * WGRP)].rearrange("p (a b) -> p a b", b=WGRP),
                        iota_g[0:EP, 0:P, :],
                        g["lo_tiles"][:, bass.ds(t, WGRP)].unsqueeze(1).broadcast_to([EP, P, WGRP]), ALU.is_equal)
                    dve.wait_ge(keys_ready, v + 1)
                    nc.vector.tensor_tensor(
                        high[:, bass.ds(slot * (WGRP * KEYW), WGRP * KEYW)].rearrange("p (a b) -> p a b", b=WGRP),
                        iota_g[0:EP, :, :], keys.unsqueeze(1).broadcast_to([EP, KEYW, WGRP]), ALU.is_equal
                    ).then_inc(made, 1)

            nc.vector.tensor_scalar(iota_g[:, :, :], g["iota"][:, 0:KEYW].unsqueeze(2).broadcast_to([P, KEYW, WGRP]),
                                    KEY_SCALE, None, ALU.mult).then_inc(iota_ready, 1)
            dve.wait_ge(iota_ready, 1)
            dve.sem_inc(placed, 4)
            lo_hi(0, 0)
            mask(0, 0)
            def turn(i, first):
                before, offset = load_ranges(nc, g["win_table"], DVE, i * WT, WT, MOST)
                for h in range(2):
                    n = 2 * i + h
                    for u in range(RG):
                        if u % 2 == 0:
                            window(i, (h * RG + u) // 2, before, offset)
                        if u == 0:
                            dve.wait_ge(count_rows_ready, n * RG + 1)
                            dve.wait_ge(placed, n * RG + 4)
                            lo_hi(n + 1, 1 - h)
                        pick(n, h, u)
                        if u == 7:
                            mask(n + 1, 1 - h)
                    dve.wait_ge(placed, n * RG + RG + 4)
                    if not first:
                        dve.wait_ge(scattered[h], ALL * i)
                    nc.vector.tensor_copy(place_i[:, h, :], place[:, h, :]).then_inc(places_ready, 1)

            turn(0, True)
            with dve.Fori(1, NG // 2) as i:
                turn(i, False)

        @block.scalar
        def _(act):
            act.sem_inc(rows_ready, 2)

            def lo_rows(n, h, q):
                act.wait_ge(turned_ready, n + 1)
                nc.scalar.copy(lo_rows_b[:, h, q], turned[:, q, :, 0:EP])
                nc.scalar.copy(lo_rows_f[:, h, q], turned[:, q, :, 0:EP]).then_inc(lo_rows_ready, 1)

            def window(k, j, before):
                act.wait_ge(used, before[j + 1] + 2)
                nc.scalar.copy(slab[:, :, bass.ds(k * (WT * W) + j * W, W)], part[j % 2][:, :, :]
                               ).then_inc(copied, 1)

            nc.scalar.copy(counts[:, 0, :], g["start"][:, 0:HI]).then_inc(counts_ready, 1)
            for q in range(2):
                lo_rows(0, 0, q)
            def turn(i, k, first):
                before, _ = load_ranges(nc, g["win_table"], ACTE, i * WT, WT, MOST)
                act.wait_ge(slab_free, i + 1)
                for h in range(2):
                    n = 2 * i + h
                    for u in range(RG):
                        act.wait_ge(updated, n * RG + u + 1)
                        nc.scalar.copy(counts[:, (u + 1) % 2, :], running[:, :]).then_inc(counts_ready, 1)
                        if u in (3, 5):
                            lo_rows(n + 1, 1 - h, u // 4)
                        if u == 7:
                            act.wait_ge(attr_in[h], 16 * (i + 1))
                            if not first:
                                act.wait_ge(scattered[h], ALL * i)
                            nc.scalar.copy(rows[:, h, :, 0:DA], attr[:, h])
                            nc.scalar.copy(rows[:, h, :, DA:ROW],
                                           g["sdw"][:, bass.ds(n * RG, RG), :]).then_inc(rows_ready, 1)
                        if u % 2 and h * RG + u > 1:
                            window(k, (h * RG + u) // 2 - 1, before)
                window(k, WT - 1, before)

            turn(0, 0, True)
            with act.Fori(1, RING) as k:
                turn(k, k, False)
            with act.Fori(1, NG // 2 // RING) as r:
                with act.Fori(0, RING) as k:
                    turn(r * RING + k, k, False)

        @block.tensor
        def _(pe):
            pe.sem_inc(count_rows_ready, 1)

            def turn(n, h):
                pe.wait_ge(oh_ready, n + 1)
                for q in range(2):
                    for u in range(QUAD):
                        last = nc.tensor.transpose(turned[:, q, u, 0:EP],
                                                   oh_lo[:, h, :, q * QUAD + u], g["identb"][0:EP, 0:EP])
                last.then_inc(turned_ready, 1)

            def compare(n, h):
                for q in range(2):
                    pe.wait_ge(lo_rows_ready, 2 * n + q + 1)
                    for u in range(QUAD):
                        x = lo_rows_b[:, h, q, u, :]
                        last = nc.tensor.matmul(same[q][:, u * EP:(u + 1) * EP], x, x, start=True, stop=True)
                    last.then_inc(same_ready, 1)

            def chain(n, h, u):
                q, v = divmod(u, QUAD)
                if v == 0:
                    pe.wait_ge(earlier_ready, 2 * n + q + 1)
                pe.wait_ge(counts_ready, n * RG + u + 1)
                nc.tensor.matmul(running[:, :], oh_lo[:, h, :, u], oh_hi[:, h, :, u], start=False, stop=True,
                                 skip_group_check=True).then_inc(updated, 1)
                if u % 2 == 0:
                    pe.wait_ge(placed, n * RG + u + 2)
                out = count_rows[u // 2 % 2][:, u % 2, :]
                nc.tensor.matmul(out, lo_rows_f[:, h, q, v, :], counts[:, u % 2, :], start=True, stop=False)
                nc.tensor.matmul(out, earlier[:, h, q, v, :], oh_hi[:, h, :, u], start=False,
                                 stop=True).then_inc(count_rows_ready, 1)

            def window(i, j, before):
                out = part[j % 2][:, :, :].rearrange("p a b -> p (a b)")
                pe.wait_ge(copied, i * WT + j + 1)
                nc.tensor.matmul(out, g["zerob"][0:EP, 0:P], g["zerob"][0:EP, 0:KEYW], start=True, stop=True)
                with pe.Fori(before[j], before[j + 1]) as v:
                    slot = v & 1
                    pe.wait_ge(made, v + 1)
                    for k in range(WGRP):
                        last = nc.tensor.matmul(out, low[:, bass.DynSlice(slot * (P * WGRP) + k, P, WGRP)],
                                                high[:, bass.DynSlice(slot * (WGRP * KEYW) + k, KEYW, WGRP)],
                                                start=False, stop=True, skip_group_check=True)
                    last.then_inc(used, 1)

            pe.sem_inc(used, 2)
            pe.sem_inc(copied, 2)
            nc.tensor.matmul(running[:, :], g["ident"][:, :], g["start"][:, 0:HI], start=True, stop=True)
            turn(0, 0)
            compare(0, 0)
            with pe.Fori(0, NG // 2) as i:
                before, _ = load_ranges(nc, g["win_table"], PE, i * WT, WT, MOST)
                for h in range(2):
                    n = 2 * i + h
                    for u in range(RG):
                        if u == 2:
                            turn(n + 1, 1 - h)
                        if u == 7:
                            compare(n + 1, 1 - h)
                        chain(n, h, u)
                        if u % 2:
                            window(i, (h * RG + u) // 2, before)


def scan_sorted(nc, g, sorted_rows, scanned, carries):
    J = 160
    STEPS = NT // J
    with Scope(nc) as s:
        rows = [s.sb(f"scan_rows{b}", [EP, J, ROW], F32) for b in range(2)]
        out = [s.sb(f"scan_out{b}", [EP, J, 2 * DA], F32) for b in range(2)]
        cap = s.sb("cap", [EP, J], F32)
        differs = s.sb("differs", [EP, J], F32)
        last_key = s.sb("last_key", [EP, 1], F32)
        carry = s.sb("carry", [EP, 2 * DA], F32)
        state = s.sb("state", [2 * DA, EP], F32)
        turned_carry = s.sb("turned_carry", [2 * DA, EP], F32)
        key_row = s.sb("key_row", [2 * DA, EP], F32)
        keep = s.sb("keep", [2 * DA, EP], F32)
        keep_cap = s.sb("keep_cap", [DA, EP], F32)
        carry_in = s.sb("carry_in", [EP, 2 * DA], F32)
        ps_carry = s.ps("ps_carry", [2 * DA, EP])
        ps_key = s.ps("ps_key", [2 * DA, EP])
        ps_in = s.ps("ps_in", [EP, 2 * DA])
        rows_in = [s.sem(f"rows_in{b}") for b in range(2)]
        rows_out = [s.sem(f"rows_out{b}") for b in range(2)]
        dve_step = s.sem("dve_step")
        scans_done = s.sem("scans_done")
        pe_done = s.sem("pe_done")
        shifted = s.sem("shifted")
        carried = s.sem("carried")
        block = s.block()
        src_v = sorted_rows[:, :].rearrange("(p j) c -> p j c", p=EP)
        dst_v = scanned[:, :].rearrange("(p j) c -> p j c", p=EP)

        @block.sync
        def _(sp):
            for k in range(STEPS):
                if k >= 2:
                    sp.wait_ge(scans_done, k - 1)
                two_parts(sp, rows[k % 2][:, :, :], src_v[:, k * J:(k + 1) * J, :], rows_in[k % 2])

        @block.scalar
        def _(act):
            for k in range(STEPS):
                act.wait_ge(scans_done, k + 1)
                two_parts(act, dst_v[:, k * J:(k + 1) * J, :], out[k % 2][:, :, :], rows_out[k % 2])
            act.wait_ge(carried, 1)
            act.dma_start(carries[:, :], carry_in[:, :]).then_inc(rows_out[0], 16)
            act.wait_ge(rows_out[0], 16 * (STEPS + 1))
            act.wait_ge(rows_out[1], 16 * STEPS)

        @block.vector
        def _(dve):
            step = Serial(dve, dve_step)
            step(nc.vector.memset(last_key[:, :], -1.0))
            step(nc.vector.memset(carry[:, :], 0.0))
            for k in range(STEPS):
                rk, ok = rows[k % 2], out[k % 2]
                same = g["same_src"][:, k * J:(k + 1) * J]
                dve.wait_ge(rows_in[k % 2], 32 * (k // 2 + 1))
                src_c, dst_c, w_c = (rk[:, :, DA + c] for c in range(3))
                nc.vector.tensor_tensor(same[:, 0:1], src_c[:, 0:1], last_key[:, :], ALU.is_equal)
                step(nc.vector.tensor_tensor(same[:, 1:J], src_c[:, 1:J], src_c[:, 0:J - 1], ALU.is_equal))
                nc.vector.tensor_scalar(cap[:, :], same, -0.5, HUGE, ALU.add, ALU.mult)
                nc.vector.tensor_copy(last_key[:, :], src_c[:, J - 1:J])
                nc.vector.tensor_copy(g["dst_sorted"][:, k * J:(k + 1) * J], dst_c)
                step(nc.vector.tensor_tensor(differs[:, :], src_c, dst_c, ALU.not_equal))
                step(nc.vector.tensor_tensor(g["w_sorted"][:, k * J:(k + 1) * J], w_c, differs[:, :], ALU.mult))
                if k >= 2:
                    dve.wait_ge(rows_out[k % 2], 32 * (k // 2))
                for f in range(DA):
                    nc.vector.tensor_tensor_scan(ok[:, :, f], cap[:, :], rk[:, :, f], carry[:, f:f + 1],
                                                 ALU.min, ALU.max)
                    last = nc.vector.tensor_tensor_scan(ok[:, :, DA + f], same, rk[:, :, f],
                                                        carry[:, DA + f:DA + f + 1], ALU.mult, ALU.add)
                last.then_inc(scans_done, 1)
                dve.wait_ge(scans_done, k + 1)
                step(nc.vector.tensor_copy(carry[:, :], ok[:, J - 1, :]))
            dve.wait_ge(pe_done, 1)
            step(nc.vector.tensor_copy(turned_carry[:, :], ps_carry[:, :]))
            step(nc.vector.tensor_copy(key_row[:, :], ps_key[:, :]))
            step(nc.vector.memset(keep[:, 0:1], 0.0))
            step(nc.vector.tensor_tensor(keep[:, 1:EP], key_row[:, 1:EP], key_row[:, 0:EP - 1], ALU.is_equal))
            step(nc.vector.tensor_copy(g["keep_run"][:, :], keep[:, :]))
            step(nc.vector.tensor_scalar(keep_cap[:, :], keep[0:DA, :], -0.5, HUGE, ALU.add, ALU.mult))
            step(nc.vector.memset(state[:, 0:1], 0.0))
            step(nc.vector.tensor_tensor_scan(state[0:DA, 1:EP], keep_cap[:, 0:EP - 1], turned_carry[0:DA, 0:EP - 1],
                                              0.0, ALU.min, ALU.max))
            step(nc.vector.tensor_tensor_scan(state[DA:2 * DA, 1:EP], keep[DA:2 * DA, 0:EP - 1],
                                              turned_carry[DA:2 * DA, 0:EP - 1], 0.0, ALU.mult, ALU.add))
            nc.vector.sem_inc(shifted, 1)
            dve.wait_ge(pe_done, 2)
            nc.vector.tensor_copy(carry_in[:, :], ps_in[:, :]).then_inc(carried, 1)

        @block.tensor
        def _(pe):
            pe.wait_ge(dve_step, 2 + 4 * STEPS)
            nc.tensor.matmul(ps_key[:, :], last_key[:, :].broadcast_to([EP, 2 * DA]), g["ident"][0:EP, 0:EP],
                             start=True, stop=True)
            nc.tensor.transpose(ps_carry[:, :], carry[:, :], g["ident"][0:EP, 0:EP]).then_inc(pe_done, 1)
            pe.wait_ge(shifted, 1)
            nc.tensor.transpose(ps_in[:, :], state[:, :], g["ident"][0:2 * DA, 0:2 * DA]).then_inc(pe_done, 1)


def locate_runs(nc, g):
    with Scope(nc) as s:
        end = s.sb("end", [P, HI], F32)
        part = s.sb("part", [P, HI], F32)
        rest = s.sb("rest", [P, HI], F32)
        test = s.sb("test", [P, HI], F32)
        part_i = s.sb("run_part_i", [P, HI], I32)
        dve_step = s.sem("dve_step")
        block = s.block()

        @block.vector
        def _(dve):
            step = Serial(dve, dve_step)
            start, deg = g["start"][:, 0:HI], g["out_deg"][:, 0:HI]
            step(nc.vector.tensor_tensor(end[:, :], start, deg, ALU.add))
            step(nc.vector.tensor_scalar(end[:, :], end[:, :], -1.0, 0.0, ALU.add, ALU.max))
            step(nc.vector.tensor_copy(g["end_i"][:, :], end[:, :]))
            step(nc.vector.tensor_scalar(part[:, :], end[:, :], 1.0 / NT, None, ALU.mult))
            step(nc.vector.tensor_copy(part_i[:, :], part[:, :]))
            step(nc.vector.tensor_copy(part[:, :], part_i[:, :]))
            step(nc.vector.scalar_tensor_tensor(rest[:, :], part[:, :], -float(NT), end[:, :], ALU.mult, ALU.add))
            step(nc.vector.tensor_scalar(test[:, :], rest[:, :], float(NT), None, ALU.is_ge))
            step(nc.vector.tensor_tensor(part[:, :], part[:, :], test[:, :], ALU.add))
            step(nc.vector.tensor_scalar(test[:, :], rest[:, :], 0.0, None, ALU.is_lt))
            step(nc.vector.tensor_tensor(part[:, :], part[:, :], test[:, :], ALU.subtract))
            step(nc.vector.tensor_copy(g["end_part_i"][:, :], part[:, :]))
            step(nc.vector.scalar_tensor_tensor(test[:, :], part[:, :], float(NT), start, ALU.mult, ALU.is_gt))
            step(nc.vector.tensor_scalar(g["has_out"][:, :], deg, 0.0, None, ALU.is_gt))
            step(nc.vector.tensor_tensor(g["spans"][:, :], test[:, :], g["has_out"][:, :], ALU.mult))


def gather_runs(nc, pool, g, scanned, carries, ends, carry_in, sem):
    for b in range(HI):
        pool.indirect_dma_start(ends[:, b, :], None, scanned[:, :],
                                bass.IndirectOffsetOnAxis(ap=g["end_i"][:, b:b + 1], axis=0)).then_inc(sem, 16)
        pool.indirect_dma_start(carry_in[:, b, :], None, carries[:, :],
                                bass.IndirectOffsetOnAxis(ap=g["end_part_i"][:, b:b + 1], axis=0)
                                ).then_inc(sem, 16)


def find_ranges(nc, g, scratch):
    Q = KB + 1
    ROWLEN = Q * P
    with Scope(nc) as s:
        least = s.sb("least", [P, NT], F32)
        greatest = s.sb("greatest", [P, NT], F32)
        count_i = s.sb("tile_count_i", [P, NT], I32)
        up = s.sb("up", [P, NT], F32)
        down = s.sb("down", [P, NT], F32)
        meets = s.sb("meets", [P, NT], F32)
        meets2 = s.sb("meets2", [P, NT], F32)
        first_t = s.sb("first_target", [P, Q], F32)
        last_t = s.sb("last_target", [P, Q], F32)
        ends = s.sb("range_ends", [P, 2, Q], F32)
        turned_sb = s.sb("ranges_turned", [Q, 2, P], F32)
        row = s.sb("range_row", [1, 2, ROWLEN], F32)
        steps = s.sb("range_steps", [1, ROWLEN], F32)
        steps_i = s.sb("range_steps_i", [1, ROWLEN], I32)
        cum = s.sb("range_cum", [1, ROWLEN], F32)
        zero = s.sb("range_zero", [1, ROWLEN], F32)
        spread = s.ps("spread", [P, 8, 512])
        consts = s.sem("consts")
        spread_ready = s.sem("spread_ready")
        dve_step = s.sem("dve_step")
        ends_ready = s.sem("ends_ready")
        turned_ready = s.sem("turned_ready")
        stored = s.sem("stored")
        rows_ready = s.sem("rows_ready")
        block = s.block()

        @block.gpsimd
        def _(pool):
            pool.iota(count_i[:, :], pattern=[[1, NT]], base=0, channel_multiplier=0).then_inc(consts, 1)
            pool.memset(zero[:, :], 0.0).then_inc(consts, 1)

        @block.tensor
        def _(pe):
            for c in range(2):
                for b in range(TB):
                    rows = P if b < TB - 1 else TLAST
                    last = nc.tensor.matmul(spread[:, 4 * c + b // 4, (b % 4) * P:(b % 4) * P + rows],
                                            g["span"][0:rows, c, b:b + 1].broadcast_to([rows, P]),
                                            g["ident"][0:rows, 0:rows], start=True, stop=True)
            last.then_inc(spread_ready, 1)
            pe.wait_ge(ends_ready, 1)
            for c in range(2):
                last = nc.tensor.transpose(spread[0:Q, 0, c * P:(c + 1) * P], ends[:, c, :], g["ident"][:, :])
            last.then_inc(turned_ready, 1)

        @block.vector
        def _(dve):
            step = Serial(dve, dve_step)
            for q in range(KB):
                step(nc.vector.tensor_scalar(first_t[:, q:q + 1], g["rowid"][:, :], float(W), float(W * P * q),
                                             ALU.mult, ALU.add))
            step(nc.vector.tensor_scalar(first_t[:, KB:Q], g["rowid"][:, :], float(P), None, ALU.mult))
            step(nc.vector.tensor_scalar(last_t[:, 0:KB], first_t[:, 0:KB], float(W - 1), None, ALU.add))
            step(nc.vector.tensor_scalar(last_t[:, KB:Q], first_t[:, KB:Q], float(P - 1), None, ALU.add))
            dve.wait_ge(consts, 2)
            step(nc.vector.tensor_scalar(up[:, :], count_i[:, :], 1.0, None, ALU.add))
            step(nc.vector.tensor_scalar(down[:, :], count_i[:, :], -1.0, float(NT), ALU.mult, ALU.add))
            dve.wait_ge(spread_ready, 1)
            for x, c in ((least, 0), (greatest, 1)):
                step(nc.vector.tensor_copy(x[:, :], spread[:, 4 * c:4 * c + 4, :].rearrange("p a b -> p (a b)")[:, 0:NT]))
            for q in range(Q):
                step(nc.vector.tensor_scalar(meets[:, :], least[:, :], last_t[:, q:q + 1], None, ALU.is_le))
                step(nc.vector.scalar_tensor_tensor(meets[:, :], greatest[:, :], first_t[:, q:q + 1], meets[:, :],
                                                    ALU.is_ge, ALU.mult))
                for x, c in ((up, 0), (down, 1)):
                    step(nc.vector.tensor_tensor_reduce(out=meets2[:, :], in0=meets[:, :], in1=x[:, :], scale=1.0,
                                                        scalar=0.0, op0=ALU.mult, op1=ALU.max,
                                                        accum_out=ends[:, c, q:q + 1]))
            dve.sem_inc(ends_ready, 1)
            dve.wait_ge(turned_ready, 1)
            nc.vector.tensor_copy(turned_sb[:, :, :], spread[0:Q, 0, 0:2 * P].rearrange("q (c p) -> q c p", c=2)
                                  ).then_inc(rows_ready, 1)
            dve.wait_ge(stored, 32)
            behind, left = row[:, 0, :], row[:, 1, :]
            step(nc.vector.tensor_tensor(steps[:, :], behind, left, ALU.add))
            step(nc.vector.tensor_scalar(steps[:, :], steps[:, :], -float(NT), 1.0, ALU.add, ALU.max))
            step(nc.vector.tensor_scalar(left, left, -1.0, float(NT), ALU.mult, ALU.add))
            step(nc.vector.tensor_scalar(left, left, float(NT - 1), None, ALU.min))
            win, blk = slice(0, NWIN), slice(KB * P, KB * P + NB)
            step(nc.vector.tensor_scalar(steps[:, win], steps[:, win], float(WGRP - 1), None, ALU.add))
            step(nc.vector.tensor_scalar(steps[:, blk], steps[:, blk], float(HGRP - 1), None, ALU.add))
            for part, shift in ((win, 2), (blk, 4)):
                step(nc.vector.tensor_copy(steps_i[:, part], steps[:, part]))
                step(nc.vector.tensor_single_scalar(steps_i[:, part], steps_i[:, part], shift,
                                                    ALU.arith_shift_right))
                step(nc.vector.tensor_copy(steps[:, part], steps_i[:, part]))
            step(nc.vector.tensor_scalar(cum[:, blk], steps[:, blk], -float(HGRP), float(NT), ALU.mult, ALU.add))
            step(nc.vector.tensor_tensor(left[:, blk], left[:, blk], cum[:, blk], ALU.min))
            for part, n, size, table in ((win, NWIN, WGRP, g["win_table"]), (blk, NB, HGRP, g["blk_table"])):
                step(nc.vector.tensor_tensor_scan(cum[:, part], steps[:, part], zero[:, part], 0.0, ALU.add, ALU.add))
                step(nc.vector.memset(table[:, 0:2 * n + 2], 0))
                step(nc.vector.tensor_copy(table[:, 2:2 * n + 2:2], cum[:, part]))
                step(nc.vector.tensor_tensor(cum[:, part], cum[:, part], steps[:, part], ALU.subtract))
                step(nc.vector.scalar_tensor_tensor(table[:, 1:2 * n + 1:2], cum[:, part], float(size), left[:, part],
                                                    ALU.mult, ALU.subtract))

        @block.sync
        def _(sp):
            sp.wait_ge(rows_ready, 1)
            sp.dma_start(scratch[:, :, :].rearrange("c q p -> q c p"), turned_sb[:, :, :]).then_inc(stored, 16)
            sp.wait_ge(stored, 16)
            sp.dma_start(row[:, :, :], scratch[:, :, :].rearrange("c q p -> c (q p)").unsqueeze(0)).then_inc(stored, 16)


def load_ranges(nc, table, engine, first, count, most):
    _, v = nc.values_load_multi_w_load_instructions(table[0:1, bass.ds(first * 2, 2 * count + 2)], engines=[engine],
                                                    min_val=0, max_val=most, skip_runtime_bounds_check_because=RANGES)
    return [x & ((1 << 20) - 1) for x in v[0::2]], v[1::2]


def split_three(step, nc, out, rest, x):
    step(nc.vector.memset(out[:, :, 3 * D:3 * D + 1], 1.0))
    step(nc.vector.tensor_copy(out[:, :, 0:D], x))
    step(nc.vector.tensor_tensor(rest, x, out[:, :, 0:D], ALU.subtract))
    step(nc.vector.tensor_copy(out[:, :, D:2 * D], rest))
    step(nc.vector.tensor_tensor(rest, rest, out[:, :, D:2 * D], ALU.subtract))
    step(nc.vector.tensor_copy(out[:, :, 2 * D:3 * D], rest))


def sum_over_sources(nc, turn, slabs, parts, sums):
    PH = 7
    PIECES = HI // PH
    BLOCKS = SPAN // P
    TURNS = NPAD // SPAN
    PART = 3 * D + 1
    with Scope(nc, turn) as s:
        piece = [s.sb(f"piece{k}", [P, PH, SPAN], BF16) for k in range(PIECES)]
        three = s.sb("three_parts", [P, 2, PART], F32)
        partial = s.sb("partial_sum", [P, 2, D], F32)
        bank = [s.ps(f"sum_bank{b}", [P, PART]) for b in range(BLOCKS)]
        piece_in = [s.sem(f"piece_in{k}") for k in range(PIECES)]
        piece_used = s.sem("piece_used")
        block_ready = s.sem("block_ready")
        copied = s.sem("copied")
        partial_ready = s.sem("partial_ready")
        added = s.sem("added")
        block = s.block()

        @block.sync
        def _(sp):
            with sp.Fori(0, TURNS) as n:
                for k in range(PIECES):
                    sp.wait_ge(piece_used, n * PIECES + k + 1)
                    sp.dma_start(piece[k][:, :, :].rearrange("p a b -> p (a b)"),
                                 slabs[bass.ds(n, 1), :, k * PH * SPAN:(k + 1) * PH * SPAN]
                                 .rearrange("a p c -> p (a c)")).then_inc(piece_in[k], 16)

        @block.tensor
        def _(pe):
            pe.sem_inc(piece_used, PIECES)
            pe.sem_inc(copied, BLOCKS)
            with pe.Fori(0, TURNS) as n:
                for k in range(PIECES):
                    pe.wait_ge(piece_in[k], n * 16 + 16)
                    for b in range(BLOCKS):
                        if k == 0:
                            pe.wait_ge(copied, n * BLOCKS + b + 1)
                        for j in range(PH):
                            hb = k * PH + j
                            last = nc.tensor.matmul(bank[b][:, :], piece[k][:, j, b * P:(b + 1) * P], parts[:, hb, :],
                                                    start=hb == 0, stop=hb == HI - 1)
                        if k == PIECES - 1:
                            last.then_inc(block_ready, 1)
                    if k < PIECES - 1:
                        last.then_inc(piece_used, 1)
                pe.wait_ge(block_ready, n * BLOCKS + BLOCKS)
                pe.sem_inc(piece_used, 1)

        @block.scalar
        def _(act):
            act.sem_inc(added, 2)
            with act.Fori(0, TURNS // 2) as i:
                for c in range(2 * BLOCKS):
                    n = i * (2 * BLOCKS) + c
                    act.wait_ge(block_ready, n + 1)
                    act.wait_ge(added, n + 1)
                    nc.scalar.copy(three[:, c % 2, :], bank[c % BLOCKS][:, :]).then_inc(copied, 1)

        @block.vector
        def _(dve):
            with dve.Fori(0, TURNS // 2) as i:
                for c in range(2 * BLOCKS):
                    n = i * (2 * BLOCKS) + c
                    t = three[:, c % 2, :]
                    out = sums[:, bass.ds(n * (D + 1), D + 1)]
                    dve.wait_ge(copied, n + BLOCKS + 1)
                    nc.vector.tensor_tensor(partial[:, c % 2, :], t[:, D:2 * D], t[:, 2 * D:3 * D], ALU.add
                                            ).then_inc(partial_ready, 1)
                    nc.vector.tensor_copy(out[:, D:D + 1], t[:, 3 * D:PART])
                    dve.wait_ge(partial_ready, n + 1)
                    nc.vector.tensor_tensor(out[:, 0:D], partial[:, c % 2, :], t[:, 0:D], ALU.add).then_inc(added, 1)


def wide(x, width=D):
    return x.unsqueeze(2).broadcast_to([P, x.shape[1], width])


def layer_norm_relu(step, nc, act_sqrt, g, out, tmp, col):
    x = g["x"][:, :, :]
    mean, var = col[:, 0, :], col[:, 1, :]
    step(nc.vector.tensor_reduce(mean, x, AX_X, ALU.add))
    step(nc.vector.tensor_scalar(mean, mean, 1.0 / D, None, ALU.mult))
    step(nc.vector.tensor_tensor(out[:, :, :], x, wide(mean), ALU.subtract))
    step(nc.vector.tensor_tensor(tmp[:, :, :], out[:, :, :], out[:, :, :], ALU.mult))
    step(nc.vector.tensor_reduce(var, tmp[:, :, :], AX_X, ALU.add))
    step(nc.vector.tensor_scalar(var, var, 1.0 / D, 1e-5, ALU.mult, ALU.add))
    act_sqrt()
    step(nc.vector.reciprocal(var, var))
    step(nc.vector.scalar_tensor_tensor(out[:, :, :], out[:, :, :], 0.0, wide(var), ALU.max, ALU.mult))


def edge_statistics_layer(nc, g, scanned, carries, x_in, u, w1, b1, w2, b2):
    NF = 3 * DA
    with Scope(nc) as s:
        ends = s.sb("ends", [P, HI, 2 * DA], F32)
        carry_in = s.sb("run_carry", [P, HI, 2 * DA], F32)
        feats = s.sb("feats", [P, HI, NF], F32)
        feats_t = s.sb("feats_t", [NF, HI * P], F32)
        hidden = s.sb("hidden", [HID, HI * P], F32)
        off = s.sb("off", [P, HI], F32)
        inv = s.sb("inv", [P, HI], F32)
        w1_sb = s.sb("w1_sb", [NF, HID], F32)
        w2_sb = s.sb("w2_sb", [HID, D], F32)
        w1_u = s.sb("w1_u", [HID, 1], F32)
        u_col = s.sb("u_col", [HID, 1], F32)
        bias = s.sb("bias", [HID, 1], F32)
        b2_row = s.sb("b2_row", [P, D], F32)
        turned = [s.ps(f"feats_turned{b}", [NF, 4, P]) for b in range(2)]
        ps_hidden = [s.ps(f"ps_hidden{b}", [HID, 512]) for b in range(2)]
        ps_out = [s.ps(f"ps_out{b}", [P, 8, D]) for b in range(2)]
        loaded = s.sem("loaded")
        gathered = s.sem("gathered")
        dve_step = s.sem("dve_step")
        bias_ready = s.sem("bias_ready")
        feats_ready = s.sem("feats_ready")
        turned_ready = s.sem("turned_ready")
        turned_copied = s.sem("turned_copied")
        hidden_ready = s.sem("hidden_ready")
        hidden_copied = s.sem("hidden_copied")
        out_ready = s.sem("out_ready")
        added = s.sem("added")
        block = s.block()
        CH = -(-HI // 4)
        OC = -(-HI // 8)
        x, full = g["x"], (N // P) * P

        @block.sync
        def _(sp):
            sp.dma_start(w1_sb[:, :], w1[0:NF, :]).then_inc(loaded, 16)
            sp.dma_start(w1_u[:, :], w1[NF:NF + 1, :].rearrange("a h -> h a")).then_inc(loaded, 16)
            sp.dma_start(u_col[:, :], u[0:1, 0:1].broadcast_to([HID, 1])).then_inc(loaded, 16)
            sp.dma_start(bias[:, :], b1.unsqueeze(1)).then_inc(loaded, 16)
            sp.dma_start(w2_sb[:, :], w2).then_inc(loaded, 16)
            sp.dma_start(b2_row[:, :], b2.unsqueeze(0).broadcast_to([P, D])).then_inc(loaded, 16)
            sp.wait_ge(dve_step, 1)
            sp.dma_start(x[:, 0:N // P, :], x_in[0:full, :].rearrange("(b p) f -> p b f", p=P)).then_inc(loaded, 16)
            sp.dma_start(x[0:N - full, N // P, :], x_in[full:N, :]).then_inc(loaded, 16)

        @block.gpsimd
        def _(pool):
            gather_runs(nc, pool, g, scanned, carries, ends, carry_in, gathered)

        @block.vector
        def _(dve):
            step = Serial(dve, dve_step)
            step(nc.vector.memset(x[:, N // P, :], 0.0))
            step(nc.vector.tensor_scalar(off[:, :], g["spans"][:, :], -1.0, HUGE, ALU.add, ALU.mult))
            step(nc.vector.tensor_scalar(inv[:, :], g["out_deg"][:, 0:HI], 1.0, None, ALU.max))
            step(nc.vector.reciprocal(inv[:, :], inv[:, :]))
            dve.wait_ge(loaded, 8 * 16)
            nc.vector.scalar_tensor_tensor(bias[:, :], w1_u[:, :], u_col[:, 0:1], bias[:, :], ALU.mult,
                                           ALU.add).then_inc(bias_ready, 1)
            step(nc.vector.tensor_tensor(x[:, :, :], x[:, :, :], b2_row[:, :].unsqueeze(1).broadcast_to([P, HI, D]),
                                         ALU.add))
            dve.wait_ge(gathered, 16 * 2 * HI)
            total, most, mean = (feats[:, :, c * DA:(c + 1) * DA] for c in range(3))
            step(nc.vector.tensor_tensor(carry_in[:, :, :], carry_in[:, :, :], wide(g["spans"][:, :]), ALU.mult))
            step(nc.vector.tensor_tensor(total, ends[:, :, DA:], carry_in[:, :, DA:], ALU.add))
            step(nc.vector.tensor_tensor(total, total, wide(g["has_out"][:, :], DA), ALU.mult))
            step(nc.vector.tensor_tensor(mean, total, wide(inv[:, :], DA), ALU.mult))
            step(nc.vector.tensor_tensor(most, carry_in[:, :, 0:DA], wide(off[:, :], DA), ALU.add))
            step(nc.vector.tensor_tensor(most, most, ends[:, :, 0:DA], ALU.max))
            nc.vector.tensor_tensor(most, most, wide(g["has_out"][:, :], DA), ALU.mult).then_inc(feats_ready, 1)
            for c in range(OC):
                n = min(8, HI - 8 * c)
                dve.wait_ge(out_ready, c + 1)
                nc.vector.tensor_tensor(x[:, 8 * c:8 * c + n, :], x[:, 8 * c:8 * c + n, :], ps_out[c % 2][:, 0:n, :],
                                        ALU.add).then_inc(added, 1)

        @block.scalar
        def _(act):
            act.wait_ge(bias_ready, 1)
            def copy(c):
                n = min(4, HI - 4 * c)
                act.wait_ge(turned_ready, c + 1)
                nc.scalar.copy(feats_t[:, c * 512:c * 512 + n * P].rearrange("p (a b) -> p a b", b=P),
                               turned[c % 2][:, 0:n, :]).then_inc(turned_copied, 1)

            copy(0)
            for c in range(CH):
                if c + 1 < CH:
                    copy(c + 1)
                n = min(4, HI - 4 * c)
                act.wait_ge(hidden_ready, c + 1)
                nc.scalar.activation(hidden[:, c * 512:c * 512 + n * P], ps_hidden[c % 2][:, 0:n * P], ACT.Relu,
                                     bias=bias[:, 0:1]).then_inc(hidden_copied, 1)

        @block.tensor
        def _(pe):
            def turn(c):
                if c >= 2:
                    pe.wait_ge(turned_copied, c - 1)
                for a in range(min(4, HI - 4 * c)):
                    last = nc.tensor.transpose(turned[c % 2][:, a, :], feats[:, 4 * c + a, :], g["ident"][:, :])
                last.then_inc(turned_ready, 1)

            pe.wait_ge(feats_ready, 1)
            turn(0)
            for c in range(CH):
                if c + 1 < CH:
                    turn(c + 1)
                n = min(4, HI - 4 * c)
                pe.wait_ge(turned_copied, c + 1)
                if c >= 2:
                    pe.wait_ge(hidden_copied, c - 1)
                nc.tensor.matmul(ps_hidden[c % 2][:, 0:n * P], w1_sb[:, :], feats_t[:, c * 512:c * 512 + n * P],
                                 start=True, stop=True).then_inc(hidden_ready, 1)
            for c in range(OC):
                n = min(8, HI - 8 * c)
                pe.wait_ge(hidden_copied, min(CH, 2 * c + 2))
                if c >= 2:
                    pe.wait_ge(added, c - 1)
                for a in range(n):
                    b = 8 * c + a
                    last = nc.tensor.matmul(ps_out[c % 2][:, a, :], hidden[:, b * P:(b + 1) * P], w2_sb[:, :],
                                            start=True, stop=True)
                last.then_inc(out_ready, 1)


def kept(nc, ctx, g):
    for name, shape, dt in (
        ("ident", [P, P], F32), ("identb", [P, P], BF16), ("below", [P, P], F32), ("belowb", [P, P], BF16),
        ("ones", [P, P], F32), ("zerob", [P, 512], BF16), ("iota", [P, 512], FP16), ("rowid", [P, 1], F32),
        ("rowid_i", [P, 1], I32), ("dkey", [EP, NT], F32),
        ("span", [P, 2, TB], F32), ("out_deg", [P, NB], F32), ("start", [P, NB], F32),
        ("same_src", [EP, NT], F32), ("dst_sorted", [EP, NT], I32), ("w_sorted", [EP, NT], F32),
        ("end_i", [P, HI], I32), ("end_part_i", [P, HI], I32), ("has_out", [P, HI], F32), ("spans", [P, HI], F32),
        ("x", [P, HI, D], F32), ("win_table", [1, 2 * NWIN + 2], I32), ("blk_table", [1, 2 * NB + 2], I32),
        ("keep_run", [D, EP], F32),
    ):
        g[name] = ctx.enter_context(nc.sbuf_tensor(name, shape, dt))


def kept_to_rank(nc, ctx, g):
    for name, shape, dt in (("winbase", [P, NWIN], F32), ("mkeys", [EP, TPAD], F32), ("lo_tiles", [EP, TPAD], BF16),
                            ("sdw", [EP, NT, 3], F32), ("lo", [EP, NT + RG], FP16), ("hi", [EP, NT + RG], FP16),
                            ("iota_rg", [P, P, RG], FP16)):
        g[name] = ctx.enter_context(nc.sbuf_tensor(name, shape, dt))


def normalise(nc, g, turn, h, parts=None, by_degree=None):
    with Scope(nc, turn) as s:
        tmp = s.sb("norm_tmp", [P, HI, D], F32)
        scaled = s.sb("norm_scaled", [P, HI, D], F32)
        col = s.sb("norm_col", [P, 2, HI], F32)
        dve_step = s.sem("dve_step")
        var_ready = s.sem("var_ready")
        root_ready = s.sem("root_ready")
        block = s.block()

        @block.vector
        def _(dve):
            step = Serial(dve, dve_step)

            def roots():
                dve.sem_inc(var_ready, 1)
                dve.wait_ge(root_ready, 1)

            if by_degree is not None:
                step(nc.vector.tensor_scalar(by_degree[:, :], g["out_deg"][:, 0:HI], 1.0, None, ALU.add))
            layer_norm_relu(step, nc, roots, g, h, tmp, col)
            if by_degree is not None:
                step(nc.vector.reciprocal(by_degree[:, :], by_degree[:, :]))
                step(nc.vector.tensor_tensor(scaled[:, :, :], h[:, :, :], wide(by_degree[:, :]), ALU.mult))
                split_three(step, nc, parts, tmp[:, :, :], scaled[:, :, :])
            elif parts is not None:
                split_three(step, nc, parts, tmp[:, :, :], h[:, :, :])

        @block.scalar
        def _(act):
            act.wait_ge(var_ready, 1)
            if by_degree is not None:
                nc.scalar.activation(by_degree[:, :], by_degree[:, :], ACT.Sqrt)
            nc.scalar.activation(col[:, 1, :], col[:, 1, :], ACT.Sqrt).then_inc(root_ready, 1)


def convolution_layer(nc, g, slabs, w, b):
    CH = -(-HI // 4)
    with Scope(nc) as keep:
        h = keep.sb("conv_h", [P, HI, D], F32)
        parts = keep.sb("conv_parts", [P, HI, 3 * D + 1], BF16)
        rs = keep.sb("conv_rs", [P, HI], F32)
        sums = keep.sb("conv_sums", [P, NB * (D + 1)], F32)
        normalise(nc, g, "_conv", h, parts, rs)
        sum_over_sources(nc, "_conv", slabs, parts, sums)
        with Scope(nc) as s:
            w_sb = s.sb("conv_w", [2 * D, D], F32)
            b_row = s.sb("conv_b_row", [P, D], F32)
            deg = s.sb("conv_deg", [P, HI], F32)
            factor = s.sb("conv_factor", [P, HI], F32)
            both = s.sb("conv_both", [P, HI, 2 * D], F32)
            ht = s.sb("conv_ht", [P, 2, 512], F32)
            turned = [s.ps(f"conv_turned{k}", [P, 512]) for k in range(2)]
            own = [s.ps(f"conv_own{k}", [P, 4, D]) for k in range(2)]
            loaded = s.sem("loaded")
            deg_ready = s.sem("deg_ready")
            root_ready = s.sem("root_ready")
            both_ready = s.sem("both_ready")
            turned_ready = s.sem("turned_ready")
            turned_copied = s.sem("turned_copied")
            ready = s.sem("products_ready")
            added = s.sem("added")
            dve_step = s.sem("dve_step")
            block = s.block()
            x = g["x"]

            @block.sync
            def _(sp):
                sp.dma_start(w_sb[:, :], w).then_inc(loaded, 16)
                sp.dma_start(b_row[:, :], b.unsqueeze(0).broadcast_to([P, D])).then_inc(loaded, 16)

            @block.tensor
            def _(pe):
                def turn(c):
                    if c >= 2:
                        pe.wait_ge(turned_copied, c - 1)
                    for a in range(min(4, HI - 4 * c)):
                        last = nc.tensor.transpose(turned[c % 2][:, a * P:(a + 1) * P], both[:, 4 * c + a, :],
                                                   g["ident"][:, :])
                    last.then_inc(turned_ready, 1)

                pe.wait_ge(both_ready, 1)
                turn(0)
                pe.wait_ge(loaded, 2 * 16)
                for c in range(CH):
                    if c + 1 < CH:
                        turn(c + 1)
                    pe.wait_ge(turned_copied, c + 1)
                    if c >= 2:
                        pe.wait_ge(added, c - 1)
                    for a in range(min(4, HI - 4 * c)):
                        last = nc.tensor.matmul(own[c % 2][:, a, :], ht[:, c % 2, a * P:(a + 1) * P], w_sb[:, :],
                                                start=True, stop=True)
                    last.then_inc(ready, 1)

            @block.scalar
            def _(act):
                act.wait_ge(deg_ready, 1)
                nc.scalar.activation(factor[:, :], deg[:, :], ACT.Sqrt).then_inc(root_ready, 1)
                for c in range(CH):
                    n = min(4, HI - 4 * c) * P
                    act.wait_ge(turned_ready, c + 1)
                    if c >= 2:
                        act.wait_ge(ready, c - 1)
                    nc.scalar.copy(ht[:, c % 2, 0:n], turned[c % 2][:, 0:n]).then_inc(turned_copied, 1)

            @block.vector
            def _(dve):
                step = Serial(dve, dve_step)
                columns = sums[:, 0:HI * (D + 1)].rearrange("p (b f) -> p b f", f=D + 1)
                mean = both[:, :, D:2 * D]
                nc.vector.tensor_scalar(deg[:, :], columns[:, :, D], 1.0, None, ALU.add).then_inc(deg_ready, 1)
                step(nc.vector.tensor_copy(both[:, :, 0:D], h[:, :, :]))
                step(nc.vector.tensor_tensor(mean, h[:, :, :], wide(rs[:, :]), ALU.mult))
                step(nc.vector.tensor_tensor(mean, mean, columns[:, :, 0:D], ALU.add))
                dve.wait_ge(root_ready, 1)
                step(nc.vector.tensor_tensor(factor[:, :], factor[:, :], deg[:, :], ALU.mult))
                step(nc.vector.reciprocal(factor[:, :], factor[:, :]))
                nc.vector.tensor_tensor(mean, mean, wide(factor[:, :]), ALU.mult).then_inc(both_ready, 1)
                dve.wait_ge(loaded, 2 * 16)
                step(nc.vector.tensor_tensor(x[:, :, :], x[:, :, :], b_row[:, :].unsqueeze(1).broadcast_to([P, HI, D]),
                                             ALU.add))
                for c in range(CH):
                    n = min(4, HI - 4 * c)
                    blocks = slice(4 * c, 4 * c + n)
                    dve.wait_ge(ready, c + 1)
                    nc.vector.tensor_tensor(x[:, blocks, :], x[:, blocks, :], own[c % 2][:, 0:n, :], ALU.add
                                            ).then_inc(added, 1)


def scan_messages(nc, g, table, scanned, carries, edge_attr_64):
    MOST = NB * NT
    HALF = HGRP // 2
    J = NT // NB
    STEPS = NT // J
    U = 5
    with Scope(nc) as s:
        index = [s.sb(f"gather_index{b}", [EP, J], I32) for b in range(U)]
        got = [s.sb(f"gathered_rows{b}", [EP, J, D], F32) for b in range(U)]
        out = [s.sb(f"message_sums{b}", [EP, J, D], F32) for b in range(U)]
        carry = s.sb("sum_carry", [EP, D], F32)
        state = s.sb("sum_state", [D, EP], F32)
        turned_carry = s.sb("sum_turned_carry", [D, EP], F32)
        carry_in = s.sb("sum_carry_in", [EP, D], F32)
        attr = [s.sb(f"attr_half{b}", [EP, HALF, D + 1], F32) for b in range(2)]
        keys = s.sb("block_keys", [EP, HGRP], F32)
        hot = s.sb("block_hot", [EP, HGRP, P], F32)
        base = s.sb("block_base", [P, NB], F32)
        iota_f = s.sb("iota_f", [P, P], F32)
        total = [s.ps(f"block_total{b}", [P, D + 1]) for b in range(U)]
        ps_carry = s.ps("ps_sum_carry", [D, EP])
        ps_in = s.ps("ps_sum_in", [EP, D])
        index_ready = s.sem("index_ready")
        gathered = [s.sem(f"gathered{b}") for b in range(U)]
        weighted = s.sem("weighted")
        scans_done = s.sem("scans_done")
        carry_ready = s.sem("carry_ready")
        sums_out = [s.sem(f"sums_out{b}") for b in range(U)]
        pool_turns = s.sem("pool_turns")
        dve_step = s.sem("dve_step")
        pe_done = s.sem("pe_done")
        carried = s.sem("carried")
        consts = s.sem("block_consts")
        attr_in = [s.sem(f"attr_in{b}") for b in range(2)]
        keys_ready = s.sem("keys_ready")
        made = s.sem("made")
        used = s.sem("used")
        copied = s.sem("copied")
        block = s.block()
        dst_v = scanned[:, :].rearrange("(p j) c -> p (j c)", p=EP)
        attr_rows = edge_attr_64.rearrange("(t e) f -> e t f", e=EP)

        @block.gpsimd
        def _(pool):
            pool.sem_inc(scans_done, U)
            with pool.Fori(0, STEPS // U) as i:
                for b in range(U):
                    pool.wait_ge(scans_done, U * i + b + 1)
                    pool.tensor_copy(index[b][:, :], g["dst_sorted"][:, bass.ds((U * i + b) * J, J)]
                                     ).then_inc(index_ready, 1)
                    pool.wait_ge(index_ready, U * i + b + 1)
                    pool.sem_inc(pool_turns, 1)
                    for j in range(J):
                        pool.indirect_dma_start(got[b][:, j, :], None, table[:, :],
                                                bass.IndirectOffsetOnAxis(ap=index[b][:, j:j + 1], axis=0)
                                                ).then_inc(gathered[b], 16)

        @block.scalar
        def _(act):
            with act.Fori(0, STEPS // U) as i:
                before, _ = load_ranges(nc, g["blk_table"], ACTE, i * U, U, MOST)
                for b in range(U):
                    act.wait_ge(used, before[b + 1] * HGRP + HGRP)
                    nc.scalar.copy(g["attr_sum"][:, bass.ds((i * U + b) * (D + 1), D + 1)], total[b][:, :]
                                   ).then_inc(copied, 1)

        @block.vector
        def _(dve):
            for b in range(2):
                nc.vector.memset(attr[b][:, :, D:D + 1], 1.0).then_inc(consts, 1)
            nc.vector.tensor_copy(iota_f[:, :], g["iota"][:, 0:P]).then_inc(consts, 1)
            nc.vector.tensor_scalar(base[:, :], g["iota"][:, 0:NB], float(P), None, ALU.mult).then_inc(consts, 1)
            nc.vector.memset(carry[:, :], 0.0).then_inc(carry_ready, 1)
            dve.wait_ge(consts, 4)
            dve.sem_inc(made, HGRP)
            with dve.Fori(0, STEPS // U) as i:
                before, offset = load_ranges(nc, g["blk_table"], DVE, i * U, U, MOST)
                for b in range(U):
                    with dve.Fori(before[b], before[b + 1]) as v:
                        t = nc.s_assert_within(v * HGRP - offset[b], 0, NT - HGRP,
                                               skip_runtime_bounds_check_because=RANGES)
                        dve.wait_ge(made, v * HGRP + HGRP)
                        nc.vector.tensor_scalar(keys[:, :], g["dkey"][:, bass.ds(t, HGRP)],
                                                base[0:EP, bass.ds(i * U + b, 1)], None,
                                                ALU.subtract).then_inc(keys_ready, 1)
                        dve.wait_ge(keys_ready, v + 1)
                        for j in range(HGRP):
                            dve.wait_ge(used, v * HGRP + j + 1)
                            nc.vector.tensor_scalar(hot[:, j, :], iota_f[0:EP, :], keys[:, j:j + 1], None,
                                                    ALU.is_equal).then_inc(made, 1)
                    n = U * i + b
                    dve.wait_ge(gathered[b], 16 * J * (i + 1))
                    w = g["w_sorted"][:, bass.ds(n * J, J)]
                    nc.vector.tensor_tensor(got[b][:, :, :], got[b][:, :, :], w.unsqueeze(2).broadcast_to([EP, J, D]),
                                            ALU.mult).then_inc(weighted, 1)
                    dve.wait_ge(weighted, n + 1)
                    dve.wait_ge(carry_ready, n + 1)
                    dve.wait_ge(sums_out[b], 32 * i + 1)
                    for f in range(D):
                        last = nc.vector.tensor_tensor_scan(out[b][:, :, f], g["same_src"][:, bass.ds(n * J, J)],
                                                            got[b][:, :, f], carry[:, f:f + 1], ALU.mult, ALU.add)
                    last.then_inc(scans_done, 1)
                    dve.wait_ge(scans_done, n + 1 + U)
                    nc.vector.tensor_copy(carry[:, :], out[b][:, J - 1, :]).then_inc(carry_ready, 1)
            step = Serial(dve, dve_step)
            dve.wait_ge(pe_done, 1)
            step(nc.vector.tensor_copy(turned_carry[:, :], ps_carry[:, :]))
            step(nc.vector.memset(state[:, 0:1], 0.0))
            step(nc.vector.tensor_tensor_scan(state[:, 1:EP], g["keep_run"][:, 0:EP - 1], turned_carry[:, 0:EP - 1],
                                              0.0, ALU.mult, ALU.add))
            dve.wait_ge(pe_done, 2)
            nc.vector.tensor_copy(carry_in[:, :], ps_in[:, :]).then_inc(carried, 1)

        @block.tensor
        def _(pe):
            pe.sem_inc(used, HGRP)
            pe.sem_inc(copied, U)
            with pe.Fori(0, STEPS // U) as i:
                before, _ = load_ranges(nc, g["blk_table"], PE, i * U, U, MOST)
                for b in range(U):
                    pe.wait_ge(copied, i * U + b + 1)
                    nc.tensor.matmul(total[b][:, :], g["zerob"][0:EP, 0:P], g["zerob"][0:EP, 0:D + 1], start=True,
                                     stop=True)
                    with pe.Fori(before[b], before[b + 1]) as v:
                        for j in range(HGRP):
                            if j % HALF == 0:
                                pe.wait_ge(attr_in[j // HALF], v * 16 + 16)
                            pe.wait_ge(made, v * HGRP + HGRP + j + 1)
                            nc.tensor.matmul(total[b][:, :], hot[:, j, :], attr[j // HALF][:, j % HALF, :],
                                             start=False, stop=True, skip_group_check=True).then_inc(used, 1)
            pe.wait_ge(carry_ready, STEPS + 1)
            nc.tensor.transpose(ps_carry[:, :], carry[:, :], g["ident"][0:EP, 0:EP]).then_inc(pe_done, 1)
            pe.wait_ge(dve_step, 3)
            nc.tensor.transpose(ps_in[:, :], state[:, :], g["ident"][0:D, 0:D]).then_inc(pe_done, 1)

        @block.sync
        def _(sp):
            for b in range(U):
                sp.sem_inc(sums_out[b], 1)
            sp.wait_ge(consts, 2)
            with sp.Fori(0, STEPS // U) as i:
                before, offset = load_ranges(nc, g["blk_table"], SPE, i * U, U, MOST)
                for b in range(U):
                    n = U * i + b
                    with sp.Fori(before[b], before[b + 1]) as v:
                        t = nc.s_assert_within(v * HGRP - offset[b], 0, NT - HGRP,
                                               skip_runtime_bounds_check_because=RANGES)
                        for k in range(2):
                            sp.wait_ge(used, v * HGRP + (k + 1) * HALF)
                            sp.dma_start(attr[k][:, :, 0:D], attr_rows[:, bass.ds(t + k * HALF, HALF), :]
                                         ).then_inc(attr_in[k], 16)
                    sp.wait_ge(scans_done, n + 1 + U)
                    two_parts(sp, dst_v[:, bass.ds(n * J * D, J * D)], out[b][:, :, :].rearrange("p j f -> p (j f)"),
                              sums_out[b])
            for b in range(U):
                sp.wait_ge(sums_out[b], 32 * STEPS // U + 1)
            sp.wait_ge(carried, 1)
            sp.dma_start(carries[:, :], carry_in[:, :]).then_inc(sums_out[0], 16)
            sp.wait_ge(sums_out[0], 32 * STEPS // U + 17)


def weighted_layer(nc, g, table, scanned, carries, eps, edge_attr_64):
    with Scope(nc) as keep:
        h = keep.sb("weighted_h", [P, HI, D], F32)
        normalise(nc, g, "_weighted", h)
        with Scope(nc) as s:
            stored = s.sem("table_stored")
            block = s.block()

            @block.sync
            def _(sp):
                sp.dma_start(table[:, :].rearrange("(b p) f -> p b f", p=P), h[:, :, :]).then_inc(stored, 16)
                sp.wait_ge(stored, 16)

        scan_messages(nc, g, table, scanned, carries, edge_attr_64)
        with Scope(nc) as s:
            ends = s.sb("message_ends", [P, HI, D], F32)
            carry_in = s.sb("message_carry", [P, HI, D], F32)
            factor = s.sb("one_eps", [P, 1], F32)
            loaded = s.sem("loaded")
            gathered = s.sem("gathered")
            dve_step = s.sem("dve_step")
            block = s.block()
            x = g["x"]

            @block.sync
            def _(sp):
                sp.dma_start(factor[:, :], eps.unsqueeze(0).broadcast_to([P, 1])).then_inc(loaded, 16)

            @block.gpsimd
            def _(pool):
                gather_runs(nc, pool, g, scanned, carries, ends, carry_in, gathered)

            @block.vector
            def _(dve):
                step = Serial(dve, dve_step)
                dve.wait_ge(loaded, 16)
                step(nc.vector.tensor_scalar(factor[:, :], factor[:, :], 1.0, None, ALU.add))
                step(nc.vector.scalar_tensor_tensor(x[:, :, :], h[:, :, :], factor[:, 0:1], x[:, :, :], ALU.mult,
                                                    ALU.add))
                dve.wait_ge(gathered, 16 * 2 * HI)
                step(nc.vector.tensor_tensor(carry_in[:, :, :], carry_in[:, :, :], wide(g["spans"][:, :]), ALU.mult))
                step(nc.vector.tensor_tensor(ends[:, :, :], ends[:, :, :], carry_in[:, :, :], ALU.add))
                step(nc.vector.tensor_tensor(ends[:, :, :], ends[:, :, :], wide(g["has_out"][:, :]), ALU.mult))
                step(nc.vector.tensor_tensor(x[:, :, :], x[:, :, :], ends[:, :, :], ALU.add))


def split_features(nc, parts, h):
    with Scope(nc) as s:
        rest = s.sb("split_rest", [P, HI, D], F32)
        dve_step = s.sem("dve_step")
        block = s.block()

        @block.vector
        def _(dve):
            split_three(Serial(dve, dve_step), nc, parts, rest[:, :, :], h[:, :, :])


def turn_weights(nc, g, w_msg, b_msg, w_ih, w_hh, b_ih, b_hh, weights):
    with Scope(nc) as s:
        msg = s.sb("msg_nat", [P, 2, 3 * D + 1], F32)
        inp = s.sb("in_nat", [P, 2, 2, P], F32)
        hid = s.sb("hid_nat", [P, 2, 3, D + 1], F32)
        bias = s.sb("hid_bias", [P, 2], F32)
        turned = [[s.ps(f"weights_turned{t}_{k}", [P, 2, P]) for k in range(4)] for t in range(2)]
        cleared = s.sem("cleared")
        loaded = s.sem("loaded")
        nat_ready = s.sem("nat_ready")
        turned_ready = s.sem("turned_ready")
        copied = s.sem("copied")
        block = s.block()
        G = 2 * D

        def load(queue, t):
            queue.dma_start(msg[:, t, 0:3 * D], w_msg[t, :, :]).then_inc(loaded, 16)
            queue.dma_start(msg[:, t, 3 * D:3 * D + 1], b_msg[t, :].unsqueeze(1)).then_inc(loaded, 16)
            queue.dma_start(inp[:, t, 0, :], w_ih[t, 0:G, :]).then_inc(loaded, 16)
            queue.dma_start(inp[0:D, t, 1, :], w_ih[t, G:3 * D, :]).then_inc(loaded, 16)
            queue.dma_start(hid[:, t, 0, 0:D], w_hh[t, 0:G, :]).then_inc(loaded, 16)
            queue.dma_start(hid[:, t, 0, D:D + 1], b_hh[t, 0:G].unsqueeze(1)).then_inc(loaded, 16)
            queue.dma_start(bias[:, t:t + 1], b_ih[t, 0:G].unsqueeze(1)).then_inc(loaded, 16)
            queue.dma_start(hid[0:D, t, 2, 0:D], w_hh[t, G:3 * D, :]).then_inc(loaded, 16)
            queue.dma_start(hid[0:D, t, 2, D:D + 1], b_hh[t, G:3 * D].unsqueeze(1)).then_inc(loaded, 16)
            queue.wait_ge(cleared, 1)
            queue.dma_start(hid[0:D, t, 1, D:D + 1], b_ih[t, G:3 * D].unsqueeze(1)).then_inc(loaded, 16)

        @block.sync
        def _(sp):
            load(sp, 0)

        @block.scalar
        def _(act):
            load(act, 1)

        @block.vector
        def _(dve):
            nc.vector.memset(hid[:, :, 1, :], 0.0).then_inc(cleared, 1)
            dve.wait_ge(loaded, 20 * 16)
            for t in range(2):
                nc.vector.tensor_tensor(hid[:, t, 0, D:D + 1], hid[:, t, 0, D:D + 1], bias[:, t:t + 1], ALU.add
                                        ).then_inc(nat_ready, 1)
            for t in range(2):
                w_ds, we, w_in, w_hid = weights[t]
                bank = turned[t]
                dve.wait_ge(turned_ready, t + 1)
                nc.vector.tensor_copy(w_ds[:, :], bank[0][:, 0, :])
                nc.vector.tensor_copy(we[:, :], bank[1][0:D + 1, 0, :])
                nc.vector.tensor_copy(w_in[:, 0:G], bank[1][:, 1, :])
                nc.vector.tensor_copy(w_in[:, G:3 * D], bank[2][:, 0, 0:D])
                nc.vector.tensor_copy(w_hid[:, 0:G], bank[2][0:D + 1, 1, :])
                nc.vector.tensor_copy(w_hid[:, G:3 * D], bank[3][0:D + 1, 0, 0:D])
                nc.vector.tensor_copy(w_hid[:, 3 * D:4 * D], bank[3][0:D + 1, 1, 0:D]).then_inc(copied, 1)

        @block.tensor
        def _(pe):
            ident, half = g["ident"][:, :], g["ident"][0:D, 0:D]
            for t in range(2):
                bank = turned[t]
                pe.wait_ge(nat_ready, t + 1)
                nc.tensor.transpose(bank[0][:, 0, :], msg[:, t, 0:2 * D], ident)
                nc.tensor.transpose(bank[1][0:D + 1, 0, :], msg[:, t, 2 * D:3 * D + 1], ident)
                nc.tensor.transpose(bank[1][:, 1, :], inp[:, t, 0, :], ident)
                nc.tensor.transpose(bank[2][:, 0, 0:D], inp[0:D, t, 1, :], half)
                nc.tensor.transpose(bank[2][0:D + 1, 1, :], hid[:, t, 0, :], ident)
                nc.tensor.transpose(bank[3][0:D + 1, 0, 0:D], hid[0:D, t, 1, :], half)
                nc.tensor.transpose(bank[3][0:D + 1, 1, 0:D], hid[0:D, t, 2, :], half).then_inc(turned_ready, 1)


def gated_update(nc, g, t, h, sums, w_ds, we, w_in, w_hid):
    CH = -(-HI // 4)
    PAIRS = -(-HI // 2)
    with Scope(nc, f"_round{t}") as s:
        scaled = s.sb("scaled_h", [P, 2, 4, 2 * D], F32)
        ht = s.sb("gru_ht", [D + 1, 2, 512], F32)
        ct = s.sb("gru_ct", [P, 2, 512], F32)
        et = s.sb("gru_et", [D + 1, 2, 512], F32)
        at = s.sb("gru_at", [P, 2, 512], F32)
        rz = s.sb("gru_rz", [P, 2, 2, 2 * D], F32)
        new = s.sb("gru_new", [P, 2, 2, D], F32)
        diff = s.sb("gru_diff", [P, 2, D], F32)
        ps_h = s.ps("ps_ht", [D, 4, P])
        ps_c = s.ps("ps_ct", [P, 4, P])
        ps_e = s.ps("ps_et", [D + 1, 4, P])
        ps_a = s.ps("ps_at", [P, 512])
        gates = [s.ps(f"ps_gates{k}", [P, 2, 4 * D]) for k in range(4)]
        scaled_ready = s.sem("scaled_ready")
        turned_ready = s.sem("turned_ready")
        copied_act = s.sem("copied_act")
        copied_dve = s.sem("copied_dve")
        sum_ready = s.sem("sum_ready")
        sum_copied = s.sem("sum_copied")
        gates_ready = s.sem("gates_ready")
        rz_ready = s.sem("rz_ready")
        pre_ready = s.sem("pre_ready")
        new_ready = s.sem("new_ready")
        updated = s.sem("updated")
        dve_step = s.sem("dve_step")
        ones_ready = s.sem("ones_ready")
        block = s.block()

        def blocks(c):
            return min(4, HI - 4 * c)

        def pairs(c):
            return range(2 * c, min(2 * c + 2, PAIRS))

        def paired(p):
            return min(2, HI - 2 * p)

        @block.tensor
        def _(pe):
            def turn(c):
                pe.wait_ge(scaled_ready, c + 1)
                if c:
                    pe.wait_ge(copied_act, c)
                    pe.wait_ge(copied_dve, c)
                for a in range(blocks(c)):
                    b = 4 * c + a
                    nc.tensor.transpose(ps_h[:, a, :], h[:, b, :], g["ident"][:, :])
                    nc.tensor.transpose(ps_e[:, a, :], g["attr_sum"][:, b * (D + 1):(b + 1) * (D + 1)],
                                        g["ident"][:, :])
                    last = nc.tensor.transpose(ps_c[:, a, :], scaled[:, c % 2, a, :], g["ident"][:, :])
                last.then_inc(turned_ready, 1)

            turn(0)
            pe.wait_ge(ones_ready, 1)
            for c in range(CH):
                if c + 1 < CH:
                    turn(c + 1)
                n = blocks(c) * P
                pe.wait_ge(copied_act, c + 1)
                pe.wait_ge(copied_dve, c + 1)
                if c:
                    pe.wait_ge(sum_copied, c)
                nc.tensor.matmul(ps_a[:, 0:n], w_ds[:, :], ct[:, c % 2, 0:n], start=True, stop=False)
                nc.tensor.matmul(ps_a[:, 0:n], we[:, :], et[:, c % 2, 0:n], start=False, stop=True
                                 ).then_inc(sum_ready, 1)
                pe.wait_ge(sum_copied, c + 1)
                for p in pairs(c):
                    if p >= 4:
                        pe.wait_ge(pre_ready, p - 3)
                    for k in range(paired(p)):
                        col = (2 * (p % 2) + k) * P
                        nc.tensor.matmul(gates[p % 4][:, k, :], ht[:, c % 2, col:col + P], w_hid[:, :], start=True,
                                         stop=True)
                        last = nc.tensor.matmul(gates[p % 4][:, k, 0:3 * D], at[:, c % 2, col:col + P], w_in[:, :],
                                                start=False, stop=True, skip_group_check=True)
                    last.then_inc(gates_ready, 1)

        @block.scalar
        def _(act):
            def copy(c):
                n = blocks(c)
                act.wait_ge(turned_ready, c + 1)
                if c >= 2:
                    act.wait_ge(gates_ready, 2 * c - 2)
                for out, bank, rows in ((ht, ps_h, D), (et, ps_e, D + 1)):
                    last = nc.scalar.copy(out[0:rows, c % 2, 0:n * P].rearrange("p (a b) -> p a b", b=P), bank[:, 0:n, :])
                last.then_inc(copied_act, 1)

            def gate(p):
                act.wait_ge(gates_ready, p + 1)
                if p >= 2:
                    act.wait_ge(updated, p - 1)
                nc.scalar.activation(rz[:, p % 2, 0:paired(p), :], gates[p % 4][:, 0:paired(p), 0:2 * D], ACT.Sigmoid
                                     ).then_inc(rz_ready, 1)

            def tanh(p):
                act.wait_ge(pre_ready, p + 1)
                state = new[:, p % 2, 0:paired(p), :]
                nc.scalar.activation(state, state, ACT.Tanh).then_inc(new_ready, 1)

            copy(0)
            for c in range(CH):
                if c + 1 < CH:
                    copy(c + 1)
                for p in pairs(c):
                    gate(p)
                    if p:
                        tanh(p - 1)
            tanh(PAIRS - 1)

        @block.vector
        def _(dve):
            step = Serial(dve, dve_step)
            for b in range(2):
                last = nc.vector.memset(ht[D:D + 1, b, :], 1.0)
            last.then_inc(ones_ready, 1)
            columns = sums[:, 0:HI * (D + 1)].rearrange("p (b f) -> p b f", f=D + 1)
            counts = columns[:, :, D]

            def scale(c):
                n = blocks(c)
                if c >= 2:
                    dve.wait_ge(turned_ready, c - 1)
                nc.vector.tensor_copy(scaled[:, c % 2, 0:n, D:2 * D], columns[:, 4 * c:4 * c + n, 0:D])
                nc.vector.tensor_tensor(scaled[:, c % 2, 0:n, 0:D], h[:, 4 * c:4 * c + n, :],
                                        wide(counts[:, 4 * c:4 * c + n]), ALU.mult).then_inc(scaled_ready, 1)

            def copy(c):
                n = blocks(c)
                dve.wait_ge(turned_ready, c + 1)
                if c >= 2:
                    dve.wait_ge(sum_ready, c - 1)
                nc.vector.tensor_copy(ct[:, c % 2, 0:n * P].rearrange("p (a b) -> p a b", b=P), ps_c[:, 0:n, :]
                                      ).then_inc(copied_dve, 1)

            def before_tanh(p):
                n = paired(p)
                pre = new[:, p % 2, 0:n, :]
                dve.wait_ge(rz_ready, p + 1)
                step(nc.vector.tensor_tensor(pre, rz[:, p % 2, 0:n, 0:D], gates[p % 4][:, 0:n, 3 * D:4 * D], ALU.mult))
                nc.vector.tensor_tensor(pre, pre, gates[p % 4][:, 0:n, 2 * D:3 * D], ALU.add).then_inc(pre_ready, 1)

            def update(p):
                n = paired(p)
                state, d = h[:, 2 * p:2 * p + n, :], diff[:, 0:n, :]
                dve.wait_ge(new_ready, p + 1)
                step(nc.vector.tensor_tensor(d, state, new[:, p % 2, 0:n, :], ALU.subtract))
                step(nc.vector.tensor_tensor(d, d, rz[:, p % 2, 0:n, D:2 * D], ALU.mult))
                nc.vector.tensor_tensor(state, d, new[:, p % 2, 0:n, :], ALU.add).then_inc(updated, 1)
                dve.wait_ge(updated, p + 1)

            scale(0)
            copy(0)
            for c in range(CH):
                if c + 1 < CH:
                    scale(c + 1)
                dve.wait_ge(sum_ready, c + 1)
                if c >= 2:
                    dve.wait_ge(gates_ready, 2 * c - 2)
                n = blocks(c) * P
                nc.vector.tensor_copy(at[:, c % 2, 0:n], ps_a[:, 0:n]).then_inc(sum_copied, 1)
                if c + 1 < CH:
                    copy(c + 1)
                for p in pairs(c):
                    before_tanh(p)
                    if p:
                        update(p - 1)
            update(PAIRS - 1)


def gated_layer(nc, g, slabs, w_msg, b_msg, w_ih, w_hh, b_ih, b_hh, out):
    with Scope(nc) as keep:
        h = keep.sb("gated_h", [P, HI, D], F32)
        parts = keep.sb("gated_parts", [P, HI, 3 * D + 1], BF16)
        weights = [(keep.sb(f"w_ds{t}", [P, P], F32), keep.sb(f"we{t}", [D + 1, P], F32),
                    keep.sb(f"w_in{t}", [P, 3 * D], F32), keep.sb(f"w_hid{t}", [D + 1, 4 * D], F32))
                   for t in range(2)]
        normalise(nc, g, "_gated", h, parts)
        turn_weights(nc, g, w_msg, b_msg, w_ih, w_hh, b_ih, b_hh, weights)
        for t in range(2):
            with Scope(nc, f"_round{t}") as s:
                sums = s.sb("gated_sums", [P, NB * (D + 1)], F32)
                sum_over_sources(nc, f"_round{t}", slabs, parts, sums)
                gated_update(nc, g, t, h, sums, *weights[t])
            if t == 0:
                split_features(nc, parts, h)
        with Scope(nc) as s:
            ready = s.sem("result_ready")
            stored = s.sem("result_stored")
            block = s.block()
            x, full = g["x"], (N // P) * P

            @block.vector
            def _(dve):
                nc.vector.tensor_tensor(x[:, :, :], x[:, :, :], h[:, :, :], ALU.add).then_inc(ready, 1)

            @block.sync
            def _(sp):
                sp.wait_ge(ready, 1)
                sp.dma_start(out[0:full, :].rearrange("(b p) f -> p b f", p=P), x[:, 0:N // P, :]).then_inc(stored, 16)
                sp.dma_start(out[full:N, :], x[0:N - full, N // P, :]).then_inc(stored, 16)
                sp.wait_ge(stored, 32)


def gnn_kernel(nc, x, src, dst, edge_attr_32, edge_attr_64, edge_weight, u, w1, b1, w2, b2, conv_w, conv_b, eps,
               w_msg, b_msg, w_ih, w_hh, b_ih, b_hh, out):
    g = {}
    Scope.spent.clear()
    slabs = nc.dram_tensor("slabs", [NSLAB // 2, P, HI * SPAN], BF16)
    scratch = nc.dram_tensor("range_rows", [2, KB + 1, P], F32)
    sorted_rows = nc.dram_tensor("sorted_rows", [E, ROW], F32)
    scanned = nc.dram_tensor("scanned", [E, D], F32)
    carries = nc.dram_tensor("carries", [EP, D], F32)
    table = nc.dram_tensor("feature_table", [HI * P, D], F32)
    with ExitStack() as ctx:
        kept(nc, ctx, g)
        with ExitStack() as to_rank:
            kept_to_rank(nc, to_rank, g)
            prepare_keys(nc, g, src, dst, edge_weight)
            count_sources(nc, g)
            find_ranges(nc, g, scratch)
            rank_and_build(nc, g, edge_attr_32, sorted_rows, slabs)
        scan_sorted(nc, g, sorted_rows, scanned, carries)
        locate_runs(nc, g)
        edge_statistics_layer(nc, g, scanned, carries, x, u, w1, b1, w2, b2)
        convolution_layer(nc, g, slabs, conv_w, conv_b)
        clear_spent(nc)
        g["attr_sum"] = ctx.enter_context(nc.sbuf_tensor("attr_sum", [P, NB * (D + 1)], F32))
        weighted_layer(nc, g, table, scanned, carries, eps, edge_attr_64)
        gated_layer(nc, g, slabs, w_msg, b_msg, w_ih, w_hh, b_ih, b_hh, out)


_INS = ['x', 'src', 'dst', 'edge_attr_32', 'edge_attr_64', 'edge_weight', 'L0_gnn_u', 'L0_gnn_W1', 'L0_gnn_b1',
        'L0_gnn_W2', 'L0_gnn_b2', 'L1_gnn_W', 'L1_gnn_b', 'L2_gnn_eps', 'L3_gnn_w_msg', 'L3_gnn_b_msg',
        'L3_gnn_w_ih', 'L3_gnn_w_hh', 'L3_gnn_b_ih', 'L3_gnn_b_hh']
_OUTS = [((N, D), 'float32')]


def kernel(**inputs):
    import numpy as _np
    import concourse.bacc as _bacc
    from concourse import mybir as _mybir
    from concourse.bass_utils import run_bass_kernel_spmd as _run

    nc = _bacc.Bacc("TRN2", target_bir_lowering=False, num_devices=1)
    arrays, args = {}, []
    for name in _INS:
        a = _np.ascontiguousarray(inputs[name])
        arrays[f"in_{name}_dram"] = a
        args.append(nc.dram_tensor(f"in_{name}_dram", a.shape, _mybir.dt.from_np(a.dtype), kind="ExternalInput").ap())
    for i, (shape, dtype) in enumerate(_OUTS):
        dt = _mybir.dt.from_np(_np.dtype(dtype))
        args.append(nc.dram_tensor(f"out_{i}_dram", shape, dt, kind="ExternalOutput").ap())
    gnn_kernel(nc, *args)
    r = _run(nc, [arrays], core_ids=[0])
    return r.results[0]["out_0_dram"]
```
